# Optimizing a Trainium2 kernel written in Bass

```python
import numpy as np
import jax
import jax.numpy as jnp

def _softmax(x, axis=-1):
    return jax.nn.softmax(x, axis=axis)

def _gelu(x):
    return jax.nn.gelu(x, approximate=True)

def _silu(x):
    return jax.nn.silu(x)

def _sigmoid(x):
    return jax.nn.sigmoid(x)

def _layernorm(x, axis=-1, eps=1e-05):
    m = jnp.mean(x, axis=axis, keepdims=True)
    v = jnp.var(x, axis=axis, keepdims=True)
    return (x - m) / jnp.sqrt(v + eps)

def _scatter_add(tgt, idx, src, axis=0):
    return tgt.at[idx].add(src)

def _segment_sum(src, seg, n):
    return jax.ops.segment_sum(src, seg, n)
kernel_name = 'mk_prb_d4_jaxref_r8_e1c631'

def setup_inputs(seed: int=0):
    np.random.seed(seed)
    _w = jnp.asarray

    def _L0_attn_setup():
        import jax, jax.numpy as jnp
        import numpy as np
        B, S, D = (2, 256, 128)
        H, DQ, DV = (16, 64, 64)
        key = jax.random.key(seed)
        k1, k2, k3, k4, k5 = jax.random.split(key, 5)
        scale = 0.02
        return {'x': jax.random.normal(k1, (B, S, D), dtype=jnp.float32), 'w_q': jax.random.normal(k2, (H, DQ, D), dtype=jnp.float32) * scale, 'w_k': jax.random.normal(k3, (H, DQ, D), dtype=jnp.float32) * scale, 'w_v': jax.random.normal(k4, (H, DV, D), dtype=jnp.float32) * scale, 'w_o': jax.random.normal(k5, (D, H * DV), dtype=jnp.float32) * scale}
    _L0_attn_in = _L0_attn_setup()

    def _L0_ffn_setup():
        import jax, jax.numpy as jnp
        import numpy as np
        B, S, D, H, E = (2, 256, 128, 512, 8)
        TOP_K = 2
        key = jax.random.key(seed)
        ks = jax.random.split(key, 5)
        scale = 0.02
        return {'x': jax.random.normal(ks[0], (B, S, D), dtype=jnp.float32), 'gate_w': jax.random.normal(ks[1], (D, E), dtype=jnp.float32) * scale, 'gate_b': jnp.zeros((E,), dtype=jnp.float32), 'w1': jax.random.normal(ks[2], (E, D, H), dtype=jnp.float32) * scale, 'b1': jnp.zeros((E, H), dtype=jnp.float32), 'w2': jax.random.normal(ks[3], (E, H, D), dtype=jnp.float32) * scale, 'b2': jnp.zeros((E, D), dtype=jnp.float32)}
    _L0_ffn_in = _L0_ffn_setup()

    def _L1_attn_setup():
        import jax, jax.numpy as jnp
        import numpy as np
        NUM_HEADS = 16
        key = jax.random.key(seed)
        k1, k2, k3 = jax.random.split(key, 3)
        B, D, N = (2, 256, 128)
        x = jax.random.normal(k1, (B, D, N), dtype=jnp.float32)
        W_qkv = jax.random.normal(k2, (N, 3 * N), dtype=jnp.float32) * (1.0 / np.sqrt(N))
        b_qkv = jax.random.normal(k3, (3 * N,), dtype=jnp.float32) * 0.01
        return {'x': x, 'W_qkv': W_qkv, 'b_qkv': b_qkv}
    _L1_attn_in = _L1_attn_setup()

    def _L1_ffn_setup():
        import jax, jax.numpy as jnp
        import numpy as np
        DIM = 128
        DEPTH = 6
        HEADS = 16
        DIM_HEAD = 64
        WINDOW = 32
        INNER = HEADS * DIM_HEAD
        DIM_INNER = int(DIM * 4 * 2 / 3)
        QK_SCALE = 8.0

        def shift_tokens(t):
            a, s = jnp.split(t, 2, -1)
            s = jnp.pad(s, ((0, 0), (1, 0), (0, 0)))[:, :-1]
            return jnp.concatenate([a, s], -1)

        def l2norm(t):
            return t / jnp.maximum(jnp.linalg.norm(t, axis=-1, keepdims=True), 1e-12)

        def rotate_half(x):
            x1, x2 = jnp.split(x, 2, -1)
            return jnp.concatenate([-x2, x1], -1)

        def rotary_tables(n):
            half = jnp.arange(0, DIM_HEAD, 2, dtype=jnp.float32)
            inv_freq = 1.0 / 10000.0 ** (half / DIM_HEAD)
            t = jnp.arange(n, dtype=jnp.float32)
            freqs = t[:, None] * inv_freq[None, :]
            freqs = jnp.concatenate([freqs, freqs], -1)
            base_scale = (half + 0.4 * DIM_HEAD) / (1.4 * DIM_HEAD)
            power = (t - n // 2) / (WINDOW // 2)
            scale = base_scale[None, :] ** power[:, None]
            scale = jnp.concatenate([scale, scale], -1)
            return (freqs, scale)

        def local_attention(q, k, v):
            b, h, n, d = q.shape
            w = WINDOW
            nw = n // w
            bq = q.reshape(b, h, nw, w, d)
            bk = k.reshape(b, h, nw, w, d)
            bv = v.reshape(b, h, nw, w, d)

            def look(t):
                p = jnp.pad(t, ((0, 0), (0, 0), (1, 0), (0, 0), (0, 0)))
                return jnp.concatenate([p[:, :, :nw], p[:, :, 1:]], axis=3)
            bk2, bv2 = (look(bk), look(bv))
            seq = jnp.arange(n).reshape(nw, w)
            seq_p = jnp.pad(seq, ((1, 0), (0, 0)), constant_values=-1)
            jt = jnp.concatenate([seq_p[:nw], seq_p[1:]], axis=1)
            it = seq[:, :, None]
            jb = jt[:, None, :]
            mask = (it < jb) | (it > jb + w) | (jb == -1)
            sim = jnp.einsum('bhwie,bhwje->bhwij', bq, bk2) * QK_SCALE
            sim = jnp.where(mask, -jnp.finfo(sim.dtype).max, sim)
            attn = jax.nn.softmax(sim, -1)
            out = jnp.einsum('bhwij,bhwje->bhwie', attn, bv2)
            return out.reshape(b, h, n, d)

        def attn_layer(x, Wqkv, qs, ksc, Wo):
            b, n, _ = x.shape
            qkv = x @ Wqkv
            q, k, v = jnp.split(qkv, 3, -1)
            sh = lambda t: t.reshape(b, n, HEADS, DIM_HEAD).transpose(0, 2, 1, 3)
            q, k, v = (sh(q), sh(k), sh(v))
            q = l2norm(q) * qs
            k = l2norm(k) * ksc
            freqs, scale = rotary_tables(n)
            cos, sin = (jnp.cos(freqs), jnp.sin(freqs))
            q = q * cos * scale + rotate_half(q) * sin * scale
            inv = 1.0 / scale
            k = k * cos * inv + rotate_half(k) * sin * inv
            out = local_attention(q, k, v)
            out = out.transpose(0, 2, 1, 3).reshape(b, n, INNER)
            return out @ Wo

        def ffn_layer(x, g, bln, W1, b1, W2, b2):
            mu = x.mean(-1, keepdims=True)
            var = ((x - mu) ** 2).mean(-1, keepdims=True)
            xn = (x - mu) / jnp.sqrt(var + 1e-05) * g + bln
            hg = xn @ W1 + b1
            a, gate = jnp.split(hg, 2, -1)
            return a * jax.nn.gelu(gate, approximate=False) @ W2 + b2
        key = jax.random.key(seed)
        ks = jax.random.split(key, 8)
        B, N = (2, 256)
        init = lambda k, shape: jax.random.normal(k, shape, jnp.float32) * 0.02
        return {'x': jax.random.normal(ks[0], (B, N, DIM), jnp.float32), 'Wqkv': init(ks[1], (DEPTH, DIM, 3 * INNER)), 'q_scale': jnp.ones((DEPTH, DIM_HEAD), jnp.float32), 'k_scale': jnp.ones((DEPTH, DIM_HEAD), jnp.float32), 'Wo': init(ks[2], (DEPTH, INNER, DIM)), 'ln_g': jnp.ones((DEPTH, DIM), jnp.float32), 'ln_b': jnp.zeros((DEPTH, DIM), jnp.float32), 'W1': init(ks[3], (DEPTH, DIM, 2 * DIM_INNER)), 'b1': jnp.zeros((DEPTH, 2 * DIM_INNER), jnp.float32), 'W2': init(ks[4], (DEPTH, DIM_INNER, DIM)), 'b2': jnp.zeros((DEPTH, DIM), jnp.float32)}
    _L1_ffn_in = _L1_ffn_setup()

    def _L2_attn_setup():
        import jax, jax.numpy as jnp
        import numpy as np
        EMBED = 128
        HEADS = 16
        HEAD_DIM = EMBED // HEADS
        RANK = 8
        ALPHA = 16
        SCALE_LORA = ALPHA / RANK

        def _lora_linear(x, W, b, A, B):
            return x @ W.T + b + SCALE_LORA * (x @ A.T @ B.T)
        key = jax.random.key(seed)
        ks = jax.random.split(key, 17)
        d = {'x': jax.random.normal(ks[0], (2, 256, EMBED), dtype=jnp.float32)}
        names = ['q', 'k', 'v', 'o']
        i = 1
        for n in names:
            d[f'W{n}'] = jax.random.normal(ks[i], (EMBED, EMBED), dtype=jnp.float32) * 0.02
            i += 1
            d[f'b{n}'] = jnp.zeros((EMBED,), dtype=jnp.float32)
            d[f'A{n}'] = jax.random.normal(ks[i], (RANK, EMBED), dtype=jnp.float32) * 0.02
            i += 1
            d[f'B{n}'] = jax.random.normal(ks[i], (EMBED, RANK), dtype=jnp.float32) * 0.02
            i += 1
        return d
    _L2_attn_in = _L2_attn_setup()

    def _L2_ffn_setup():
        import jax, jax.numpy as jnp
        import numpy as np

        def _binarize(w):
            alpha = jax.lax.stop_gradient(jnp.mean(jnp.abs(w), axis=1, keepdims=True))
            bw = alpha * jnp.sign(w)
            return w + jax.lax.stop_gradient(bw - w)
        key = jax.random.key(seed)
        k1, k2, k3, k4, k5 = jax.random.split(key, 5)
        D, H = (128, 512)
        x = jax.random.normal(k1, (64, 196, D), dtype=jnp.float32)
        w1 = jax.random.normal(k2, (H, D), dtype=jnp.float32) * 0.02
        b1 = jax.random.normal(k3, (H,), dtype=jnp.float32) * 0.02
        w2 = jax.random.normal(k4, (D, H), dtype=jnp.float32) * 0.02
        b2 = jax.random.normal(k5, (D,), dtype=jnp.float32) * 0.02
        return {'x': x, 'w1': w1, 'b1': b1, 'w2': w2, 'b2': b2}
    _L2_ffn_in = _L2_ffn_setup()

    def _L3_attn_setup():
        import jax, jax.numpy as jnp
        import numpy as np
        B, S, D, H = (2, 256, 128, 16)
        DH = D // H
        RD = DH // 2
        EPS = 1e-05

        def _rope(x):
            seq = x.shape[-2]
            inv_freq = 1.0 / 10000.0 ** (jnp.arange(0, RD, 2, dtype=jnp.float32) / RD)
            t = jnp.arange(seq, dtype=jnp.float32)
            freqs = t[:, None] * inv_freq[None, :]
            freqs = jnp.repeat(freqs, 2, axis=-1)
            cosf, sinf = (jnp.cos(freqs), jnp.sin(freqs))
            xr, xp = (x[..., :RD], x[..., RD:])
            pairs = xr.reshape(*xr.shape[:-1], RD // 2, 2)
            rot = jnp.stack([-pairs[..., 1], pairs[..., 0]], axis=-1).reshape(xr.shape)
            return jnp.concatenate([xr * cosf + rot * sinf, xp], axis=-1)
        key = jax.random.key(seed)
        ks = jax.random.split(key, 4)
        s = 0.02
        return {'X': jax.random.normal(ks[0], (B, S, D), jnp.float32), 'W_in': jax.random.normal(ks[1], (D, 3 * D), jnp.float32) * s, 'b_in': jnp.zeros((3 * D,), jnp.float32), 'W_out': jax.random.normal(ks[2], (D, D), jnp.float32) * s, 'b_out': jnp.zeros((D,), jnp.float32), 'gamma': jnp.ones((D,), jnp.float32), 'beta': jnp.zeros((D,), jnp.float32)}
    _L3_attn_in = _L3_attn_setup()

    def _L3_ffn_setup():
        import jax, jax.numpy as jnp
        import numpy as np
        NUM_EXPERTS = 8
        TOP_K = 2
        CAPACITY_FACTOR = 1.25
        key = jax.random.key(seed)
        ks = jax.random.split(key, 5)
        B, S, D, H, E = (4, 256, 128, 256, NUM_EXPERTS)
        scale = 0.02
        return {'x': jax.random.normal(ks[0], (B, S, D), dtype=jnp.float32), 'gate_w': jax.random.normal(ks[1], (E, D), dtype=jnp.float32) * scale, 'gate_proj_w': jax.random.normal(ks[2], (E, H, D), dtype=jnp.float32) * scale, 'up_proj_w': jax.random.normal(ks[3], (E, H, D), dtype=jnp.float32) * scale, 'down_proj_w': jax.random.normal(ks[4], (E, D, H), dtype=jnp.float32) * scale}
    _L3_ffn_in = _L3_ffn_setup()
    _d = {'L0_attn_x': _L0_attn_in['x'], 'L0_attn_w_q': _L0_attn_in['w_q'], 'L0_attn_w_k': _L0_attn_in['w_k'], 'L0_attn_w_v': _L0_attn_in['w_v'], 'L0_attn_w_o': _L0_attn_in['w_o'], 'L0_ffn_gate_w': _L0_ffn_in['gate_w'], 'L0_ffn_gate_b': _L0_ffn_in['gate_b'], 'L0_ffn_w1': _L0_ffn_in['w1'], 'L0_ffn_b1': _L0_ffn_in['b1'], 'L0_ffn_w2': _L0_ffn_in['w2'], 'L0_ffn_b2': _L0_ffn_in['b2'], 'L1_attn_W_qkv': _L1_attn_in['W_qkv'], 'L1_attn_b_qkv': _L1_attn_in['b_qkv'], 'L1_ffn_Wqkv': _L1_ffn_in['Wqkv'], 'L1_ffn_q_scale': _L1_ffn_in['q_scale'], 'L1_ffn_k_scale': _L1_ffn_in['k_scale'], 'L1_ffn_Wo': _L1_ffn_in['Wo'], 'L1_ffn_ln_g': _L1_ffn_in['ln_g'], 'L1_ffn_ln_b': _L1_ffn_in['ln_b'], 'L1_ffn_W1': _L1_ffn_in['W1'], 'L1_ffn_b1': _L1_ffn_in['b1'], 'L1_ffn_W2': _L1_ffn_in['W2'], 'L1_ffn_b2': _L1_ffn_in['b2'], 'L2_attn_Wq': _L2_attn_in['Wq'], 'L2_attn_bq': _L2_attn_in['bq'], 'L2_attn_Aq': _L2_attn_in['Aq'], 'L2_attn_Bq': _L2_attn_in['Bq'], 'L2_attn_Wk': _L2_attn_in['Wk'], 'L2_attn_bk': _L2_attn_in['bk'], 'L2_attn_Ak': _L2_attn_in['Ak'], 'L2_attn_Bk': _L2_attn_in['Bk'], 'L2_attn_Wv': _L2_attn_in['Wv'], 'L2_attn_bv': _L2_attn_in['bv'], 'L2_attn_Av': _L2_attn_in['Av'], 'L2_attn_Bv': _L2_attn_in['Bv'], 'L2_attn_Wo': _L2_attn_in['Wo'], 'L2_attn_bo': _L2_attn_in['bo'], 'L2_attn_Ao': _L2_attn_in['Ao'], 'L2_attn_Bo': _L2_attn_in['Bo'], 'L2_ffn_w1': _L2_ffn_in['w1'], 'L2_ffn_b1': _L2_ffn_in['b1'], 'L2_ffn_w2': _L2_ffn_in['w2'], 'L2_ffn_b2': _L2_ffn_in['b2'], 'L3_attn_W_in': _L3_attn_in['W_in'], 'L3_attn_b_in': _L3_attn_in['b_in'], 'L3_attn_W_out': _L3_attn_in['W_out'], 'L3_attn_b_out': _L3_attn_in['b_out'], 'L3_attn_gamma': _L3_attn_in['gamma'], 'L3_attn_beta': _L3_attn_in['beta'], 'L3_ffn_gate_w': _L3_ffn_in['gate_w'], 'L3_ffn_gate_proj_w': _L3_ffn_in['gate_proj_w'], 'L3_ffn_up_proj_w': _L3_ffn_in['up_proj_w'], 'L3_ffn_down_proj_w': _L3_ffn_in['down_proj_w']}
    _x0 = _d['L0_attn_x']
    _d['L0_attn_x'] = jax.random.normal(jax.random.fold_in(jax.random.key(seed), 1), (16, 256, 128), dtype=_x0.dtype)
    del _x0
    return _d

def reference(L0_attn_x, L0_attn_w_q, L0_attn_w_k, L0_attn_w_v, L0_attn_w_o, L0_ffn_gate_w, L0_ffn_gate_b, L0_ffn_w1, L0_ffn_b1, L0_ffn_w2, L0_ffn_b2, L1_attn_W_qkv, L1_attn_b_qkv, L1_ffn_Wqkv, L1_ffn_q_scale, L1_ffn_k_scale, L1_ffn_Wo, L1_ffn_ln_g, L1_ffn_ln_b, L1_ffn_W1, L1_ffn_b1, L1_ffn_W2, L1_ffn_b2, L2_attn_Wq, L2_attn_bq, L2_attn_Aq, L2_attn_Bq, L2_attn_Wk, L2_attn_bk, L2_attn_Ak, L2_attn_Bk, L2_attn_Wv, L2_attn_bv, L2_attn_Av, L2_attn_Bv, L2_attn_Wo, L2_attn_bo, L2_attn_Ao, L2_attn_Bo, L2_ffn_w1, L2_ffn_b1, L2_ffn_w2, L2_ffn_b2, L3_attn_W_in, L3_attn_b_in, L3_attn_W_out, L3_attn_b_out, L3_attn_gamma, L3_attn_beta, L3_ffn_gate_w, L3_ffn_gate_proj_w, L3_ffn_up_proj_w, L3_ffn_down_proj_w):

    def _L0_attn_ref(x, w_q, w_k, w_v, w_o):
        import jax, jax.numpy as jnp
        import numpy as np
        B, S, D = (2, 256, 128)
        H, DQ, DV = (16, 64, 64)
        b, s, d = x.shape
        q = jnp.einsum('bsd,hqd->bhsq', x, w_q)
        k = jnp.einsum('bsd,hqd->bhsq', x, w_k)
        v = jnp.einsum('bsd,hvd->bhsv', x, w_v)
        scores = jnp.einsum('bhsq,bhtq->bhst', q, k)
        causal = jnp.triu(jnp.ones((s, s), dtype=bool), k=1)
        masked = jnp.where(causal, -jnp.inf, scores)
        dq = w_q.shape[1]
        weights = jax.nn.softmax(masked / jnp.sqrt(jnp.float32(dq)), axis=-1)
        out = jnp.einsum('bhst,bhtv->bhsv', weights, v)
        cat = out.transpose(0, 2, 1, 3).reshape(b, s, -1)
        return jnp.einsum('bsf,df->bsd', cat, w_o)

    def _L0_ffn_ref(x, gate_w, gate_b, w1, b1, w2, b2):
        import jax, jax.numpy as jnp
        import numpy as np
        B, S, D, H, E = (2, 256, 128, 512, 8)
        TOP_K = 2
        gate_logits = jnp.einsum('bsd,de->bse', x, gate_w) + gate_b
        gate_weights = jax.nn.softmax(gate_logits, axis=-1)
        topk_values, topk_indices = jax.lax.top_k(gate_weights, TOP_K)
        hidden = jax.nn.relu(jnp.einsum('bsd,edh->bseh', x, w1) + b1)
        expert_out = jnp.einsum('bseh,ehd->bsed', hidden, w2) + b2
        sel = jnp.take_along_axis(expert_out, topk_indices[..., None], axis=2)
        return jnp.sum(topk_values[..., None] * sel, axis=2)

    def _L1_attn_ref(x, W_qkv, b_qkv):
        import jax, jax.numpy as jnp
        import numpy as np
        NUM_HEADS = 16
        B, D, N = x.shape
        H = NUM_HEADS
        p = N // H
        qkv = (x @ W_qkv + b_qkv).reshape(B, D, 3, H, p).transpose(2, 0, 3, 1, 4)
        q, k, v = (qkv[0], qkv[1], qkv[2])
        scores = jax.nn.softmax(jnp.einsum('bhip,bhjp->bhij', q, k), axis=-1)
        out = jnp.einsum('bhij,bhjp->bhip', scores, v)
        return out.reshape(B, D, N)

    def _L1_ffn_ref(x, Wqkv, q_scale, k_scale, Wo, ln_g, ln_b, W1, b1, W2, b2):
        import jax, jax.numpy as jnp
        import numpy as np
        DIM = 128
        DEPTH = 6
        HEADS = 16
        DIM_HEAD = 64
        WINDOW = 32
        INNER = HEADS * DIM_HEAD
        DIM_INNER = int(DIM * 4 * 2 / 3)
        QK_SCALE = 8.0

        def shift_tokens(t):
            a, s = jnp.split(t, 2, -1)
            s = jnp.pad(s, ((0, 0), (1, 0), (0, 0)))[:, :-1]
            return jnp.concatenate([a, s], -1)

        def l2norm(t):
            return t / jnp.maximum(jnp.linalg.norm(t, axis=-1, keepdims=True), 1e-12)

        def rotate_half(x):
            x1, x2 = jnp.split(x, 2, -1)
            return jnp.concatenate([-x2, x1], -1)

        def rotary_tables(n):
            half = jnp.arange(0, DIM_HEAD, 2, dtype=jnp.float32)
            inv_freq = 1.0 / 10000.0 ** (half / DIM_HEAD)
            t = jnp.arange(n, dtype=jnp.float32)
            freqs = t[:, None] * inv_freq[None, :]
            freqs = jnp.concatenate([freqs, freqs], -1)
            base_scale = (half + 0.4 * DIM_HEAD) / (1.4 * DIM_HEAD)
            power = (t - n // 2) / (WINDOW // 2)
            scale = base_scale[None, :] ** power[:, None]
            scale = jnp.concatenate([scale, scale], -1)
            return (freqs, scale)

        def local_attention(q, k, v):
            b, h, n, d = q.shape
            w = WINDOW
            nw = n // w
            bq = q.reshape(b, h, nw, w, d)
            bk = k.reshape(b, h, nw, w, d)
            bv = v.reshape(b, h, nw, w, d)

            def look(t):
                p = jnp.pad(t, ((0, 0), (0, 0), (1, 0), (0, 0), (0, 0)))
                return jnp.concatenate([p[:, :, :nw], p[:, :, 1:]], axis=3)
            bk2, bv2 = (look(bk), look(bv))
            seq = jnp.arange(n).reshape(nw, w)
            seq_p = jnp.pad(seq, ((1, 0), (0, 0)), constant_values=-1)
            jt = jnp.concatenate([seq_p[:nw], seq_p[1:]], axis=1)
            it = seq[:, :, None]
            jb = jt[:, None, :]
            mask = (it < jb) | (it > jb + w) | (jb == -1)
            sim = jnp.einsum('bhwie,bhwje->bhwij', bq, bk2) * QK_SCALE
            sim = jnp.where(mask, -jnp.finfo(sim.dtype).max, sim)
            attn = jax.nn.softmax(sim, -1)
            out = jnp.einsum('bhwij,bhwje->bhwie', attn, bv2)
            return out.reshape(b, h, n, d)

        def attn_layer(x, Wqkv, qs, ksc, Wo):
            b, n, _ = x.shape
            qkv = x @ Wqkv
            q, k, v = jnp.split(qkv, 3, -1)
            sh = lambda t: t.reshape(b, n, HEADS, DIM_HEAD).transpose(0, 2, 1, 3)
            q, k, v = (sh(q), sh(k), sh(v))
            q = l2norm(q) * qs
            k = l2norm(k) * ksc
            freqs, scale = rotary_tables(n)
            cos, sin = (jnp.cos(freqs), jnp.sin(freqs))
            q = q * cos * scale + rotate_half(q) * sin * scale
            inv = 1.0 / scale
            k = k * cos * inv + rotate_half(k) * sin * inv
            out = local_attention(q, k, v)
            out = out.transpose(0, 2, 1, 3).reshape(b, n, INNER)
            return out @ Wo

        def ffn_layer(x, g, bln, W1, b1, W2, b2):
            mu = x.mean(-1, keepdims=True)
            var = ((x - mu) ** 2).mean(-1, keepdims=True)
            xn = (x - mu) / jnp.sqrt(var + 1e-05) * g + bln
            hg = xn @ W1 + b1
            a, gate = jnp.split(hg, 2, -1)
            return a * jax.nn.gelu(gate, approximate=False) @ W2 + b2
        for i in range(DEPTH):
            x = attn_layer(shift_tokens(x), Wqkv[i], q_scale[i], k_scale[i], Wo[i]) + x
            x = ffn_layer(shift_tokens(x), ln_g[i], ln_b[i], W1[i], b1[i], W2[i], b2[i]) + x
        return x

    def _L2_attn_ref(x, Wq, bq, Aq, Bq, Wk, bk, Ak, Bk, Wv, bv, Av, Bv, Wo, bo, Ao, Bo):
        import jax, jax.numpy as jnp
        import numpy as np
        EMBED = 128
        HEADS = 16
        HEAD_DIM = EMBED // HEADS
        RANK = 8
        ALPHA = 16
        SCALE_LORA = ALPHA / RANK

        def _lora_linear(x, W, b, A, B):
            return x @ W.T + b + SCALE_LORA * (x @ A.T @ B.T)
        N, S, _ = x.shape
        Q = _lora_linear(x, Wq, bq, Aq, Bq).reshape(N, S, HEADS, HEAD_DIM)
        K = _lora_linear(x, Wk, bk, Ak, Bk).reshape(N, S, HEADS, HEAD_DIM)
        V = _lora_linear(x, Wv, bv, Av, Bv).reshape(N, S, HEADS, HEAD_DIM)
        energy = jnp.einsum('nqhd,nkhd->nhqk', Q, K) / jnp.sqrt(jnp.float32(HEAD_DIM))
        attn = jax.nn.softmax(energy, axis=-1)
        out = jnp.einsum('nhqk,nkhd->nqhd', attn, V).reshape(N, S, EMBED)
        return _lora_linear(out, Wo, bo, Ao, Bo)

    def _L2_ffn_ref(x, w1, b1, w2, b2):
        import jax, jax.numpy as jnp
        import numpy as np

        def _binarize(w):
            alpha = jax.lax.stop_gradient(jnp.mean(jnp.abs(w), axis=1, keepdims=True))
            bw = alpha * jnp.sign(w)
            return w + jax.lax.stop_gradient(bw - w)
        bw1 = _binarize(w1)
        h = jnp.einsum('bsd,hd->bsh', x, bw1) + b1
        h = jax.nn.gelu(h, approximate=False)
        bw2 = _binarize(w2)
        out = jnp.einsum('bsh,dh->bsd', h, bw2) + b2
        return out

    def _L3_attn_ref(X, W_in, b_in, W_out, b_out, gamma, beta):
        import jax, jax.numpy as jnp
        import numpy as np
        B, S, D, H = (2, 256, 128, 16)
        DH = D // H
        RD = DH // 2
        EPS = 1e-05

        def _rope(x):
            seq = x.shape[-2]
            inv_freq = 1.0 / 10000.0 ** (jnp.arange(0, RD, 2, dtype=jnp.float32) / RD)
            t = jnp.arange(seq, dtype=jnp.float32)
            freqs = t[:, None] * inv_freq[None, :]
            freqs = jnp.repeat(freqs, 2, axis=-1)
            cosf, sinf = (jnp.cos(freqs), jnp.sin(freqs))
            xr, xp = (x[..., :RD], x[..., RD:])
            pairs = xr.reshape(*xr.shape[:-1], RD // 2, 2)
            rot = jnp.stack([-pairs[..., 1], pairs[..., 0]], axis=-1).reshape(xr.shape)
            return jnp.concatenate([xr * cosf + rot * sinf, xp], axis=-1)
        b, s, d = X.shape
        mu = jnp.mean(X, axis=-1, keepdims=True)
        var = jnp.var(X, axis=-1, keepdims=True)
        xn = (X - mu) * jax.lax.rsqrt(var + EPS) * gamma + beta
        qkv = xn @ W_in + b_in
        q, k, v = jnp.split(qkv, 3, axis=-1)

        def to_heads(t):
            return t.reshape(b, s, H, DH).transpose(0, 2, 1, 3)
        q, k, v = (to_heads(q), to_heads(k), to_heads(v))
        q, k = (_rope(q), _rope(k))
        scores = jnp.einsum('bhqd,bhkd->bhqk', q, k) / jnp.sqrt(jnp.float32(DH))
        attn = jax.nn.softmax(scores, axis=-1)
        ctx = jnp.einsum('bhqk,bhkd->bhqd', attn, v)
        ctx = ctx.transpose(0, 2, 1, 3).reshape(b, s, d)
        return ctx @ W_out + b_out + X

    def _L3_ffn_ref(x, gate_w, gate_proj_w, up_proj_w, down_proj_w):
        import jax, jax.numpy as jnp
        import numpy as np
        NUM_EXPERTS = 8
        TOP_K = 2
        CAPACITY_FACTOR = 1.25
        B, S, D = x.shape
        E, K = (NUM_EXPERTS, TOP_K)
        T = B * S
        xf = x.reshape(T, D)
        logits = xf @ gate_w.T
        probs = jax.nn.softmax(logits, axis=-1)
        top_p, top_i = jax.lax.top_k(probs, K)
        w = top_p / (jnp.sum(top_p, axis=-1, keepdims=True) + 1e-09)
        capacity = int(CAPACITY_FACTOR * T / E)
        oh = jax.nn.one_hot(top_i, E, dtype=jnp.int32)
        rank = jnp.cumsum(oh, axis=0) - 1
        my_rank = jnp.sum(rank * oh, axis=-1)
        keep = (my_rank < capacity).astype(w.dtype)
        comb = jnp.einsum('tk,tke->te', w * keep, oh.astype(w.dtype))
        out = jnp.zeros_like(xf)
        for e in range(E):
            g = jax.nn.silu(xf @ gate_proj_w[e].T)
            u = xf @ up_proj_w[e].T
            y = g * u @ down_proj_w[e].T
            out = out + comb[:, e:e + 1] * y
        return out.reshape(B, S, D)
    x = L0_attn_x
    xn = _layernorm(x, axis=-1)
    x = x + _L0_attn_ref(xn, L0_attn_w_q, L0_attn_w_k, L0_attn_w_v, L0_attn_w_o) + _L0_ffn_ref(xn, L0_ffn_gate_w, L0_ffn_gate_b, L0_ffn_w1, L0_ffn_b1, L0_ffn_w2, L0_ffn_b2)
    xn = _layernorm(x, axis=-1)
    x = x + _L1_attn_ref(xn, L1_attn_W_qkv, L1_attn_b_qkv) + _L1_ffn_ref(xn, L1_ffn_Wqkv, L1_ffn_q_scale, L1_ffn_k_scale, L1_ffn_Wo, L1_ffn_ln_g, L1_ffn_ln_b, L1_ffn_W1, L1_ffn_b1, L1_ffn_W2, L1_ffn_b2)
    xn = _layernorm(x, axis=-1)
    x = x + _L2_attn_ref(xn, L2_attn_Wq, L2_attn_bq, L2_attn_Aq, L2_attn_Bq, L2_attn_Wk, L2_attn_bk, L2_attn_Ak, L2_attn_Bk, L2_attn_Wv, L2_attn_bv, L2_attn_Av, L2_attn_Bv, L2_attn_Wo, L2_attn_bo, L2_attn_Ao, L2_attn_Bo) + _L2_ffn_ref(xn, L2_ffn_w1, L2_ffn_b1, L2_ffn_w2, L2_ffn_b2)
    xn = _layernorm(x, axis=-1)
    x = x + _L3_attn_ref(xn, L3_attn_W_in, L3_attn_b_in, L3_attn_W_out, L3_attn_b_out, L3_attn_gamma, L3_attn_beta) + _L3_ffn_ref(xn, L3_ffn_gate_w, L3_ffn_gate_proj_w, L3_ffn_up_proj_w, L3_ffn_down_proj_w)
    return x

_drawn_inputs = setup_inputs


def setup_inputs(seed=0):
    import zlib

    import numpy as np

    out = dict(_drawn_inputs(seed))
    spreads = {'L0_ffn_gate_b': (0.0, 0.356),
     'L0_ffn_b1': (0.0, 0.8),
     'L0_ffn_b2': (0.0, 0.319),
     'L1_ffn_q_scale': (1.0, 0.6),
     'L1_ffn_k_scale': (1.0, 0.6),
     'L1_ffn_ln_g': (1.0, 0.6),
     'L1_ffn_ln_b': (0.0, 0.8),
     'L1_ffn_b1': (0.0, 0.8),
     'L1_ffn_b2': (0.0, 0.1),
     'L2_attn_bq': (0.0, 0.8),
     'L2_attn_bk': (0.0, 2.0),
     'L2_attn_bv': (0.0, 0.8),
     'L2_attn_bo': (0.0, 0.1),
     'L3_attn_b_in': (0.0, 0.8),
     'L3_attn_b_out': (0.0, 0.8),
     'L3_attn_gamma': (1.0, 0.6),
     'L3_attn_beta': (0.0, 0.8)}
    factors = {'L0_attn_w_q': 8.0,
     'L0_attn_w_k': 8.0,
     'L0_ffn_w1': 3.525,
     'L0_ffn_w2': 2.779,
     'L1_attn_b_qkv': 8.0,
     'L1_ffn_W1': 3.746,
     'L1_ffn_W2': 3.681,
     'L2_attn_Wq': 8.0,
     'L2_attn_Aq': 8.0,
     'L2_attn_Bq': 8.0,
     'L2_attn_Wk': 8.0,
     'L2_attn_Ak': 8.0,
     'L2_attn_Bk': 8.0,
     'L2_attn_Wv': 8.0,
     'L2_attn_Av': 8.0,
     'L2_attn_Bv': 8.0,
     'L2_attn_Wo': 5.225,
     'L2_attn_Ao': 8.0,
     'L2_attn_Bo': 8.0,
     'L2_ffn_w1': 3.478,
     'L2_ffn_b1': 8.0,
     'L2_ffn_w2': 3.381,
     'L2_ffn_b2': 5.74,
     'L3_attn_W_in': 8.0,
     'L3_attn_W_out': 8.0,
     'L3_ffn_gate_w': 8.0,
     'L3_ffn_gate_proj_w': 8.0,
     'L3_ffn_up_proj_w': 8.0,
     'L3_ffn_down_proj_w': 8.0}
    for name, (base, spread) in spreads.items():
        noise = np.random.default_rng([zlib.crc32(name.encode()), seed]).standard_normal(out[name].shape)
        drawn = base * np.exp(spread * noise) if base else spread * noise
        out[name] = jnp.asarray(drawn.astype(out[name].dtype))
    for name, factor in factors.items():
        out[name] = (out[name] * factor).astype(out[name].dtype)
    return out
```

```python
from contextlib import ExitStack

import numpy as np

import concourse.bass as bass
from concourse import mybir

F32 = mybir.dt.float32
BF16 = mybir.dt.bfloat16
ACT = mybir.ActivationFunctionType
ALU = mybir.AluOpType
X_AXIS = mybir.AxisListType.X
XY_AXIS = mybir.AxisListType.XY

D = 128
SEQ = 256
TOK = 16 * SEQ
GT = 512
NG = TOK // GT
NT = TOK // 128
HEADS = 16
EPS = 1e-5
LN_EXP = "natural_log_exp_and_others"
NEG = -1.0e30


START = 1


def at_group(g, width=GT):
    return bass.ds(g * width, width)


class Stage:

    def __init__(self, nc, name):
        self.nc, self.name, self.ctx, self.semaphores = nc, name, ExitStack(), []

    def __enter__(self):
        self.ctx.__enter__()
        return self

    def __exit__(self, *a):
        left = self.ctx.__exit__(*a)
        if a[0] is None:
            self.nc.clear_and_free_semaphores(self.semaphores)
            self.nc.all_engine_barrier()
        return left

    def sb(self, name, shape, dt=F32):
        return self.ctx.enter_context(self.nc.sbuf_tensor(f"{self.name}_{name}", shape, dt))

    def ps(self, name, shape, dt=F32):
        return self.ctx.enter_context(self.nc.psum_tensor(f"{self.name}_{name}_ps", shape, dt))

    def sems(self, names):
        new = [self.nc.alloc_semaphore(f"{self.name}_{n}") for n in names.split()]
        self.semaphores += new
        return new

    def block(self):
        for semaphore in self.semaphores:
            self.nc.gpsimd.sem_inc(semaphore, 1)
        self.nc.all_engine_barrier()
        return self.ctx.enter_context(self.nc.Block())


def load_stage(nc, R, IN):
    with Stage(nc, "load") as s:
        raw = s.sb("raw", [128, IN["c_bf"].shape[1]])
        (loaded, cast) = s.sems("loaded cast")
        block = s.block()

        @block.sync
        def _(sp):
            sp.dma_start(R["x"][:, :], IN["x_t"]).then_inc(loaded, 16)
            sp.dma_start(R["ident"][:, :], IN["c_ident"]).then_inc(loaded, 16)
            sp.dma_start(raw[:, :], IN["c_bf"]).then_inc(loaded, 16)
            sp.wait_ge(loaded, START + 48)

        @block.vector
        def _(ve):
            ve.memset(R["mean_w"][:, :], 1.0 / D).then_inc(cast, 1)
            ve.memset(R["eps"][:, :], EPS).then_inc(cast, 1)
            ve.wait_ge(loaded, START + 48)
            ve.tensor_copy(R["c_bf"][:, :], raw[:, :]).then_inc(cast, 1)
            ve.tensor_copy(R["pair_cols"][:, :], raw[:, raw.shape[1] - 2:]).then_inc(cast, 1)
            ve.wait_ge(cast, START + 4)


def norm_stage(nc, R, name, again=False):
    with Stage(nc, name) as s:
        xc, sq, lnv, rstd = (s.sb(n, [128, GT]) for n in ("xc", "sq", "lnv", "rstd"))
        mean_ps, var_ps = s.ps("mean", [128, GT]), s.ps("var", [128, GT])
        mean_done, centred, squared, var_done, ln_done, rstd_done, normed = s.sems(
            "mean_done centred squared var_done ln_done rstd_done normed")
        block = s.block()
        x, xn = (R["xn"], R["xn"]) if again else (R["x"], R["xn"])

        @block.tensor
        def _(pe):
            with pe.Fori(0, NG) as g:
                pe.wait_ge(centred, START + g)
                pe.matmul(mean_ps[:, :], R["mean_w"][:, :], x[:, at_group(g)], start=True, stop=True).then_inc(mean_done, 1)
                pe.wait_ge(squared, START + g + 1)
                pe.matmul(var_ps[:, :], R["mean_w"][:, :], sq[:, :], start=True, stop=True).then_inc(var_done, 1)

        @block.scalar
        def _(act):
            act.preload_act_table_set(LN_EXP)
            with act.Fori(0, NG) as g:
                act.wait_ge(centred, START + g + 1)
                act.activation(sq[:, :], xc[:, :], ACT.Square).then_inc(squared, 1)
                act.wait_ge(var_done, START + g + 1)
                act.activation(lnv[:, :], var_ps[:, :], ACT.Ln, bias=R["eps"][:, :]).then_inc(ln_done, 1)
                act.wait_ge(ln_done, START + g + 1)
                act.wait_ge(normed, START + g)
                act.activation(rstd[:, :], lnv[:, :], ACT.Exp, scale=-0.5).then_inc(rstd_done, 1)

        @block.vector
        def _(ve):
            with ve.Fori(0, NG) as g:
                ve.wait_ge(mean_done, START + g + 1)
                ve.wait_ge(normed, START + g)
                ve.tensor_tensor(xc[:, :], x[:, at_group(g)], mean_ps[:, :], ALU.subtract).then_inc(centred, 1)
                ve.wait_ge(rstd_done, START + g + 1)
                ve.tensor_tensor(xn[:, at_group(g)], xc[:, :], rstd[:, :], ALU.mult).then_inc(normed, 1)


def attn8_stage(nc, R, name, W, scale, affine=False, rope=False, project=False, residual=False):
    R8 = 32
    with Stage(nc, name) as s:
        xs = s.sb("xs", [128, GT])
        wq, wk = s.sb("wq", [128, 4, 128]), s.sb("wk", [128, 4, 128])
        wv, vb = s.sb("wv", [128, D]), s.sb("vb", [128, D])
        qkb, low = s.sb("qkb", [128, 8]), s.sb("low", [128, 2])
        full = s.sb("full", [128, 2, GT])
        high = s.sb("high", [128, 2, GT], BF16)
        qk = s.sb("qk", [128, 8, GT], BF16)
        q2 = s.sb("q2", [128, 2, SEQ], BF16)
        zero = s.sb("zero", [128, 1])
        v = s.sb("v", [128, 4, HEADS, 9])
        negmax = s.sb("negmax", [128, 2, 2, 4])
        mpad = s.sb("mpad", [128, 2, 2, 4, 32], BF16)
        e = s.sb("e", [128, 4, 2 * SEQ])
        rden = s.sb("rden", [128, 2, HEADS])
        on = s.sb("on", [128, 2, D])
        ot = s.sb("ot", [128, GT])
        s_ps = s.ps("s", [128, 4, 512])
        st_ps = s.ps("st", [128, 2, 512])
        o_ps = s.ps("o", [128, 2, HEADS, 9])
        m_ps = s.ps("m", [128, 512])
        (loaded, zeroed, xs_ready, proj_done, full_ready, high_ready, qk_ready, v_done, v_ready, s_done, max_ready,
         mhi_ready, mpad_ready, mt_done, q2_ready, st_done, e_ready, pv_done, rden_ready, on_ready, ot_done,
         ot_ready, y_done, x_added, aux, tmp_ready) = s.sems(
            "loaded zeroed xs_ready proj_done full_ready high_ready qk_ready v_done v_ready s_done max_ready "
            "mhi_ready mpad_ready mt_done q2_ready st_done e_ready pv_done rden_ready on_ready ot_done "
            "ot_ready y_done x_added aux tmp_ready")
        n_load = 6
        if project:
            wo, wob = s.sb("wo", [128, D]), s.sb("wob", [128, 1])
            yt = s.sb("yt", [128, GT])
            n_load += 2
        if W.get("lora"):
            lora_a, lora_b = s.sb("lora_a", [8, 4, 128]), s.sb("lora_b", [8, 4, 512])
            n_load += 2
        if affine:
            gamma, beta = s.sb("gamma", [128, 1]), s.sb("beta", [128, 1])
            n_load += 2
        if rope:
            cos, sin = s.sb("cos", [128, SEQ]), s.sb("sin", [128, SEQ])
            wqr, wkr = s.sb("wqr", [128, 4, 128]), s.sb("wkr", [128, 4, 128])
            qkbr = s.sb("qkbr", [128, 8])
            full_r = s.sb("full_r", [128, 2, GT])
            t1 = s.sb("t1", [128, 2, GT])
            t2 = s.sb("t2", [128, 2, GT])
            n_load += 5
            (rot_done, rot_ready, t_ready) = s.sems("rot_done rot_ready t_ready")
        if not project:
            mix, mix_sel, mix_mask = s.sb("mix", [128, 2, HEADS, 128]), s.sb("mix_sel", [128, 8]), s.sb("mix_mask", [128, 128])
            (mix_ready,) = s.sems("mix_ready")
            n_load += 2
        block = s.block()
        ident = R["ident"]
        identb = R["ident_bf"]
        x, xn = R["x"], R["xn"]
        mt_ps = m_ps[:, :].bitcast(BF16)
        nw = 1 if W.get("lora") else 0

        @block.sync
        def _(sp):
            for dst, src in ((wq, W["wq"]), (wk, W["wk"])):
                sp.dma_start(dst[:, :, :], src).then_inc(loaded, 16)
            sp.dma_start(wv[:, :], W["wv"]).then_inc(loaded, 16)
            sp.dma_start(vb[:, :], W["vb"].broadcast_to([128, D])).then_inc(loaded, 16)
            sp.dma_start(qkb[:, :], W["qkb"]).then_inc(loaded, 16)
            sp.dma_start(low[:, :], W["low"]).then_inc(loaded, 16)
            if project:
                sp.dma_start(wo[:, :], W["wo"]).then_inc(loaded, 16)
                sp.dma_start(wob[:, :], W["wob"]).then_inc(loaded, 16)
            if not project:
                sp.dma_start(mix_sel[:, :], W["mix_sel"]).then_inc(loaded, 16)
                sp.dma_start(mix_mask[:, :], W["mix_mask"]).then_inc(loaded, 16)
            if W.get("lora"):
                sp.dma_start(lora_a[:, :, :], W["lora_a"]).then_inc(loaded, 16)
                sp.dma_start(lora_b[:, :, :], W["lora_b"]).then_inc(loaded, 16)
            if affine:
                sp.dma_start(gamma[:, :], W["gamma"]).then_inc(loaded, 16)
                sp.dma_start(beta[:, :], W["beta"]).then_inc(loaded, 16)
            if rope:
                sp.dma_start(cos[:, :], W["cos"]).then_inc(loaded, 16)
                sp.dma_start(sin[:, :], W["sin"]).then_inc(loaded, 16)
                sp.dma_start(wqr[:, :, :], W["wqr"]).then_inc(loaded, 16)
                sp.dma_start(wkr[:, :, :], W["wkr"]).then_inc(loaded, 16)
                sp.dma_start(qkbr[:, :], W["qkbr"]).then_inc(loaded, 16)
            sp.wait_ge(loaded, START + 16 * n_load)

        @block.tensor
        def _(pe):
            pe.wait_ge(loaded, START + 16 * n_load)
            pe.wait_ge(zeroed, START + 3)
            if W.get("lora"):
                for n in range(4):
                    width = 512 if n < 2 else 128
                    mm = pe.matmul(s_ps[:, n, 0:width], lora_a[:, n, :], lora_b[:, n, 0:width], start=True, stop=True)
                    mm.then_inc(aux, 1)
                pe.wait_ge(tmp_ready, START + 4)

            def scores(g, u):
                b, a = divmod(u, 4)
                for pair in range(2):
                    if u == 0:
                        pe.wait_ge(full_ready, START + g * 8 + 8)
                        pe.wait_ge(qk_ready, START + g * 8 + 8)
                        if rope:
                            pe.wait_ge(rot_ready, START + g * 8 + 8)
                    else:
                        pe.wait_ge(max_ready, START + g * 16 + 2 * (u - 1) + pair + 1)
                    for j in (2 * pair, 2 * pair + 1):
                        p = slice(R8 * j, R8 * j + R8)
                        for t in range(2):
                            at = b * SEQ + t * 128
                            mm = pe.matmul(s_ps[:, j, t * SEQ:(t + 1) * SEQ], qk[p, a, at:at + 128],
                                           qk[p, 4 + a, b * SEQ:(b + 1) * SEQ], start=True, stop=True)
                    mm.then_inc(s_done, 1)

            def values(g, u, j):
                b, a = divmod(u, 4)
                h = 4 * a + j
                pe.wait_ge(e_ready, START + g * 32 + 4 * u + j + 1)
                if a == 0 and j == 0 and not (u == 0):
                    pe.wait_ge(on_ready, START + g * 2 + b)
                for t in range(2):
                    for k in range(2):
                        mm = pe.matmul(o_ps[:, t, h, :], e[:, j, k * SEQ + t * 128:k * SEQ + t * 128 + 128],
                                       v[:, 2 * b + k, h, :], start=(k == 0), stop=(k == 1))
                mm.then_inc(pv_done, 1)

            with pe.Fori(0, NG) as g:
                pe.wait_ge(xs_ready, START + g + 1)
                pe.wait_ge(max_ready, START + g * 16)
                for i in range(8):
                    a = i % 4
                    w = (wq if i < 4 else wk)
                    bank = i % 4 if not rope else 2 * (i % 2)
                    back = 4 if not rope else 2
                    if i >= back:
                        pe.wait_ge(full_ready, START + g * 8 + i - back + 1)
                        if rope:
                            pe.wait_ge(rot_ready, START + g * 8 + i - back + 1)
                    pe.matmul(s_ps[:, bank, :], w[:, a, :], xs[:, :], start=True, stop=True).then_inc(proj_done, 1)
                    if rope:
                        wr = (wqr if i < 4 else wkr)
                        pe.matmul(s_ps[:, bank + 1, :], wr[:, a, :], xs[:, :], start=True, stop=True).then_inc(rot_done, 1)
                pe.wait_ge(x_added if not project else ot_ready, START + (g * 2 if True else 0))
                for t in range(4):
                    mm = pe.matmul(m_ps[:, t * D:(t + 1) * D], xs[:, t * 128:(t + 1) * 128], wv[:, :], start=True, stop=True)
                mm.then_inc(v_done, 1)
                scores(g, 0)
                for u in range(8):
                    b, a = divmod(u, 4)
                    if u < 7:
                        scores(g, u + 1)
                    pe.wait_ge(mpad_ready, START + g * 8 + u + 1)
                    if u == 0:
                        pe.wait_ge(v_ready, START + g + 1)
                    else:
                        pe.wait_ge(q2_ready, START + g * 8 + u)
                    if u == 4:
                        pe.wait_ge(x_added if not project else ot_ready, START + g * 2 + 1)
                    for t in range(2):
                        mm = pe.transpose(mt_ps[:, t * 128:(t + 1) * 128],
                                          mpad[:, u % 2, t, :, :].rearrange("p j r -> p (j r)"), identb)
                    mm.then_inc(mt_done, 1)
                    pe.wait_ge(q2_ready, START + g * 8 + u + 1)
                    for j in range(4):
                        p = slice(R8 * j, R8 * j + R8)
                        n = 4 * u + j
                        if n >= 2:
                            pe.wait_ge(e_ready, START + g * 32 + n - 1)
                        else:
                            pe.wait_ge(e_ready, START + g * 32)
                        for k in range(2):
                            at = b * SEQ + k * 128
                            mm = pe.matmul(st_ps[:, j % 2, k * SEQ:(k + 1) * SEQ], qk[p, 4 + a, at:at + 128],
                                           q2[p, u % 2, :], start=True, stop=True)
                        mm.then_inc(st_done, 1)
                        if j >= 1:
                            values(g, u, j - 1)
                    values(g, u, 3)
                    if a == 3 and not project:
                        for t in range(2):
                            pe.wait_ge(mix_ready, START + g * 4 + 2 * b + t + 1)
                            for h in range(HEADS):
                                at = 256 + h * 16 + t * 8
                                mm = pe.matmul(m_ps[:, at:at + 8], mix[:, t, h, :], mix_sel[:, :], start=True, stop=True)
                        mm.then_inc(ot_done, 1)
                    elif a == 3:
                        pe.wait_ge(on_ready, START + g * 2 + b + 1)
                        for t in range(2):
                            mm = pe.transpose(m_ps[:, 256 + t * 128:384 + t * 128], on[:, t, :], ident[:, :])
                        mm.then_inc(ot_done, 1)
                if project:
                    pe.wait_ge(ot_ready, START + g * 2 + 2)
                    pe.matmul(st_ps[:, 0, :], wo[:, :], ot[:, :], start=True, stop=True).then_inc(y_done, 1)

        @block.scalar
        def _(act):
            act.preload_act_table_set(LN_EXP)
            act.wait_ge(loaded, START + 16 * n_load)

            def exps(g, u):
                for j in range(4):
                    act.wait_ge(st_done, START + g * 32 + 4 * u + j + 1)
                    act.wait_ge(pv_done, START + (g * 32 + 4 * (u - 1) + j + 1 if u else g * 32))
                    act.activation(e[:, j, :], st_ps[:, j % 2, :], ACT.Exp, scale=scale).then_inc(e_ready, 1)

            with act.Fori(0, NG) as g:
                act.wait_ge(v_done, START + g)
                if affine:
                    act.activation(xs[:, :], xn[:, at_group(g)], ACT.Identity, bias=beta[:, :], scale=gamma[:, :]).then_inc(xs_ready, 1)
                else:
                    act.activation(xs[:, :], xn[:, at_group(g)], ACT.Copy).then_inc(xs_ready, 1)
                for i in range(8):
                    act.wait_ge(proj_done, START + g * 8 + i + 1)
                    if i >= 2:
                        act.wait_ge(t_ready if rope else qk_ready, START + ((g * 24 + 3 * (i - 2) + 3) if rope else (g * 8 + i - 1)))
                    bank = i % 4 if not rope else 2 * (i % 2)
                    act.activation(full[:, i % 2, :], s_ps[:, bank, :], ACT.Identity, bias=qkb[:, i:i + 1]).then_inc(full_ready, 1)
                    if rope:
                        act.wait_ge(rot_done, START + g * 8 + i + 1)
                        act.activation(full_r[:, i % 2, :], s_ps[:, bank + 1, :], ACT.Identity, bias=qkbr[:, i:i + 1]).then_inc(rot_ready, 1)
                for u in range(8):
                    exps(g, u)

        @block.gpsimd
        def _(pool):
            pool.memset(mpad[:, :, :, :, :], 0.0).then_inc(zeroed, 1)
            pool.memset(v[:, :, :, :], 1.0).then_inc(zeroed, 1)
            pool.memset(zero[:, :], 0.0).then_inc(zeroed, 1)
            pool.wait_ge(zeroed, START + 3)
            with pool.Fori(0, NG) as g:
                for i in range(8):
                    if i >= 2:
                        pool.wait_ge(qk_ready, START + g * 8 + i - 1)
                    if rope:
                        pool.wait_ge(t_ready, START + g * 24 + 3 * i + 2)
                        pool.tensor_tensor(t1[:, i % 2, :], t1[:, i % 2, :], t2[:, i % 2, :], ALU.add).then_inc(t_ready, 1)
                        pool.wait_ge(t_ready, START + g * 24 + 3 * i + 3)
                        pool.tensor_tensor(high[:, i % 2, :], t1[:, i % 2, :], zero[:, :].to_broadcast([128, GT]), ALU.add).then_inc(high_ready, 1)
                    else:
                        pool.wait_ge(full_ready, START + g * 8 + i + 1)
                        pool.tensor_tensor(high[:, i % 2, :], full[:, i % 2, :], zero[:, :].to_broadcast([128, GT]), ALU.add).then_inc(high_ready, 1)
                if not project:
                    for b in range(2):
                        pool.wait_ge(on_ready, START + g * 2 + b + 1)
                        pool.wait_ge(ot_done, START + g * 2 + b)
                        for t in range(2):
                            pool.tensor_tensor(mix[:, t, :, :].rearrange("p h (s d) -> p h s d", d=8),
                                               on[:, t, :].rearrange("p (h d) -> p h d", h=HEADS).unsqueeze(2).to_broadcast([128, HEADS, 16, 8]),
                                               mix_mask[:, :].rearrange("p (s d) -> p s d", d=8).unsqueeze(1).to_broadcast([128, HEADS, 16, 8]),
                                               ALU.mult).then_inc(mix_ready, 1)

        @block.vector
        def _(ve):
            ve.wait_ge(loaded, START + 16 * n_load)
            ve.wait_ge(zeroed, START + 3)
            if W.get("lora"):
                for n, w in enumerate((wq, wk, wv, wo)):
                    view = w[:, :, :].rearrange("p a c -> p (a c)") if n < 2 else w[:, :]
                    ve.wait_ge(aux, START + n + 1)
                    ve.scalar_tensor_tensor(view, s_ps[:, n, 0:512 if n < 2 else 128], 2.0, view, ALU.mult, ALU.add).then_inc(tmp_ready, 1)
            two = lambda ap: ap.rearrange("p (b t) -> p b t", b=2)

            def maxima(g, u):
                b, a = divmod(u, 4)
                for pair in range(2):
                    ve.wait_ge(s_done, START + g * 16 + 2 * u + pair + 1)
                    src = s_ps[:, 2 * pair:2 * pair + 2, :].rearrange("p j (t k) -> p j t k", t=2)
                    dst = negmax[:, u % 2, :, 2 * pair:2 * pair + 2].rearrange("p t j -> p j t")
                    ve.tensor_reduce(dst, src, X_AXIS, ALU.max, negate=True).then_inc(max_ready, 1)
                ve.wait_ge(max_ready, START + g * 16 + 2 * u + 2)
                if u >= 2:
                    ve.wait_ge(mt_done, START + g * 8 + u - 1)
                ve.tensor_copy(mpad[:, u % 2, :, :, 24], negmax[:, u % 2, :, :]).then_inc(mhi_ready, 1)
                ve.wait_ge(mhi_ready, START + g * 8 + u + 1)
                ve.tensor_tensor(mpad[:, u % 2, :, :, 25], negmax[:, u % 2, :, :], mpad[:, u % 2, :, :, 24], ALU.subtract).then_inc(mpad_ready, 1)

            with ve.Fori(0, NG) as g:
                for i in range(8):
                    if rope:
                        ve.wait_ge(full_ready, START + g * 8 + i + 1)
                        if i >= 2:
                            ve.wait_ge(qk_ready, START + g * 8 + i - 1)
                            ve.wait_ge(high_ready, START + g * 8 + i - 1)
                        tab = lambda t: t[:, :].unsqueeze(1).to_broadcast([128, 2, SEQ])
                        ve.tensor_tensor(two(t1[:, i % 2, :]), two(full[:, i % 2, :]), tab(cos), ALU.mult).then_inc(t_ready, 1)
                        ve.wait_ge(rot_ready, START + g * 8 + i + 1)
                        ve.tensor_tensor(two(t2[:, i % 2, :]), two(full_r[:, i % 2, :]), tab(sin), ALU.mult).then_inc(t_ready, 1)
                        src = t1
                    else:
                        src = full
                    ve.wait_ge(high_ready, START + g * 8 + i + 1)
                    ve.scalar_tensor_tensor(qk[:, i, :], high[:, i % 2, :], low[:, i // 4:i // 4 + 1], src[:, i % 2, :],
                                            ALU.mult, ALU.add).then_inc(qk_ready, 1)
                ve.wait_ge(v_done, START + g + 1)
                vbb = vb[:, :].rearrange("p (h d) -> p h d", h=HEADS)
                for t in range(4):
                    vv = ve.tensor_tensor(v[:, t, :, 0:8], m_ps[:, t * D:(t + 1) * D].rearrange("p (h d) -> p h d", h=HEADS), vbb, ALU.add)
                vv.then_inc(v_ready, 1)
                maxima(g, 0)
                for u in range(8):
                    b, a = divmod(u, 4)
                    if u < 7:
                        maxima(g, u + 1)
                    ve.wait_ge(mt_done, START + g * 8 + u + 1)
                    if u >= 2:
                        ve.wait_ge(st_done, START + g * 32 + 4 * u - 4)
                    ve.tensor_tensor(q2[:, u % 2, :], qk[:, a, b * SEQ:(b + 1) * SEQ], mt_ps[:, 0:SEQ], ALU.add).then_inc(q2_ready, 1)
                    if a == 3:
                        ve.wait_ge(pv_done, START + g * 32 + 16 * b + 16)
                        ve.reciprocal(rden[:, :, :], o_ps[:, :, :, 8]).then_inc(rden_ready, 1)
                        ve.wait_ge(rden_ready, START + g * 2 + b + 1)
                        if b == 1:
                            ve.wait_ge(ot_done, START + g * 2 + 1)
                        for t in range(2):
                            nn = ve.tensor_tensor(on[:, t, :].rearrange("p (h d) -> p h d", h=HEADS), o_ps[:, t, :, 0:8],
                                                  rden[:, t, :].unsqueeze(2).to_broadcast([128, HEADS, 8]), ALU.mult)
                        nn.then_inc(on_ready, 1)
                        ve.wait_ge(ot_done, START + g * 2 + b + 1)
                        if project:
                            ve.tensor_copy(ot[:, b * SEQ:(b + 1) * SEQ], m_ps[:, 256:512]).then_inc(ot_ready, 1)
                        else:
                            xa = x[:, bass.ds(g * GT + b * SEQ, SEQ)]
                            ve.tensor_tensor(xa, xa, m_ps[:, 256:512], ALU.add).then_inc(x_added, 1)
                if project:
                    ve.wait_ge(y_done, START + g + 1)
                    ve.tensor_scalar(yt[:, :], st_ps[:, 0, :], wob[:, 0:1], None, ALU.add).then_inc(aux, 1)
                    ve.wait_ge(aux, START + g + 1 + 4 * nw)
                    ve.tensor_tensor(x[:, at_group(g)], x[:, at_group(g)], yt[:, :], ALU.add).then_inc(x_added, 1)
                    if residual:
                        ve.wait_ge(x_added, START + g * 2 + 1)
                        ve.tensor_tensor(x[:, at_group(g)], x[:, at_group(g)], xn[:, at_group(g)], ALU.add).then_inc(x_added, 1)


DH = 64
NB = HEADS * DH // 128


class Geometry:

    def __init__(self, R, band):
        m = R["masks"]
        if band:
            self.first_key, self.last_query = 96, 160
            self.mask_q0, self.mask_q1 = m["band"], m["band_q1"]
            self.mask_k0, self.mask_k1 = m["band_k0"], m["band_t"]
            self.q1_from = 0
        else:
            self.first_key, self.last_query = 0, 256
            self.mask_q0 = self.mask_q1 = m["causal"]
            self.mask_k0 = self.mask_k1 = m["causal_t"]
            self.q1_from = 128
        self.n_q1 = 256 - self.first_key


def attn64_core(nc, R, s, T, geo, scale, sem):
    qt, kt, v, on, negmax, mpad, mt, e = (T[n] for n in ("qt", "kt", "v", "on", "negmax", "mpad", "mt", "e"))
    s_ps, st_ps, o_ps = T["s_ps"], T["st_ps"], T["o_ps"]
    ident_bf, ones_rows = R["ident_bf"], R["pair_rows"]
    NU = 16

    class Core:
        @staticmethod
        def scores(pe, n, u):
            b, i = divmod(u, NB)
            slot = u % 2
            if u >= 2:
                pe.wait_ge(sem["max_ready"], START + n * NU + u - 1)
            for p in range(2):
                rows, bank = slice(64 * p, 64 * p + 64), 2 * slot + p
                pe.matmul(s_ps[:, bank, 0:128], qt[rows, i, b * SEQ:b * SEQ + 128],
                          kt[rows, i, b * SEQ:b * SEQ + 128], start=True, stop=False)
                pe.matmul(s_ps[:, bank, 0:128], ident_bf, geo.mask_q0, start=False, stop=True)
                lo, hi = 128, 128 + geo.n_q1
                pe.matmul(s_ps[:, bank, lo:hi], qt[rows, i, b * SEQ + 128:b * SEQ + SEQ],
                          kt[rows, i, b * SEQ + geo.first_key:(b + 1) * SEQ], start=True, stop=False)
                mm = pe.matmul(s_ps[:, bank, lo + geo.q1_from:hi], ident_bf, geo.mask_q1, start=False, stop=True)
            mm.then_inc(sem["s_done"], 1)

        @staticmethod
        def turn_max(pe, n, u):
            pe.wait_ge(sem["mpad_ready"], START + n * NU + u + 1)
            if u >= 2:
                pe.wait_ge(sem["o_read"], START + n * NU + u - 1)
            m_ps = o_ps[:, u % 2, 384:512].bitcast(BF16)
            for t in range(2):
                mm = pe.transpose(m_ps[:, t * 128:(t + 1) * 128],
                                  mpad[:, u % 2, t, :, :].rearrange("p h r -> p (h r)"), ident_bf)
            mm.then_inc(sem["mt_done"], 1)

        @staticmethod
        def turned_scores(pe, n, u, p):
            b, i = divmod(u, NB)
            rows = slice(64 * p, 64 * p + 64)
            m_rows = slice(64 * p, 64 * p + 2)
            pe.wait_ge(sem["mt_ready"], START + n * NU + u + 1)
            if 2 * u + p >= 2:
                pe.wait_ge(sem["e_ready"], START + (n * NU + u) * 2 + p - 1)
            n0 = geo.last_query
            for k, (lo, hi, q0) in enumerate(((0, n0, 0), (n0, n0 + 128, 128))):
                mask = (geo.mask_k0, geo.mask_k1)[k]
                nm = mask.shape[1]
                pe.matmul(st_ps[:, p, lo:hi], kt[rows, i, b * SEQ + k * 128:b * SEQ + k * 128 + 128],
                          qt[rows, i, b * SEQ + q0:b * SEQ + q0 + hi - lo], start=True, stop=False)
                pe.matmul(st_ps[:, p, lo:hi], ones_rows[m_rows, :], mt[m_rows, u % 2, q0:q0 + hi - lo], start=False, stop=False)
                mm = pe.matmul(st_ps[:, p, lo:lo + nm], ident_bf, mask, start=False, stop=True)
            mm.then_inc(sem["st_done"], 1)

        @staticmethod
        def values(pe, n, u, p):
            b, i = divmod(u, NB)
            pe.wait_ge(sem["e_ready"], START + (n * NU + u) * 2 + p + 1)
            n0 = geo.last_query
            h = 2 * i + p
            out = lambda t, m=128: o_ps[0:m, u % 2, (2 * t + p) * 65:(2 * t + p + 1) * 65]
            pe.matmul(out(0), e[:, u % 2, p, 0:128], v[:, 2 * b, h, :], start=True, stop=True)
            pe.matmul(out(1), e[:, u % 2, p, n0:n0 + 128], v[:, 2 * b + 1, h, :], start=True, stop=(n0 < 256))
            m = n0 - 128
            mm = pe.matmul(out(1, m), e[:, u % 2, p, 128:n0], v[:, 2 * b, h, :], start=False, stop=True,
                           skip_group_check=(n0 < 256))
            mm.then_inc(sem["pv_done"], 1)

        @staticmethod
        def exps(act, n, u, p):
            act.wait_ge(sem["st_done"], START + (n * NU + u) * 2 + p + 1)
            if u >= 2:
                act.wait_ge(sem["pv_done"], START + (n * NU + u - 2) * 2 + p + 1)
            w = geo.last_query + 128
            act.activation(e[:, u % 2, p, 0:w], st_ps[:, p, 0:w], ACT.Exp, scale=scale).then_inc(sem["e_ready"], 1)

        @staticmethod
        def maxima(ve, n, u):
            slot = u % 2
            ve.wait_ge(sem["s_done"], START + n * NU + u + 1)
            banks = s_ps[:, 2 * slot:2 * slot + 2, :]
            ve.tensor_reduce(negmax[:, slot, 0, :], banks[:, :, 0:128], X_AXIS, ALU.max, negate=True)
            ve.tensor_reduce(negmax[:, slot, 1, :], banks[:, :, 128:128 + geo.n_q1], X_AXIS, ALU.max, negate=True).then_inc(sem["max_ready"], 1)
            ve.wait_ge(sem["max_ready"], START + n * NU + u + 1)
            if u >= 2:
                ve.wait_ge(sem["mt_done"], START + n * NU + u - 1)
            ve.tensor_copy(mpad[:, slot, :, :, 0], negmax[:, slot, :, :]).then_inc(sem["mhi_ready"], 1)
            ve.wait_ge(sem["mhi_ready"], START + n * NU + u + 1)
            ve.tensor_tensor(mpad[:, slot, :, :, 1], negmax[:, slot, :, :], mpad[:, slot, :, :, 0], ALU.subtract).then_inc(sem["mpad_ready"], 1)

        @staticmethod
        def keep_max(ve, n, u):
            ve.wait_ge(sem["mt_done"], START + n * NU + u + 1)
            if u >= 2:
                ve.wait_ge(sem["st_done"], START + (n * NU + u - 1) * 2)
            ve.tensor_copy(mt[:, u % 2, :], o_ps[:, u % 2, 384:512].bitcast(BF16)).then_inc(sem["mt_ready"], 1)

        @staticmethod
        def normalise(ve, n, u):
            b, i = divmod(u, NB)
            T_ = T["rden"]
            ve.wait_ge(sem["pv_done"], START + (n * NU + u) * 2 + 2)
            o = o_ps[:, u % 2, 0:260].rearrange("q (t d) -> q t d", t=4)
            ve.reciprocal(T_[:, u % 2, :], o[:, :, 64]).then_inc(sem["rden_ready"], 1)
            ve.wait_ge(sem["rden_ready"], START + n * NU + u + 1)
            for t in range(2):
                dst = on[:, 2 * b + t, i * 128:(i + 1) * 128].rearrange("q (h d) -> q h d", h=2)
                nn = ve.tensor_tensor(dst, o[:, 2 * t:2 * t + 2, 0:64],
                                      T_[:, u % 2, 2 * t:2 * t + 2].unsqueeze(2).to_broadcast([128, 2, 64]), ALU.mult)
            nn.then_inc(sem["o_read"], 1)

        @staticmethod
        def turn_out(pe, n, i):
            if i == 0:
                pe.wait_ge(sem["max_ready"], START + n * NU + NU)
                pe.wait_ge(sem["o_read"], START + n * NU + NU)
            if i >= 4:
                pe.wait_ge(sem["ot_ready"], START + n * NB + i - 3)
            for t in range(4):
                mm = pe.transpose(s_ps[:, i % 4, t * 128:(t + 1) * 128], on[:, t, i * 128:(i + 1) * 128], R["ident"][:, :])
            mm.then_inc(sem["ot_done"], 1)

    return Core


CORE_SEMS = ("max_ready s_done mpad_ready mhi_ready mt_done mt_ready st_done e_ready pv_done o_read rden_ready "
             "ot_done ot_ready").split()


def named(s, names):
    return dict(zip(names, s.sems(" ".join(names))))


def attn64_tiles(s):
    return {
        "qt": s.sb("qt", [128, NB, GT]), "kt": s.sb("kt", [128, NB, GT]),
        "v": s.sb("v", [128, 4, HEADS, DH + 1]), "on": s.sb("on", [128, 4, HEADS * DH]),
        "negmax": s.sb("negmax", [128, 2, 2, 2]), "mpad": s.sb("mpad", [128, 2, 2, 2, 64], BF16),
        "mt": s.sb("mt", [128, 2, SEQ], BF16), "e": s.sb("e", [128, 2, 2, 384]),
        "rden": s.sb("rden", [128, 2, 4]), "ot": s.sb("ot", [128, 2, GT]),
        "s_ps": s.ps("s", [128, 4, 512]), "st_ps": s.ps("st", [128, 2, 512]), "o_ps": s.ps("o", [128, 2, 512]),
    }


def attn64_stage(nc, R, name, W, scale):
    with Stage(nc, name) as s:
        T = attn64_tiles(s)
        xs = s.sb("xs", [128, GT])
        wq, wk, wv, wo = (s.sb(n, [128, HEADS * DH]) for n in ("wq", "wk", "wv", "wo"))
        geo = Geometry(R, band=False)
        sem = named(s, CORE_SEMS + ["loaded", "zeroed", "xs_ready", "proj_done", "proj_ready", "v_done", "v_ready", "y_done", "x_added"])
        core = attn64_core(nc, R, s, T, geo, scale, sem)
        block = s.block()
        x, xn = R["x"], R["xn"]
        qt, kt, v, ot = T["qt"], T["kt"], T["v"], T["ot"]
        s_ps, st_ps = T["s_ps"], T["st_ps"]

        @block.sync
        def _(sp):
            for dst, src in ((wq, "wq"), (wk, "wk"), (wv, "wv"), (wo, "wo")):
                sp.dma_start(dst[:, :], W[src]).then_inc(sem["loaded"], 16)
            sp.wait_ge(sem["loaded"], START + 64)

        @block.tensor
        def _(pe):
            pe.wait_ge(sem["loaded"], START + 64)
            pe.wait_ge(sem["zeroed"], START + 2)
            with pe.Fori(0, NG) as g:
                pe.wait_ge(sem["xs_ready"], START + g + 1)
                pe.wait_ge(sem["ot_ready"], START + g * NB)
                for i in range(16):
                    w, c = (wq, i) if i < NB else (wk, i - NB)
                    if i >= 4:
                        pe.wait_ge(sem["proj_ready"], START + g * 16 + i - 3)
                    pe.matmul(s_ps[:, i % 4, :], w[:, c * 128:(c + 1) * 128], xs[:, :], start=True, stop=True).then_inc(sem["proj_done"], 1)
                for i in range(8):
                    t, half = divmod(i, 2)
                    pe.wait_ge(sem["v_ready"], START + (g * 8 + i - 1 if i >= 2 else g * 8))
                    if i == 0:
                        pe.wait_ge(sem["x_added"], START + g)
                    pe.matmul(st_ps[:, half, :], xs[:, t * 128:(t + 1) * 128], wv[:, half * 512:(half + 1) * 512], start=True, stop=True).then_inc(sem["v_done"], 1)
                pe.wait_ge(sem["proj_ready"], START + g * 16 + 16)
                pe.wait_ge(sem["v_ready"], START + g * 8 + 8)
                core.scores(pe, g, 0)
                for u in range(16):
                    if u < 15:
                        core.scores(pe, g, u + 1)
                    core.turn_max(pe, g, u)
                    core.turned_scores(pe, g, u, 0)
                    core.turned_scores(pe, g, u, 1)
                    core.values(pe, g, u, 0)
                    core.values(pe, g, u, 1)
                for i in range(NB):
                    core.turn_out(pe, g, i)
                    if i >= 1:
                        pe.wait_ge(sem["ot_ready"], START + g * NB + i)
                        pe.matmul(st_ps[:, 0, :], wo[:, (i - 1) * 128:i * 128], ot[:, (i - 1) % 2, :], start=(i == 1), stop=False)
                pe.wait_ge(sem["ot_ready"], START + g * NB + NB)
                pe.matmul(st_ps[:, 0, :], wo[:, (NB - 1) * 128:], ot[:, (NB - 1) % 2, :], start=False, stop=True).then_inc(sem["y_done"], 1)

        @block.scalar
        def _(act):
            act.preload_act_table_set(LN_EXP)
            with act.Fori(0, NG) as g:
                act.wait_ge(sem["v_done"], START + g * 8)
                act.activation(xs[:, :], xn[:, at_group(g)], ACT.Copy).then_inc(sem["xs_ready"], 1)
                for i in range(16):
                    dst = qt if i < NB else kt
                    act.wait_ge(sem["proj_done"], START + g * 16 + i + 1)
                    act.activation(dst[:, i % NB, :], s_ps[:, i % 4, :], ACT.Copy).then_inc(sem["proj_ready"], 1)
                for u in range(16):
                    for p in range(2):
                        core.exps(act, g, u, p)

        @block.gpsimd
        def _(pool):
            pool.memset(T["mpad"][:, :, :, :, :], 0.0).then_inc(sem["zeroed"], 1)
            pool.memset(v[:, :, :, :], 1.0).then_inc(sem["zeroed"], 1)

        @block.vector
        def _(ve):
            ve.wait_ge(sem["zeroed"], START + 2)
            with ve.Fori(0, NG) as g:
                for i in range(8):
                    t, half = divmod(i, 2)
                    ve.wait_ge(sem["v_done"], START + g * 8 + i + 1)
                    ve.tensor_copy(v[:, t, 8 * half:8 * half + 8, 0:DH], st_ps[:, half, :].rearrange("p (h d) -> p h d", h=8)).then_inc(sem["v_ready"], 1)
                core.maxima(ve, g, 0)
                for u in range(16):
                    core.keep_max(ve, g, u)
                    if u < 15:
                        core.maxima(ve, g, u + 1)
                    core.normalise(ve, g, u)
                for i in range(NB):
                    ve.wait_ge(sem["ot_done"], START + g * NB + i + 1)
                    ve.tensor_copy(ot[:, i % 2, :], s_ps[:, i % 4, :]).then_inc(sem["ot_ready"], 1)
                ve.wait_ge(sem["y_done"], START + g + 1)
                ve.tensor_tensor(x[:, at_group(g)], x[:, at_group(g)], st_ps[:, 0, :], ALU.add).then_inc(sem["x_added"], 1)


def gate_stage(nc, R, name, W, capacity):
    NE = 8
    with Stage(nc, name) as s:
        wg, bias = s.sb("wg", [128, NE]), s.sb("bias", [128, NE])
        p_, sc, t_ = (s.sb(n, [128, NT, NE]) for n in ("p", "sc", "t"))
        oh = [s.sb(f"oh{k}", [128, NT, NE]) for k in range(2)]
        red, w_, sm, rk = (s.sb(n, [128, 2, NT]) for n in ("red", "w", "sm", "rk"))
        first = s.sb("first", [128, NE])
        lg = s.ps("lg", [128, NT * NE])
        loaded, gates_done, dv, exp_ready, cum_done = s.sems("loaded gates_done dv exp_ready cum_done")
        if capacity:
            ohb = s.sb("ohb", [128, NT, 2, NE], BF16)
            cum = [s.sb(f"cum{i}", [128, NT, 2, NE]) for i in range(2)]
            rank = s.sb("rank", [128, NT, 2, NE])
            cum_ps, tot_ps = s.ps("cumps", [128, NT * 2 * NE]), s.ps("totps", [128, NT * 2 * NE])
        block = s.block()
        comb = R["comb"]
        bc = lambda t: t.unsqueeze(2).to_broadcast([128, NT, NE])
        bt = lambda t: t.unsqueeze(1).to_broadcast([128, NT, NE])

        @block.sync
        def _(sp):
            sp.dma_start(wg[:, :], W["wg"]).then_inc(loaded, 16)
            if not capacity:
                sp.dma_start(bias[:, :], W["bg"].broadcast_to([128, NE])).then_inc(loaded, 16)
            sp.wait_ge(loaded, START + (16 if capacity else 32))

        @block.tensor
        def _(pe):
            pe.wait_ge(loaded, START + (16 if capacity else 32))
            for t in range(NT):
                mm = pe.matmul(lg[:, t * NE:(t + 1) * NE], R["xn"][:, t * 128:(t + 1) * 128], wg[:, :], start=True, stop=True)
            mm.then_inc(gates_done, 1)
            if capacity:
                pe.wait_ge(cum_done, START + 1)
                flat = ohb[:, :, :, :].rearrange("p t k e -> p (t k e)")
                pe.matmul(cum_ps[:, :], R["upper_bf"], flat, start=True, stop=True)
                pe.matmul(tot_ps[:, :], R["ones_bf"], flat, start=True, stop=True).then_inc(cum_done, 1)

        @block.scalar
        def _(act):
            act.preload_act_table_set(LN_EXP)
            act.wait_ge(dv, START + 4)
            act.activation(p_[:, :, :], sc[:, :, :], ACT.Exp).then_inc(exp_ready, 1)

        @block.gpsimd
        def _(pool):
            pass

        @block.vector
        def _(ve):
            step = [0]

            def done(ins):
                step[0] += 1
                ins.then_inc(dv, 1)
                ve.wait_ge(dv, START + step[0])

            logits = lg[:, :].rearrange("p (t e) -> p t e", e=NE)
            done(ve.tensor_copy(first[:, :], R["first"]))
            ve.wait_ge(gates_done, START + 1)
            if not capacity:
                ve.wait_ge(loaded, START + 32)
                done(ve.tensor_tensor(t_[:, :, :], logits, bt(bias[:, :]), ALU.add))
            else:
                done(ve.tensor_copy(t_[:, :, :], logits))
            done(ve.tensor_reduce(red[:, 0, :], t_[:, :, :], X_AXIS, ALU.max))
            done(ve.tensor_tensor(sc[:, :, :], t_[:, :, :], bc(red[:, 0, :]), ALU.subtract))
            ve.wait_ge(exp_ready, START + 1)
            done(ve.tensor_reduce(red[:, 0, :], p_[:, :, :], X_AXIS, ALU.add))
            done(ve.reciprocal(red[:, 1, :], red[:, 0, :]))
            done(ve.tensor_tensor(p_[:, :, :], p_[:, :, :], bc(red[:, 1, :]), ALU.mult))
            done(ve.tensor_copy(sc[:, :, :], p_[:, :, :]))
            for k in range(2):
                done(ve.tensor_reduce(w_[:, k, :], sc[:, :, :], X_AXIS, ALU.max))
                done(ve.tensor_tensor(t_[:, :, :], sc[:, :, :], bc(w_[:, k, :]), ALU.is_equal))
                done(ve.tensor_tensor(t_[:, :, :], t_[:, :, :], bt(first[:, :]), ALU.mult))
                done(ve.tensor_reduce(red[:, 0, :], t_[:, :, :], X_AXIS, ALU.max))
                done(ve.tensor_tensor(oh[k][:, :, :], bt(first[:, :]), bc(red[:, 0, :]), ALU.is_equal))
                if k == 0:
                    done(ve.scalar_tensor_tensor(sc[:, :, :], oh[0][:, :, :], -2.0, sc[:, :, :], ALU.mult, ALU.add))
            if capacity:
                done(ve.tensor_tensor(sm[:, 0, :], w_[:, 0, :], w_[:, 1, :], ALU.add))
                done(ve.tensor_scalar(sm[:, 0, :], sm[:, 0, :], 1e-9, None, ALU.add))
                done(ve.reciprocal(sm[:, 1, :], sm[:, 0, :]))
                for k in range(2):
                    done(ve.tensor_tensor(w_[:, k, :], w_[:, k, :], sm[:, 1, :], ALU.mult))
                    done(ve.tensor_copy(ohb[:, :, k, :], oh[k][:, :, :]))
                ve.tensor_copy(sm[:, 0, :], w_[:, 0, :]).then_inc(cum_done, 1)
                ve.wait_ge(cum_done, START + 2)
                v4 = lambda ps: ps[:, :].rearrange("p (t k e) -> p t k e", k=2, e=NE)
                done(ve.memset(cum[0][:, 0:1, :, :], 0.0))
                done(ve.tensor_copy(cum[0][:, 1:NT, :, :], v4(tot_ps)[:, 0:NT - 1]))
                at, d = 0, 1
                while d < NT:
                    a, b = cum[at], cum[1 - at]
                    done(ve.tensor_copy(b[:, 0:d, :, :], a[:, 0:d, :, :]))
                    done(ve.tensor_tensor(b[:, d:NT, :, :], a[:, d:NT, :, :], a[:, 0:NT - d, :, :], ALU.add))
                    at, d = 1 - at, 2 * d
                done(ve.tensor_tensor(rank[:, :, :, :], cum[at][:, :, :, :], v4(cum_ps), ALU.add))
                done(ve.tensor_tensor(rank[:, :, :, :], rank[:, :, :, :], ohb[:, :, :, :], ALU.mult))
                for k in range(2):
                    done(ve.tensor_reduce(rk[:, k, :], rank[:, :, k, :], X_AXIS, ALU.add))
                    done(ve.tensor_scalar(rk[:, k, :], rk[:, k, :], float(capacity) + 0.5, None, ALU.is_lt))
                    done(ve.tensor_tensor(w_[:, k, :], w_[:, k, :], rk[:, k, :], ALU.mult))
            done(ve.tensor_tensor(t_[:, :, :], oh[0][:, :, :], bc(w_[:, 0, :]), ALU.mult))
            done(ve.tensor_tensor(sc[:, :, :], oh[1][:, :, :], bc(w_[:, 1, :]), ALU.mult))
            done(ve.tensor_tensor(comb[:, :, :], t_[:, :, :], sc[:, :, :], ALU.add))


def experts_stage(nc, R, name, W, gated):
    NE = 8
    with Stage(nc, name) as s:
        HB = 2 if gated else 4
        xs = s.sb("xs", [128, GT])
        w1 = s.sb("w1", [128, NE, 512])
        w2 = s.sb("w2", [128, NE, HB, D])
        h = s.sb("h", [128, 2, HB, GT])
        cs = s.sb("cs", [128, 4, NE])
        acc = s.sb("acc", [128, 4, D])
        h_ps, y_ps = s.ps("h", [128, 4, 512]), s.ps("y", [128, 2, 512])
        i_ps, f_ps = s.ps("i", [128, 512]), s.ps("f", [128, 512])
        (loaded, xs_ready, cs_ready, h_done, h_ready, y_done, acc_step, f_done, x_added, init_done, ct_ready, ct_done, sg_ready) = s.sems(
            "loaded xs_ready cs_ready h_done h_ready y_done acc_step f_done x_added init_done ct_ready ct_done sg_ready")
        n_load = 2
        if gated:
            sg = s.sb("sg", [128, 2, 2, GT])
        else:
            b1, b2, ct = s.sb("b1", [128, NE, 4]), s.sb("b2", [NE, D]), s.sb("ct", [NE, GT])
            n_load = 4
        block = s.block()
        x, xn, comb, ident = R["x"], R["xn"], R["comb"], R["ident"]

        @block.sync
        def _(sp):
            sp.dma_start(w1[:, :, :], W["w1"]).then_inc(loaded, 16)
            sp.dma_start(w2[:, :, :, :], W["w2"]).then_inc(loaded, 16)
            if not gated:
                sp.dma_start(b1[:, :, :], W["b1"]).then_inc(loaded, 16)
                sp.dma_start(b2[:, :], W["b2"]).then_inc(loaded, 16)
            sp.wait_ge(loaded, START + 16 * n_load)

        @block.tensor
        def _(pe):
            pe.wait_ge(loaded, START + 16 * n_load)

            def hidden(g, ex):
                for i in range(4):
                    n = 4 * ex + i
                    if n >= 4:
                        pe.wait_ge(h_ready, START + g * 32 + n - 3)
                    else:
                        pe.wait_ge(h_ready, START + g * 32)
                    pe.matmul(h_ps[:, i, :], w1[:, ex, i * 128:(i + 1) * 128], xs[:, :], start=True, stop=True).then_inc(h_done, 1)

            def down(g, ex):
                pe.wait_ge(h_ready, START + g * 32 + 4 * ex + 4)
                if ex >= 2:
                    pe.wait_ge(acc_step, START + g * 9 + ex)
                else:
                    pe.wait_ge(acc_step, START + g * 9)
                for t in range(4):
                    for c in range(HB):
                        mm = pe.matmul(y_ps[:, ex % 2, t * D:(t + 1) * D], h[:, ex % 2, c, t * 128:(t + 1) * 128],
                                       w2[:, ex, c, :], start=(c == 0), stop=(c == HB - 1))
                mm.then_inc(y_done, 1)

            with pe.Fori(0, NG) as g:
                pe.wait_ge(xs_ready, START + g + 1)
                pe.wait_ge(cs_ready, START + g + 1)
                if not gated:
                    for t in range(4):
                        mm = pe.transpose(i_ps[0:NE, t * 128:(t + 1) * 128], cs[:, t, :], ident[:, :])
                    mm.then_inc(ct_done, 1)
                    pe.wait_ge(ct_ready, START + g + 1)
                    for t in range(4):
                        mm = pe.matmul(i_ps[:, t * D:(t + 1) * D], ct[:, t * 128:(t + 1) * 128], b2[:, :], start=True, stop=True)
                    mm.then_inc(init_done, 1)
                hidden(g, 0)
                for ex in range(NE):
                    if ex < NE - 1:
                        hidden(g, ex + 1)
                    down(g, ex)
                pe.wait_ge(acc_step, START + g * 9 + 9)
                for t in range(4):
                    mm = pe.transpose(f_ps[:, t * 128:(t + 1) * 128], acc[:, t, :], ident[:, :])
                mm.then_inc(f_done, 1)

        @block.scalar
        def _(act):
            act.wait_ge(loaded, START + 16 * n_load)
            with act.Fori(0, NG) as g:
                act.wait_ge(h_done, START + g * 32)
                act.activation(xs[:, :], xn[:, at_group(g)], ACT.Copy).then_inc(xs_ready, 1)
                for ex in range(NE):
                    if gated:
                        act.wait_ge(h_ready, START + (g * 32 + 4 * (ex - 1) if ex >= 2 else g * 32))
                    else:
                        act.wait_ge(y_done, START + (g * 8 + ex - 1 if ex >= 2 else g * 8))
                    if gated:
                        for i in range(2):
                            act.wait_ge(h_done, START + g * 32 + 4 * ex + 2 * i + 1)
                            act.activation(sg[:, ex % 2, i, :], h_ps[:, 2 * i, :], ACT.Silu).then_inc(sg_ready, 1)
                    else:
                        for i in range(4):
                            act.wait_ge(h_done, START + g * 32 + 4 * ex + i + 1)
                            act.activation(h[:, ex % 2, i, :], h_ps[:, i, :], ACT.Relu, bias=b1[:, ex, i:i + 1]).then_inc(h_ready, 1)

        @block.gpsimd
        def _(pool):
            pass

        @block.vector
        def _(ve):
            with ve.Fori(0, NG) as g:
                if not gated:
                    ve.wait_ge(ct_done, START + g)
                ve.wait_ge(acc_step, START + g * 9)
                ve.tensor_copy(cs[:, :, :], comb[:, bass.ds(g * 4, 4), :]).then_inc(cs_ready, 1)
                ve.wait_ge(cs_ready, START + g + 1)
                if gated:
                    ve.wait_ge(f_done, START + g)
                    ve.memset(acc[:, :, :], 0.0).then_inc(acc_step, 1)
                else:
                    ve.wait_ge(ct_done, START + g + 1)
                    ve.tensor_copy(ct[:, :], i_ps[0:NE, :]).then_inc(ct_ready, 1)
                    ve.wait_ge(init_done, START + g + 1)
                    ve.wait_ge(f_done, START + g)
                    ve.tensor_copy(acc[:, :, :], i_ps[:, :].rearrange("p (t d) -> p t d", t=4)).then_inc(acc_step, 1)

                def product(ex):
                    for i in range(2):
                        ve.wait_ge(h_done, START + g * 32 + 4 * ex + 2 * i + 2)
                        ve.wait_ge(sg_ready, START + g * 16 + 2 * ex + i + 1)
                        ve.tensor_tensor(h[:, ex % 2, i, :], sg[:, ex % 2, i, :], h_ps[:, 2 * i + 1, :], ALU.mult).then_inc(h_ready, 2)

                if gated:
                    product(0)
                for ex in range(NE):
                    if gated and ex < NE - 1:
                        if ex >= 1:
                            ve.wait_ge(y_done, START + g * 8 + ex)
                        product(ex + 1)
                    ve.wait_ge(y_done, START + g * 8 + ex + 1)
                    ve.wait_ge(acc_step, START + g * 9 + ex + 1)
                    for t in range(4):
                        a = ve.scalar_tensor_tensor(acc[:, t, :], y_ps[:, ex % 2, t * D:(t + 1) * D], cs[:, t, ex:ex + 1],
                                                    acc[:, t, :], ALU.mult, ALU.add)
                    a.then_inc(acc_step, 1)
                ve.wait_ge(f_done, START + g + 1)
                ve.tensor_tensor(x[:, at_group(g)], x[:, at_group(g)], f_ps[:, :], ALU.add).then_inc(x_added, 1)


def binary_stage(nc, R, name, W):
    with Stage(nc, name) as s:
        w1, w1t = s.sb("w1", [128, 4, D]), s.sb("w1t", [128, 512])
        w2, w2t = s.sb("w2", [128, 512]), s.sb("w2t", [128, 4, D])
        b1, b2 = s.sb("b1", [128, 4]), s.sb("b2", [128, 1])
        a1, a2 = s.sb("a1", [128, 4]), s.sb("a2", [128, 1])
        h = s.sb("h", [128, 2, 4, GT])
        yt = s.sb("yt", [128, GT])
        h_ps, y_ps = s.ps("h", [128, 4, 512]), s.ps("y", [128, 2, 512])
        loaded, summed, scaled, signed, h_done, h_ready, y_done, yt_ready, x_added = s.sems(
            "loaded summed scaled signed h_done h_ready y_done yt_ready x_added")
        block = s.block()
        x, xn = R["x"], R["xn"]

        @block.sync
        def _(sp):
            for dst, src in ((w1[:, :, :], "w1"), (w1t[:, :], "w1t"), (w2[:, :], "w2"), (w2t[:, :, :], "w2t"), (b1[:, :], "b1"), (b2[:, :], "b2")):
                sp.dma_start(dst, W[src]).then_inc(loaded, 16)
            sp.wait_ge(loaded, START + 96)

        @block.tensor
        def _(pe):
            pe.wait_ge(signed, START + 2)

            def up(g, n):
                for i in range(4):
                    pe.matmul(h_ps[:, i, :], w1t[:, i * 128:(i + 1) * 128], xn[:, at_group(g)], start=True, stop=True).then_inc(h_done, 1)

            with pe.Fori(0, NG) as g:
                up(g, 0)
                pe.wait_ge(h_ready, START + g * 4 + 4)
                pe.wait_ge(yt_ready, START + g)
                for i in range(4):
                    mm = pe.matmul(y_ps[:, 0, :], w2t[:, i, :], h[:, 0, i, :], start=(i == 0), stop=(i == 3))
                mm.then_inc(y_done, 1)

        @block.scalar
        def _(act):
            act.wait_ge(loaded, START + 96)
            act.activation(w1t[:, :], w1t[:, :], ACT.Sign).then_inc(signed, 1)
            act.activation(w2t[:, :, :], w2t[:, :, :], ACT.Sign).then_inc(signed, 1)
            act.wait_ge(scaled, START + 2)
            with act.Fori(0, NG) as g:
                for i in range(4):
                    act.wait_ge(h_done, START + g * 4 + i + 1)
                    if i == 0:
                        act.wait_ge(y_done, START + g)
                    act.activation(h[:, 0, i, :], h_ps[:, i, :], ACT.Gelu, bias=b1[:, i:i + 1], scale=a1[:, i:i + 1]).then_inc(h_ready, 1)

        @block.gpsimd
        def _(pool):
            pass

        @block.vector
        def _(ve):
            ve.wait_ge(loaded, START + 96)
            ve.tensor_reduce(a1[:, :], w1[:, :, :], X_AXIS, ALU.add, apply_absolute_value=True).then_inc(summed, 1)
            ve.tensor_reduce(a2[:, :], w2[:, :], X_AXIS, ALU.add, apply_absolute_value=True).then_inc(summed, 1)
            ve.wait_ge(summed, START + 2)
            ve.tensor_scalar(a1[:, :], a1[:, :], 1.0 / D, None, ALU.mult).then_inc(scaled, 1)
            ve.tensor_scalar(a2[:, :], a2[:, :], 1.0 / 512, None, ALU.mult).then_inc(scaled, 1)
            ve.wait_ge(scaled, START + 2)
            with ve.Fori(0, NG) as g:
                ve.wait_ge(y_done, START + g + 1)
                ve.wait_ge(x_added, START + g)
                ve.tensor_scalar(yt[:, :], y_ps[:, 0, :], a2[:, 0:1], b2[:, 0:1], ALU.mult, ALU.add).then_inc(yt_ready, 1)
                ve.wait_ge(yt_ready, START + g + 1)
                ve.tensor_tensor(x[:, at_group(g)], x[:, at_group(g)], yt[:, :], ALU.add).then_inc(x_added, 1)


DEPTH = 6
FF = 341
WA, WM = 6148, 1161
FB = [(0, 128), (128, 256), (256, 341)]


def local_stage(nc, R, name, W):
    with Stage(nc, name) as s:
        T = attn64_tiles(s)
        xs = s.sb("xs", [128, GT])
        wa, wm = s.sb("wa", [128, WA]), s.sb("wm", [128, WM])
        w_qk = wa[:, 0:2048].rearrange("p (a c) -> p a c", a=2)
        w_rot = wa[:, 2048:4096].rearrange("p (a c) -> p a c", a=2)
        wv, wo, scales = wa[:, 4096:5120], wa[:, 5120:6144], wa[:, 6144:6148]
        w1 = wm[:, 0:768].rearrange("p (a c) -> p a c", a=6)
        w2 = wm[:, 768:1152].rearrange("p (a c) -> p a c", a=3)
        cols = wm[:, 1152:1161]
        tables = s.sb("tables", [128, 4, SEQ])
        tab = s.sb("tab", [128, 4, SEQ])
        sq, m1, m2 = (s.sb(n, [128, 2, GT]) for n in ("sq", "m1", "m2"))
        nrm = s.sb("nrm", [128, 3, 128])
        rpad = s.sb("rpad", [128, 4, 3, 32], BF16)
        rt = s.sb("rt", [96, GT], BF16)
        xc, sqx, lnv, rstd, xg, y_t = (s.sb(n, [128, GT]) for n in ("xc", "sqx", "lnv", "rstd", "xg", "y_t"))
        gl, h = s.sb("gl", [128, 3, GT]), s.sb("h", [128, 3, GT])
        ten = s.sb("ten", [128, 1])
        geo = Geometry(R, band=True)
        sem = named(s, CORE_SEMS + [
            "loaded", "zeroed", "attn_w", "mlp_w", "tab_ready", "xs_ready", "proj_done", "rot_done", "squared", "m_ready",
            "summed", "norm_done", "norm_step", "split_ready", "rt_done", "rt_ready", "spread_done", "qk_ready", "v_done",
            "v_ready", "y_done", "y_added", "mean_done", "centred", "sqx_ready", "var_done", "ln_done", "rstd_ready", "xg_step",
            "xg_ready", "shifted", "up_done", "gl_ready", "h_ready", "out_done", "out_step", "out_added", "attn_free", "mlp_free", "x_added"])
        core = attn64_core(nc, R, s, T, geo, 8.0, sem)
        block = s.block()
        x, y = R["x"], R["xn"]
        qt, kt, v, ot = T["qt"], T["kt"], T["v"], T["ot"]
        s_ps, st_ps, o_ps = T["s_ps"], T["st_ps"], T["o_ps"]
        qk = [qt, kt]
        rp_ps = st_ps[:, 1, :]
        two = lambda ap: ap.rearrange("p (b t) -> p b t", b=2)
        n_attn, n_mlp = 5, 3

        @block.sync
        def _(sp):
            sp.dma_start(tables[:, :, :], W["tables"]).then_inc(sem["loaded"], 16)
            with sp.Fori(0, DEPTH) as d:
                off_a, off_m = sp.snap(d * (128 * WA)), sp.snap(d * (128 * WM))
                sp.wait_ge(sem["y_added"], START + d * NG)
                sp.dma_start(wa[:, :], W["wa"][bass.ds(off_a, 128 * WA)].rearrange("(p c) -> p c", p=128)).then_inc(sem["attn_w"], 16)
                sp.wait_ge(sem["out_added"], START + d * NG)
                sp.dma_start(wm[:, :], W["wm"][bass.ds(off_m, 128 * WM)].rearrange("(p c) -> p c", p=128)).then_inc(sem["mlp_w"], 16)
            sp.wait_ge(sem["attn_w"], START + DEPTH * 16)
            sp.wait_ge(sem["mlp_w"], START + DEPTH * 16)
            sp.wait_ge(sem["loaded"], START + 16)

        @block.tensor
        def _(pe):
            pe.wait_ge(sem["zeroed"], START + 5)

            def attn(n):
                pe.wait_ge(sem["xs_ready"], START + (2 * n + 1 if False else n + 1))
                pe.wait_ge(sem["ot_ready"], START + n * NB)
                for i in range(16):
                    a, c = divmod(i, NB)
                    bank = 2 * (i % 2)
                    pe.wait_ge(sem["m_ready"], START + (n * 32 + 2 * (i - 1) if i >= 2 else n * 32))
                    pe.wait_ge(sem["squared"], START + (n * 16 + i - 1 if i >= 2 else n * 16))
                    pe.matmul(s_ps[:, bank, :], w_qk[:, a, c * 128:(c + 1) * 128], xs[:, :], start=True, stop=True).then_inc(sem["proj_done"], 1)
                    pe.matmul(s_ps[:, bank + 1, :], w_rot[:, a, c * 128:(c + 1) * 128], xs[:, :], start=True, stop=True).then_inc(sem["rot_done"], 1)
                    if i >= 1:
                        norms(n, i - 1)
                norms(n, 15)
                for i in range(8):
                    t, half = divmod(i, 2)
                    pe.wait_ge(sem["v_ready"], START + (n * 8 + i - 1 if i >= 2 else n * 8))
                    pe.matmul(o_ps[:, half, :], xs[:, t * 128:(t + 1) * 128], wv[:, half * 512:(half + 1) * 512], start=True, stop=True).then_inc(sem["v_done"], 1)
                pe.wait_ge(sem["split_ready"], START + n + 1)
                turned = st_ps[0:96, 0, 0:256].bitcast(BF16)
                for t in range(4):
                    mm = pe.transpose(turned[:, t * 128:(t + 1) * 128], rpad[:, t, :, :].rearrange("p l h -> p (l h)"), R["ident_bf"])
                mm.then_inc(sem["rt_done"], 1)
                pe.wait_ge(sem["rt_ready"], START + n + 1)
                pe.wait_ge(sem["m_ready"], START + n * 32 + 32)
                for i in range(16):
                    if i >= 4:
                        pe.wait_ge(sem["qk_ready"], START + n * 16 + i - 3)
                    pe.matmul(s_ps[:, i % 4, :], R["head_rows"][:, i, :], rt[:, :], start=True, stop=True).then_inc(sem["spread_done"], 1)
                pe.wait_ge(sem["qk_ready"], START + n * 16 + 16)
                pe.wait_ge(sem["v_ready"], START + n * 8 + 8)
                core.scores(pe, n, 0)
                for u in range(16):
                    if u < 15:
                        core.scores(pe, n, u + 1)
                    core.turn_max(pe, n, u)
                    core.turned_scores(pe, n, u, 0)
                    core.turned_scores(pe, n, u, 1)
                    core.values(pe, n, u, 0)
                    core.values(pe, n, u, 1)
                for i in range(NB):
                    core.turn_out(pe, n, i)
                    if i >= 1:
                        pe.wait_ge(sem["ot_ready"], START + n * NB + i)
                        pe.matmul(st_ps[:, 0, :], wo[:, (i - 1) * 128:i * 128], ot[:, (i - 1) % 2, :], start=(i == 1), stop=False)
                pe.wait_ge(sem["ot_ready"], START + n * NB + NB)
                pe.matmul(st_ps[:, 0, :], wo[:, (NB - 1) * 128:], ot[:, (NB - 1) % 2, :], start=False, stop=True).then_inc(sem["y_done"], 1)

            def norms(n, i):
                pe.wait_ge(sem["squared"], START + n * 16 + i + 1)
                if i == 0:
                    pe.wait_ge(sem["norm_step"], START + n * 8)
                for t in range(4):
                    mm = pe.matmul(rp_ps[:, t * 32 + 2 * i:t * 32 + 2 * i + 2], sq[:, i % 2, t * 128:(t + 1) * 128], R["pair_cols"][:, :], start=True, stop=True)
                mm.then_inc(sem["norm_done"], 1)

            def mlp(n):
                pe.wait_ge(sem["shifted"], START + n + 1)
                pe.wait_ge(sem["out_added"], START + n)
                pe.matmul(s_ps[:, 0, :], R["mean_w"][:, :], xs[:, :], start=True, stop=True).then_inc(sem["mean_done"], 1)
                pe.wait_ge(sem["sqx_ready"], START + n + 1)
                pe.matmul(s_ps[:, 1, :], R["mean_w"][:, :], sqx[:, :], start=True, stop=True).then_inc(sem["var_done"], 1)
                pe.wait_ge(sem["xg_ready"], START + n + 1)
                banks = [st_ps[:, 0, :], st_ps[:, 1, :], o_ps[:, 0, :], s_ps[:, 2, :], s_ps[:, 3, :], o_ps[:, 1, :]]
                for i, (a, b) in enumerate(FB + FB):
                    pe.matmul(banks[i][0:b - a, :], w1[:, i, 0:b - a], xg[:, :], start=True, stop=True).then_inc(sem["up_done"], 1)
                for i, (a, b) in enumerate(FB):
                    pe.wait_ge(sem["h_ready"], START + n * 3 + i + 1)
                    mm = pe.matmul(s_ps[:, 0, :], w2[0:b - a, i, :], h[0:b - a, i, :], start=(i == 0), stop=(i == 2))
                mm.then_inc(sem["out_done"], 1)

            with pe.Fori(0, DEPTH) as d:
                with pe.Fori(0, NG) as g:
                    pe.wait_ge(sem["attn_w"], START + d * 16 + 16)
                    attn(d * NG + g)
                with pe.Fori(0, NG) as g:
                    pe.wait_ge(sem["mlp_w"], START + d * 16 + 16)
                    mlp(d * NG + g)

        @block.scalar
        def _(act):
            act.wait_ge(sem["zeroed"], START + 5)

            def shift(g, ready):
                act.activation(xs[0:64, :], y[0:64, at_group(g)], ACT.Copy)
                for b in range(2):
                    last = act.activation(xs[64:128, b * SEQ + 1:(b + 1) * SEQ], y[64:128, bass.ds(g * GT + b * SEQ, SEQ - 1)], ACT.Copy)
                last.then_inc(ready, 1)

            def attn(n, g, d):
                act.wait_ge(sem["v_done"], START + n * 8)
                act.wait_ge(sem["out_added"], START + d * NG)
                shift(g, sem["xs_ready"])
                for i in range(16):
                    act.wait_ge(sem["proj_done"], START + n * 16 + i + 1)
                    act.wait_ge(sem["m_ready"], START + n * 32 + 2 * i + 1)
                    act.wait_ge(sem["norm_done"], START + (n * 16 + i - 1 if i >= 2 else n * 16))
                    act.activation(sq[:, i % 2, :], s_ps[:, 2 * (i % 2), :], ACT.Square).then_inc(sem["squared"], 1)
                act.wait_ge(sem["norm_step"], START + n * 8 + 1)
                act.activation(nrm[:, 1, :], nrm[:, 0, :], ACT.Ln, scale=float(2 ** 20)).then_inc(sem["norm_step"], 1)
                act.wait_ge(sem["norm_step"], START + n * 8 + 2)
                act.activation(nrm[:, 0, :], nrm[:, 1, :], ACT.Exp, scale=-0.5, bias=ten[:, :]).then_inc(sem["norm_step"], 1)
                for u in range(16):
                    for p in range(2):
                        core.exps(act, n, u, p)

            def mlp(n, g, d):
                act.wait_ge(sem["v_done"], START + d * 64 + 64)
                act.wait_ge(sem["y_added"], START + d * NG + NG)
                act.wait_ge(sem["centred"], START + n)
                shift(g, sem["shifted"])
                act.wait_ge(sem["centred"], START + n + 1)
                act.activation(sqx[:, :], xc[:, :], ACT.Square).then_inc(sem["sqx_ready"], 1)
                act.wait_ge(sem["var_done"], START + n + 1)
                act.activation(lnv[:, :], s_ps[:, 1, :], ACT.Ln, bias=R["eps"][:, :]).then_inc(sem["ln_done"], 1)
                act.wait_ge(sem["ln_done"], START + n + 1)
                act.activation(rstd[:, :], lnv[:, :], ACT.Exp, scale=-0.5).then_inc(sem["rstd_ready"], 1)
                act.wait_ge(sem["xg_step"], START + n + 1)
                act.activation(xg[:, :], xc[:, :], ACT.Identity, scale=cols[:, 0:1], bias=cols[:, 1:2]).then_inc(sem["xg_ready"], 1)
                banks = [s_ps[:, 2, :], s_ps[:, 3, :], o_ps[:, 1, :]]
                for i, (a, b) in enumerate(FB):
                    act.wait_ge(sem["up_done"], START + n * 6 + 3 + i + 1)
                    act.activation(gl[0:b - a, i, :], banks[i][0:b - a, :], ACT.Gelu, bias=cols[0:b - a, 5 + i:6 + i]).then_inc(sem["gl_ready"], 1)

            with act.Fori(0, DEPTH) as d:
                act.preload_act_table_set(LN_EXP)
                with act.Fori(0, NG) as g:
                    attn(d * NG + g, g, d)
                with act.Fori(0, NG) as g:
                    mlp(d * NG + g, g, d)

        @block.gpsimd
        def _(pool):
            pool.memset(T["mpad"][:, :, :, :, :], 0.0).then_inc(sem["zeroed"], 1)
            pool.memset(v[:, :, :, :], 1.0).then_inc(sem["zeroed"], 1)
            pool.memset(rpad[:, :, :, :], 0.0).then_inc(sem["zeroed"], 1)
            pool.memset(xs[:, :], 0.0).then_inc(sem["zeroed"], 1)
            pool.memset(ten[:, :], float(10 * np.log(2.0))).then_inc(sem["zeroed"], 1)
            pool.wait_ge(sem["zeroed"], START + 5)

            with pool.Fori(0, DEPTH) as d:
                with pool.Fori(0, NG) as g:
                    n = d * NG + g
                    for i in range(16):
                        pool.wait_ge(sem["m_ready"], START + n * 32 + 2 * i + 2)
                        pool.tensor_tensor(qk[i // NB][:, i % NB, :], m1[:, i % 2, :], m2[:, i % 2, :], ALU.add).then_inc(sem["summed"], 1)

        @block.vector
        def _(ve):
            ve.wait_ge(sem["zeroed"], START + 5)
            ve.wait_ge(sem["loaded"], START + 16)

            def attn(n, g):
                for i in range(16):
                    a, c = divmod(i, NB)
                    if i >= 2:
                        ve.wait_ge(sem["summed"], START + n * 16 + i - 1)
                    else:
                        ve.wait_ge(sem["summed"], START + n * 16)
                    tb = lambda k: tab[:, k, :].unsqueeze(1).to_broadcast([128, 2, SEQ])
                    ve.wait_ge(sem["proj_done"], START + n * 16 + i + 1)
                    ve.tensor_tensor(two(m1[:, i % 2, :]), two(s_ps[:, 2 * (i % 2), :]), tb(2 * a), ALU.mult).then_inc(sem["m_ready"], 1)
                    ve.wait_ge(sem["rot_done"], START + n * 16 + i + 1)
                    ve.tensor_tensor(two(m2[:, i % 2, :]), two(s_ps[:, 2 * (i % 2) + 1, :]), tb(2 * a + 1), ALU.mult).then_inc(sem["m_ready"], 1)
                ve.wait_ge(sem["norm_done"], START + n * 16 + 16)
                ve.tensor_scalar(nrm[:, 0, :], rp_ps[:, 0:128], 1e-24, None, ALU.max).then_inc(sem["norm_step"], 1)
                for i in range(8):
                    t, half = divmod(i, 2)
                    ve.wait_ge(sem["v_done"], START + n * 8 + i + 1)
                    ve.tensor_copy(v[:, t, 8 * half:8 * half + 8, 0:DH], o_ps[:, half, :].rearrange("p (h d) -> p h d", h=8)).then_inc(sem["v_ready"], 1)
                ve.wait_ge(sem["norm_step"], START + n * 8 + 3)
                r = lambda k: nrm[:, k, :].rearrange("p (t h) -> p t h", t=4)
                ve.tensor_copy(rpad[:, :, 0, :], r(0)).then_inc(sem["norm_step"], 1)
                ve.wait_ge(sem["norm_step"], START + n * 8 + 4)
                ve.tensor_tensor(r(1), r(0), rpad[:, :, 0, :], ALU.subtract).then_inc(sem["norm_step"], 1)
                ve.wait_ge(sem["norm_step"], START + n * 8 + 5)
                ve.tensor_copy(rpad[:, :, 1, :], r(1)).then_inc(sem["norm_step"], 1)
                ve.wait_ge(sem["norm_step"], START + n * 8 + 6)
                ve.tensor_tensor(r(2), r(1), rpad[:, :, 1, :], ALU.subtract).then_inc(sem["norm_step"], 1)
                ve.wait_ge(sem["norm_step"], START + n * 8 + 7)
                ve.tensor_copy(rpad[:, :, 2, :], r(2)).then_inc(sem["split_ready"], 1)
                ve.wait_ge(sem["rt_done"], START + n + 1)
                ve.tensor_copy(rt[:, :], st_ps[0:96, 0, 0:256].bitcast(BF16)).then_inc(sem["rt_ready"], 1)
                ve.wait_ge(sem["rt_ready"], START + n + 1)
                ve.tensor_copy(nrm[:, 2, 0:1], nrm[:, 2, 1:2]).then_inc(sem["norm_step"], 1)
                for i in range(16):
                    a, c = divmod(i, NB)
                    ve.wait_ge(sem["spread_done"], START + n * 16 + i + 1)
                    ve.wait_ge(sem["summed"], START + n * 16 + i + 1)
                    ve.tensor_tensor(qk[a][:, c, :], qk[a][:, c, :], s_ps[:, i % 4, :], ALU.mult).then_inc(sem["qk_ready"], 1)
                core.maxima(ve, n, 0)
                for u in range(16):
                    core.keep_max(ve, n, u)
                    if u < 15:
                        core.maxima(ve, n, u + 1)
                    core.normalise(ve, n, u)
                for i in range(NB):
                    ve.wait_ge(sem["ot_done"], START + n * NB + i + 1)
                    ve.tensor_copy(ot[:, i % 2, :], s_ps[:, i % 4, :]).then_inc(sem["ot_ready"], 1)
                ve.wait_ge(sem["y_done"], START + n + 1)
                ve.tensor_tensor(y[:, at_group(g)], y[:, at_group(g)], st_ps[:, 0, :], ALU.add).then_inc(sem["y_added"], 1)

            def mlp(n, g):
                ve.wait_ge(sem["mean_done"], START + n + 1)
                ve.tensor_tensor(xc[:, :], xs[:, :], s_ps[:, 0, :], ALU.subtract).then_inc(sem["centred"], 1)
                ve.wait_ge(sem["rstd_ready"], START + n + 1)
                ve.tensor_tensor(xc[:, :], xc[:, :], rstd[:, :], ALU.mult).then_inc(sem["xg_step"], 1)
                banks = [st_ps[:, 0, :], st_ps[:, 1, :], o_ps[:, 0, :]]
                for i, (a, b) in enumerate(FB):
                    ve.wait_ge(sem["gl_ready"], START + n * 3 + i + 1)
                    ve.scalar_tensor_tensor(h[0:b - a, i, :], banks[i][0:b - a, :], cols[0:b - a, 2 + i:3 + i], gl[0:b - a, i, :],
                                            ALU.add, ALU.mult).then_inc(sem["h_ready"], 1)
                ve.wait_ge(sem["out_done"], START + n + 1)
                ve.tensor_scalar(y_t[:, :], s_ps[:, 0, :], cols[:, 8:9], None, ALU.add).then_inc(sem["out_step"], 1)
                ve.wait_ge(sem["out_step"], START + n + 1)
                ve.tensor_tensor(y[:, at_group(g)], y[:, at_group(g)], y_t[:, :], ALU.add).then_inc(sem["out_added"], 1)

            with ve.Fori(0, DEPTH) as d:
                ve.wait_ge(sem["attn_w"], START + d * 16 + 16)
                for k in range(4):
                    tt = ve.tensor_scalar(tab[:, k, :], tables[:, k, :], scales[:, k:k + 1], None, ALU.mult)
                    tt.then_inc(sem["tab_ready"], 1)
                with ve.Fori(0, NG) as g:
                    ve.wait_ge(sem["tab_ready"], START + d * 4 + 4)
                    attn(d * NG + g, g)
                with ve.Fori(0, NG) as g:
                    mlp(d * NG + g, g)
            with ve.Fori(0, NG) as g:
                ve.wait_ge(sem["out_added"], START + DEPTH * NG)
                ve.tensor_tensor(x[:, at_group(g)], x[:, at_group(g)], y[:, at_group(g)], ALU.add).then_inc(sem["x_added"], 1)


def store_stage(nc, R, out):
    with Stage(nc, "store") as s:
        (stored,) = s.sems("stored")
        block = s.block()

        @block.sync
        def _(sp):
            sp.dma_start(out, R["x"][:, :]).then_inc(stored, 16)
            sp.wait_ge(stored, START + 16)


CONST_BF = [("ident", 128), ("causal", 128), ("causal_t", 128), ("band", 128), ("band_q1", 160), ("band_k0", 160),
            ("band_t", 128), ("pair_rows", 128), ("upper", 128), ("ones", 128), ("first", 8), ("head_rows", 2048), ("pair_cols", 2)]


def build(nc, IN, out, stages):
    with ExitStack() as ctx:
        sb = lambda n, shape, dt=F32: ctx.enter_context(nc.sbuf_tensor(n, shape, dt))
        R = {"x": sb("x_res", [128, TOK]), "xn": sb("xn_res", [128, TOK]), "ident": sb("ident", [128, 128]),
             "mean_w": sb("mean_w", [128, 128]), "eps": sb("eps", [128, 1]), "comb": sb("comb", [128, NT, 8]),
             "pair_cols": sb("pair_cols", [128, 2]), "c_bf": sb("consts_bf", [128, sum(w for _, w in CONST_BF)], BF16)}
        at, C = 0, {}
        for n, w in CONST_BF:
            C[n] = R["c_bf"][:, at:at + w]
            at += w
        R["masks"] = C
        R["ident_bf"], R["pair_rows"], R["upper_bf"], R["ones_bf"], R["first"] = C["ident"], C["pair_rows"], C["upper"], C["ones"], C["first"]
        R["head_rows"] = C["head_rows"][0:96, :].rearrange("p (i c) -> p i c", i=16)
        R["pair_src"] = C["pair_cols"]
        load_stage(nc, R, IN)
        if "norm0" in stages:
            norm_stage(nc, R, "norm0")
        if "attn0" in stages:
            attn64_stage(nc, R, "attn0", {k: IN[f"a0_{k}"] for k in ("wq", "wk", "wv", "wo")}, 0.125)
        if "ffn0" in stages:
            gate_stage(nc, R, "gate0", {"wg": IN["f0_wg"], "bg": IN["f0_bg"]}, None)
            experts_stage(nc, R, "ffn0", {k: IN[f"f0_{k}"] for k in ("w1", "w2", "b1", "b2")}, False)
        if "norm1" in stages:
            norm_stage(nc, R, "norm1")
        if "attn1" in stages:
            attn8_stage(nc, R, "attn1", {"low": IN["c_low"], "mix_sel": IN["c_mix_sel"], "mix_mask": IN["c_mix_mask"], **{k: IN[f"a1_{k}"] for k in ("wq", "wk", "wv", "vb", "qkb")}}, 1.0)
        if "ffn1" in stages:
            local_stage(nc, R, "ffn1", {"tables": IN["c_tables"], **{k: IN[f"f1_{k}"] for k in ("wa", "wm")}})
        if "norm2" in stages:
            norm_stage(nc, R, "norm2")
        if "attn2" in stages:
            attn8_stage(nc, R, "attn2", {"low": IN["c_low"], "lora": True, **{k: IN[f"a2_{k}"] for k in ("wq", "wk", "wv", "vb", "qkb", "wo", "wob", "lora_a", "lora_b")}},
                        8 ** -0.5, project=True)
        if "ffn2" in stages:
            binary_stage(nc, R, "ffn2", {k: IN[f"f2_{k}"] for k in ("w1", "w1t", "w2", "w2t", "b1", "b2")})
        if "norm3" in stages:
            norm_stage(nc, R, "norm3")
        if "ffn3" in stages:
            gate_stage(nc, R, "gate3", {"wg": IN["f3_wg"]}, int(1.25 * TOK / 8))
            experts_stage(nc, R, "ffn3", {k: IN[f"f3_{k}"] for k in ("w1", "w2")}, True)
        if "attn3" in stages:
            with Stage(nc, "copy3") as s:
                (added,) = s.sems("added")
                block = s.block()

                @block.vector
                def _(ve):
                    with ve.Fori(0, NG) as g:
                        ve.tensor_tensor(R["x"][:, at_group(g)], R["x"][:, at_group(g)], R["xn"][:, at_group(g)], ALU.add).then_inc(added, 1)
            norm_stage(nc, R, "norm3b", again=True)
            attn8_stage(nc, R, "attn3", {"low": IN["c_low"], **{k: IN[f"a3_{k}"] for k in ("wq", "wk", "wv", "vb", "qkb", "wo", "wob", "gamma", "beta", "wqr", "wkr", "qkbr")},
                                         "cos": IN["c_cos"], "sin": IN["c_sin"]},
                        8 ** -0.5, affine=True, rope=True, project=True)
        store_stage(nc, R, out)


def layouts(a):
    f = np.float32
    T = lambda w: np.ascontiguousarray(np.asarray(w).T)
    L = {"x_t": T(np.asarray(a["L0_attn_x"]).reshape(TOK, D))}
    for n in "qkv":
        L[f"a0_w{n}"] = T(np.asarray(a[f"L0_attn_w_{n}"]).reshape(HEADS * DH, D))
    blocks = lambda w, n: np.ascontiguousarray(w.reshape(n, 128, -1).transpose(1, 0, 2))
    L["a0_wo"] = blocks(T(a["L0_attn_w_o"]), NB).reshape(128, 1024)
    L["f0_wg"], L["f0_bg"] = np.asarray(a["L0_ffn_gate_w"]), np.asarray(a["L0_ffn_gate_b"]).reshape(1, 8)
    L["f0_w1"] = np.ascontiguousarray(np.asarray(a["L0_ffn_w1"]).transpose(1, 0, 2))
    L["f0_w2"] = np.ascontiguousarray(np.asarray(a["L0_ffn_w2"]).reshape(8, 4, 128, D).transpose(2, 0, 1, 3))
    L["f0_b1"] = np.ascontiguousarray(np.asarray(a["L0_ffn_b1"]).reshape(8, 4, 128).transpose(2, 0, 1))
    L["f0_b2"] = np.asarray(a["L0_ffn_b2"])

    def spread(w, key):
        o = np.zeros((w.shape[0], 4, 4, 32), w.dtype)
        o[..., 0:24] = np.tile(w.reshape(-1, 4, 4, 8), (1, 1, 1, 3))
        return o.reshape(-1, 4, 128)

    def spread_bias(bq, bk, one=1.0):
        q, k = (np.zeros((4, 4, 32), f) for _ in range(2))
        q[..., 0:24] = np.tile(bq.reshape(4, 4, 8), (1, 1, 3))
        k[..., 0:24] = np.tile(bk.reshape(4, 4, 8), (1, 1, 3))
        k[..., 24:26] = one
        return np.ascontiguousarray(np.concatenate([q, k]).reshape(8, 128).T)

    def heads8(pre, wq, wk, wv, bq, bk, bv):
        L[f"{pre}_wq"], L[f"{pre}_wk"] = spread(wq, "q"), spread(wk, "k")
        L[f"{pre}_wv"], L[f"{pre}_vb"] = np.ascontiguousarray(wv), bv.reshape(1, D)
        L[f"{pre}_qkb"] = spread_bias(bq, bk)

    w, b = np.asarray(a["L1_attn_W_qkv"]), np.asarray(a["L1_attn_b_qkv"])
    heads8("a1", w[:, 0:128], w[:, 128:256], w[:, 256:384], b[0:128], b[128:256], b[256:384])
    heads8("a2", *(T(a[f"L2_attn_W{n}"]) for n in "qkv"), *(np.asarray(a[f"L2_attn_b{n}"]) for n in "qkv"))
    L["a2_wo"], L["a2_wob"] = T(a["L2_attn_Wo"]), np.asarray(a["L2_attn_bo"]).reshape(D, 1)
    L["a2_lora_a"] = np.stack([np.asarray(a[f"L2_attn_A{n}"]) for n in "qkvo"], 1)
    lb = np.zeros((8, 4, 512), f)
    for n, c in enumerate("qkvo"):
        bt = T(a[f"L2_attn_B{c}"])
        if n < 2:
            lb[:, n] = spread(bt, "").reshape(8, 512)
        else:
            lb[:, n, 0:128] = bt
    L["a2_lora_b"] = lb
    w, b = np.asarray(a["L3_attn_W_in"]), np.asarray(a["L3_attn_b_in"])
    heads8("a3", w[:, 0:128], w[:, 128:256], w[:, 256:384], b[0:128], b[128:256], b[256:384])
    swap = np.array([1, 0, 3, 2, 4, 5, 6, 7])
    turn = lambda m: m.reshape(-1, 16, 8)[:, :, swap].reshape(m.shape[0] if m.ndim > 1 else -1, *([128] if m.ndim > 1 else []))
    L["a3_wqr"], L["a3_wkr"] = spread(turn(w[:, 0:128]), "q"), spread(turn(w[:, 128:256]), "k")
    L["a3_qkbr"] = spread_bias(turn(b[0:128]).reshape(-1), turn(b[128:256]).reshape(-1), 0.0)
    L["a3_wo"], L["a3_wob"] = np.asarray(a["L3_attn_W_out"]), np.asarray(a["L3_attn_b_out"]).reshape(D, 1)
    L["a3_gamma"], L["a3_beta"] = (np.asarray(a[f"L3_attn_{n}"]).reshape(D, 1) for n in ("gamma", "beta"))

    wq = np.asarray(a["L1_ffn_Wqkv"])
    wa = [wq[:, :, 0:2048], wq[:, :, 0:2048].reshape(DEPTH, D, 32, 2, 32)[:, :, :, ::-1].reshape(DEPTH, D, 2048), wq[:, :, 2048:],
          np.asarray(a["L1_ffn_Wo"]).reshape(DEPTH, NB, 128, D).transpose(0, 2, 1, 3).reshape(DEPTH, 128, 1024)]
    w1 = np.zeros((DEPTH, D, 6, 128), f)
    b1 = np.zeros((DEPTH, 128, 6), f)
    w2 = np.zeros((DEPTH, 128, 3, D), f)
    for i, (lo, hi) in enumerate(FB):
        for part in range(2):
            cols = slice(part * FF + lo, part * FF + hi)
            w1[:, :, 3 * part + i, 0:hi - lo] = np.asarray(a["L1_ffn_W1"])[:, :, cols]
            b1[:, 0:hi - lo, 3 * part + i] = np.asarray(a["L1_ffn_b1"])[:, cols]
        w2[:, 0:hi - lo, i] = np.asarray(a["L1_ffn_W2"])[:, lo:hi]
    qs, ks = np.asarray(a["L1_ffn_q_scale"]), np.asarray(a["L1_ffn_k_scale"])
    rot = lambda v: np.concatenate([v[:, 32:], v[:, :32]], 1)
    wa += [np.tile(v, (1, 2))[:, :, None] for v in (qs, rot(qs), ks, rot(ks))]
    wm = [w1.reshape(DEPTH, D, 768), w2.reshape(DEPTH, 128, 384)]
    wm += [np.asarray(a[f"L1_ffn_{n}"])[:, :, None] for n in ("ln_g", "ln_b")] + [b1, np.asarray(a["L1_ffn_b2"])[:, :, None]]
    L["f1_wa"], L["f1_wm"] = (np.ascontiguousarray(np.concatenate(w, 2)).reshape(-1) for w in (wa, wm))

    w1, w2 = np.asarray(a["L2_ffn_w1"]), np.asarray(a["L2_ffn_w2"])
    L["f2_w1"], L["f2_w1t"] = blocks(w1, 4), T(w1)
    L["f2_w2"], L["f2_w2t"] = w2, blocks(T(w2), 4)
    L["f2_b1"] = T(np.asarray(a["L2_ffn_b1"]).reshape(4, 128))
    L["f2_b2"] = np.asarray(a["L2_ffn_b2"]).reshape(D, 1)
    L["f3_wg"] = T(a["L3_ffn_gate_w"])
    gp, up = (np.asarray(a[f"L3_ffn_{n}_proj_w"]).reshape(8, 2, 128, D) for n in ("gate", "up"))
    L["f3_w1"] = np.ascontiguousarray(np.stack([gp, up], 2).transpose(4, 0, 1, 2, 3)).reshape(D, 8, 512)
    L["f3_w2"] = np.ascontiguousarray(np.asarray(a["L3_ffn_down_proj_w"]).reshape(8, D, 2, 128).transpose(3, 0, 2, 1))
    return L


def constants():
    f = np.float32
    i, j = np.arange(128)[:, None], np.arange(128)[None, :]
    m = lambda bad: np.where(bad, NEG, 0.0).astype(f)
    C = {"ident": np.eye(128, dtype=f), "causal": m(j > i), "causal_t": m(i > j)}
    band = lambda q, k: m((k > q) | (k < q - 32))
    j160 = np.arange(160)[None, :]
    C["band"], C["band_t"] = band(i, j), band(j, i)
    C["band_q1"] = band(128 + i, 96 + j160)
    C["band_k0"] = band(j160, i)
    pr = np.zeros((128, 128), f)
    pr[[0, 1, 64, 65]] = 1.0
    C["pair_rows"] = pr
    C["upper"] = (i <= j).astype(f)
    C["ones"] = np.ones((128, 128), f)
    C["first"] = np.broadcast_to(np.arange(8, 0, -1).astype(f), (128, 8))
    hr = np.zeros((128, 16, 128), f)
    for blk in range(16):
        for lev in range(3):
            hr[32 * lev + 2 * blk, blk, 0:64] = 1.0
            hr[32 * lev + 2 * blk + 1, blk, 64:128] = 1.0
    C["head_rows"] = hr.reshape(128, 2048)
    pc = np.zeros((128, 2), f)
    pc[0:64, 0] = pc[64:128, 1] = 1.0
    C["pair_cols"] = pc
    out = {"c_bf": np.concatenate([C[n] for n, _ in CONST_BF], 1), "c_ident": C["ident"]}
    out["c_mix_sel"] = (i // 16 == np.arange(8)[None, :]).astype(f)
    out["c_mix_mask"] = (i % 16 == j // 8).astype(f)
    low = np.zeros((4, 32, 2), f)
    low[:, 8:16, 0] = low[:, 16:24, 1] = -1.0
    out["c_low"] = low.reshape(128, 2)
    t = np.arange(SEQ, dtype=f)
    fr = np.repeat(t[:, None] * (1.0 / 10000.0 ** (np.arange(0, 4, 2, dtype=f) / f(4))).astype(f)[None], 2, -1)
    cos, sin = np.ones((4, 32, SEQ), f), np.zeros((4, 32, SEQ), f)
    for r in range(3):
        cos[:, 8 * r:8 * r + 4] = np.cos(fr).T
        sin[:, 8 * r:8 * r + 4] = np.sin(fr).T * np.array([-1, 1, -1, 1], f)[:, None]
    out["c_cos"], out["c_sin"] = cos.reshape(128, SEQ), sin.reshape(128, SEQ)
    half = np.arange(0, DH, 2, dtype=f)
    fr = t[:, None] * (1.0 / 10000.0 ** (half / f(DH))).astype(f)[None]
    sc = (((half + f(0.4 * DH)) / f(1.4 * DH))[None] ** ((t - SEQ // 2) / f(16))[:, None]).astype(f)
    both = lambda a, sign: np.tile(np.concatenate([a * sign, a], 1), (1, 2)).T
    cos, sin = np.cos(fr).astype(f), np.sin(fr).astype(f)
    inv = (f(1.0) / sc).astype(f)
    out["c_tables"] = np.ascontiguousarray(np.stack([both(cos * sc, 1), both(sin * sc, -1), both(cos * inv, 1), both(sin * inv, -1)], 1)).astype(f)
    return out


STAGES = "norm0 attn0 ffn0 norm1 attn1 ffn1 norm2 attn2 ffn2 norm3 ffn3 attn3".split()


def kernel(**inputs):
    import concourse.bacc as _bacc
    from concourse.bass_utils import run_bass_kernel_spmd as _run

    nc = _bacc.Bacc("TRN2", target_bir_lowering=False, num_devices=1)
    arrays = {n: np.ascontiguousarray(a) for n, a in {**layouts(inputs), **constants()}.items()}
    IN = {n: nc.dram_tensor(n, a.shape, mybir.dt.from_np(a.dtype), kind="ExternalInput").ap() for n, a in arrays.items()}
    out = nc.dram_tensor("out_t", (128, TOK), F32, kind="ExternalOutput").ap()
    build(nc, IN, out, STAGES)
    r = _run(nc, [arrays], core_ids=[0])
    return np.ascontiguousarray(np.asarray(r.results[0]["out_t"]).T).reshape(16, SEQ, D)
```

```python
from contextlib import ExitStack

import numpy as np

import concourse.bass as bass
from concourse import mybir

F32 = mybir.dt.float32
BF16 = mybir.dt.bfloat16
ACT = mybir.ActivationFunctionType
ALU = mybir.AluOpType
X_AXIS = mybir.AxisListType.X
XY_AXIS = mybir.AxisListType.XY

D = 128
SEQ = 256
TOK = 16 * SEQ
GT = 512
NG = TOK // GT
NT = TOK // 128
HEADS = 16
EPS = 1e-5
LN_EXP = "natural_log_exp_and_others"
GELU = "gelu_and_others"
NEG = -1.0e30


START = 1


def at_group(g, width=GT):
    return bass.ds(g * width, width)


class Stage:

    def __init__(self, nc, name):
        self.nc, self.name, self.ctx, self.semaphores = nc, name, ExitStack(), []

    def __enter__(self):
        self.ctx.__enter__()
        return self

    def __exit__(self, *a):
        left = self.ctx.__exit__(*a)
        if a[0] is None:
            self.nc.clear_and_free_semaphores(self.semaphores)
            self.nc.all_engine_barrier()
        return left

    def sb(self, name, shape, dt=F32):
        return self.ctx.enter_context(self.nc.sbuf_tensor(f"{self.name}_{name}", shape, dt))

    def ps(self, name, shape, dt=F32):
        return self.ctx.enter_context(self.nc.psum_tensor(f"{self.name}_{name}_ps", shape, dt))

    def sems(self, names):
        new = [self.nc.alloc_semaphore(f"{self.name}_{n}") for n in names.split()]
        self.semaphores += new
        return new

    def block(self):
        for semaphore in self.semaphores:
            self.nc.gpsimd.sem_inc(semaphore, 1)
        self.nc.all_engine_barrier()
        return self.ctx.enter_context(self.nc.Block())


def load_stage(nc, R, IN):
    with Stage(nc, "load") as s:
        raw = s.sb("raw", [128, IN["c_bf"].shape[1]])
        (loaded, cast) = s.sems("loaded cast")
        block = s.block()

        @block.sync
        def _(sp):
            sp.dma_start(R["x"][:, :], IN["x_t"]).then_inc(loaded, 16)
            sp.dma_start(R["ident"][:, :], IN["c_ident"]).then_inc(loaded, 16)
            sp.dma_start(raw[:, :], IN["c_bf"]).then_inc(loaded, 16)
            sp.wait_ge(loaded, START + 48)

        @block.vector
        def _(ve):
            ve.memset(R["mean_w"][:, :], 1.0 / D).then_inc(cast, 1)
            ve.memset(R["eps"][:, :], EPS).then_inc(cast, 1)
            ve.wait_ge(loaded, START + 48)
            ve.tensor_copy(R["c_bf"][:, :], raw[:, :]).then_inc(cast, 1)
            ve.tensor_copy(R["head_ones"][:, :], raw[:, raw.shape[1] - 128:]).then_inc(cast, 1)
            ve.wait_ge(cast, START + 4)


def norm_stage(nc, R, name, again=False):
    with Stage(nc, name) as s:
        xc, sq, lnv, rstd = (s.sb(n, [128, GT]) for n in ("xc", "sq", "lnv", "rstd"))
        mean_ps, var_ps = s.ps("mean", [128, GT]), s.ps("var", [128, GT])
        mean_done, centred, squared, var_done, ln_done, rstd_done, normed = s.sems(
            "mean_done centred squared var_done ln_done rstd_done normed")
        block = s.block()
        x, xn = (R["xn"], R["xn"]) if again else (R["x"], R["xn"])

        @block.tensor
        def _(pe):
            with pe.Fori(0, NG) as g:
                pe.wait_ge(centred, START + g)
                pe.matmul(mean_ps[:, :], R["mean_w"][:, :], x[:, at_group(g)], start=True, stop=True).then_inc(mean_done, 1)
                pe.wait_ge(squared, START + g + 1)
                pe.matmul(var_ps[:, :], R["mean_w"][:, :], sq[:, :], start=True, stop=True).then_inc(var_done, 1)

        @block.scalar
        def _(act):
            act.preload_act_table_set(LN_EXP)
            with act.Fori(0, NG) as g:
                act.wait_ge(centred, START + g + 1)
                act.activation(sq[:, :], xc[:, :], ACT.Square).then_inc(squared, 1)
                act.wait_ge(var_done, START + g + 1)
                act.activation(lnv[:, :], var_ps[:, :], ACT.Ln, bias=R["eps"][:, :]).then_inc(ln_done, 1)
                act.wait_ge(ln_done, START + g + 1)
                act.wait_ge(normed, START + g)
                act.activation(rstd[:, :], lnv[:, :], ACT.Exp, scale=-0.5).then_inc(rstd_done, 1)

        @block.vector
        def _(ve):
            with ve.Fori(0, NG) as g:
                ve.wait_ge(mean_done, START + g + 1)
                ve.wait_ge(normed, START + g)
                ve.tensor_tensor(xc[:, :], x[:, at_group(g)], mean_ps[:, :], ALU.subtract).then_inc(centred, 1)
                ve.wait_ge(rstd_done, START + g + 1)
                ve.tensor_tensor(xn[:, at_group(g)], xc[:, :], rstd[:, :], ALU.mult).then_inc(normed, 1)


def attn8_stage(nc, R, name, W, scale, affine=False, rope=False, project=False, residual=False):
    R8 = 32
    with Stage(nc, name) as s:
        xs = s.sb("xs", [128, GT])
        wq, wk = s.sb("wq", [128, 4, 128]), s.sb("wk", [128, 4, 128])
        wv, vb = s.sb("wv", [128, D]), s.sb("vb", [128, D])
        qkb, low = s.sb("qkb", [128, 8]), s.sb("low", [128, 2])
        full = s.sb("full", [128, 2, GT])
        high = s.sb("high", [128, 2, GT], BF16)
        qk = s.sb("qk", [128, 8, GT], BF16)
        q2 = s.sb("q2", [128, 2, SEQ], BF16)
        v = s.sb("v", [128, 4, 4, 640])
        head_cols = v[:, :, :, :].rearrange("p t a (j c) -> p t a j c", c=160)
        otr = s.sb("otr", [128, SEQ])
        negmax = s.sb("negmax", [128, 2, 2, 4])
        mpad = s.sb("mpad", [128, 2, 2, 4, 32], BF16)
        e = s.sb("e", [128, 2, 4, 2 * SEQ])
        rden = s.sb("rden", [128, 2, 4])
        on = s.sb("on", [128, 2, 2, D])
        ot = s.sb("ot", [128, GT])
        s_ps = s.ps("s", [128, 4, 512])
        st_ps = s.ps("st", [128, 2, 512])
        o_ps = s.ps("o", [128, 512])
        o_rows, o_toks = o_ps[:, 0:SEQ], o_ps[:, SEQ:512]
        m_ps = s.ps("m", [128, 512])
        (loaded, zeroed, xs_ready, proj_done, full_ready, high_ready, qk_ready, v_done, v_ready, s_done, max_ready,
         mhi_ready, mpad_ready, mt_done, q2_ready, st_done, e_ready, pv_done, rden_ready, on_ready, ot_done,
         ot_ready, y_done, x_added, aux, tmp_ready, otr_ready, toks_done) = s.sems(
            "loaded zeroed xs_ready proj_done full_ready high_ready qk_ready v_done v_ready s_done max_ready "
            "mhi_ready mpad_ready mt_done q2_ready st_done e_ready pv_done rden_ready on_ready ot_done "
            "ot_ready y_done x_added aux tmp_ready otr_ready toks_done")
        n_load = 6
        if project:
            wo, wob = s.sb("wo", [128, D]), s.sb("wob", [128, 1])
            yt = s.sb("yt", [128, GT])
            n_load += 2
        if W.get("lora"):
            lora_a, lora_b = s.sb("lora_a", [8, 4, 128]), s.sb("lora_b", [8, 4, 512])
            n_load += 2
        if affine:
            gamma, beta = s.sb("gamma", [128, 1]), s.sb("beta", [128, 1])
            n_load += 2
        if rope:
            cos, sin = s.sb("cos", [128, SEQ]), s.sb("sin", [128, SEQ])
            wqr, wkr = s.sb("wqr", [128, 4, 128]), s.sb("wkr", [128, 4, 128])
            qkbr = s.sb("qkbr", [128, 8])
            t1 = s.sb("t1", [128, 2, GT])
            t2 = s.sb("t2", [128, 2, GT])
            n_load += 5
            (rot_done, t_ready, sum_ready) = s.sems("rot_done t_ready sum_ready")
        if not project:
            mix, mix_sel, mix_mask = s.sb("mix", [128, 2, HEADS, 128]), s.sb("mix_sel", [128, 8]), s.sb("mix_mask", [128, 128])
            (mix_ready, mix_ready1) = s.sems("mix_ready mix_ready1")
            n_load += 2
        block = s.block()
        ident = R["ident"]
        identb = R["ident_bf"]
        x, xn = R["x"], R["xn"]
        mt_ps = m_ps[:, :].bitcast(BF16)
        nw = 1 if W.get("lora") else 0
        turn_out_at = 6 if project else 7

        def mixed(b, t):
            return (mix[:, t, :, :].rearrange("p h (s d) -> p h s d", d=8),
                    on[:, b, t, :].rearrange("p (h d) -> p h d", h=HEADS).unsqueeze(2).to_broadcast([128, HEADS, 16, 8]),
                    mix_mask[:, :].rearrange("p (s d) -> p s d", d=8).unsqueeze(1).to_broadcast([128, HEADS, 16, 8]))

        @block.sync
        def _(sp):
            for dst, src in ((wq, W["wq"]), (wk, W["wk"])):
                sp.dma_start(dst[:, :, :], src).then_inc(loaded, 16)
            sp.dma_start(wv[:, :], W["wv"]).then_inc(loaded, 16)
            sp.dma_start(vb[:, :], W["vb"].broadcast_to([128, D])).then_inc(loaded, 16)
            sp.dma_start(qkb[:, :], W["qkb"]).then_inc(loaded, 16)
            sp.dma_start(low[:, :], W["low"]).then_inc(loaded, 16)
            if project:
                sp.dma_start(wo[:, :], W["wo"]).then_inc(loaded, 16)
                sp.dma_start(wob[:, :], W["wob"]).then_inc(loaded, 16)
            if not project:
                sp.dma_start(mix_sel[:, :], W["mix_sel"]).then_inc(loaded, 16)
                sp.dma_start(mix_mask[:, :], W["mix_mask"]).then_inc(loaded, 16)
            if W.get("lora"):
                sp.dma_start(lora_a[:, :, :], W["lora_a"]).then_inc(loaded, 16)
                sp.dma_start(lora_b[:, :, :], W["lora_b"]).then_inc(loaded, 16)
            if affine:
                sp.dma_start(gamma[:, :], W["gamma"]).then_inc(loaded, 16)
                sp.dma_start(beta[:, :], W["beta"]).then_inc(loaded, 16)
            if rope:
                sp.dma_start(cos[:, :], W["cos"]).then_inc(loaded, 16)
                sp.dma_start(sin[:, :], W["sin"]).then_inc(loaded, 16)
                sp.dma_start(wqr[:, :, :], W["wqr"]).then_inc(loaded, 16)
                sp.dma_start(wkr[:, :, :], W["wkr"]).then_inc(loaded, 16)
                sp.dma_start(qkbr[:, :], W["qkbr"]).then_inc(loaded, 16)
            sp.wait_ge(loaded, START + 16 * n_load)

        @block.tensor
        def _(pe):
            pe.wait_ge(loaded, START + 16 * n_load)
            pe.wait_ge(zeroed, START + 3)
            if W.get("lora"):
                for n in range(4):
                    width = 512 if n < 2 else 128
                    mm = pe.matmul(s_ps[:, n, 0:width], lora_a[:, n, :], lora_b[:, n, 0:width], start=True, stop=True)
                    mm.then_inc(aux, 1)
                pe.wait_ge(tmp_ready, START + 4)

            def scores(g, u):
                b, a = divmod(u, 4)
                for pair in range(2):
                    if u == 0:
                        if not rope:
                            pe.wait_ge(full_ready, START + g * 8 + 8)
                        pe.wait_ge(qk_ready, START + g * 8 + 8)
                    else:
                        pe.wait_ge(max_ready, START + g * 16 + 2 * (u - 1) + pair + 1)
                    for j in (2 * pair, 2 * pair + 1):
                        p = slice(R8 * j, R8 * j + R8)
                        for t in range(2):
                            at = b * SEQ + t * 128
                            mm = pe.matmul(s_ps[:, j, t * SEQ:(t + 1) * SEQ], qk[p, a, at:at + 128],
                                           qk[p, 4 + a, b * SEQ:(b + 1) * SEQ], start=True, stop=True)
                    mm.then_inc(s_done, 1)

            def values(g, u, j):
                b, a = divmod(u, 4)
                pe.wait_ge(e_ready, START + g * 32 + 4 * u + j + 1)
                if j == 0:
                    pe.wait_ge(on_ready, START + g * 8 + u)
                for k in range(2):
                    mm = pe.matmul(o_rows, v[:, 2 * b + k, a, 128 * j:128 * j + 128], e[:, u % 2, j, k * SEQ:(k + 1) * SEQ],
                                   start=(j == 0 and k == 0), stop=(j == 3 and k == 1))
                mm.then_inc(pv_done, 1)

            def turn_values(g, u):
                pe.wait_ge(otr_ready, START + g * 8 + u + 1)
                for t in range(2):
                    mm = pe.transpose(o_toks[:, t * 128:(t + 1) * 128], otr[:, t * 128:(t + 1) * 128], ident[:, :])
                mm.then_inc(toks_done, 1)

            def turn_max(g, u):
                pe.wait_ge(mpad_ready, START + g * 8 + u + 1)
                if u == 0:
                    pe.wait_ge(v_ready, START + g + 1)
                else:
                    pe.wait_ge(q2_ready, START + g * 8 + u)
                if u == turn_out_at + 1:
                    pe.wait_ge(x_added if not project else ot_ready, START + g * 2 + 1)
                for t in range(2):
                    mm = pe.transpose(mt_ps[:, t * 128:(t + 1) * 128],
                                      mpad[:, u % 2, t, :, :].rearrange("p j r -> p (j r)"), identb)
                mm.then_inc(mt_done, 1)

            def turned_scores(g, u, j):
                b, a = divmod(u, 4)
                pe.wait_ge(q2_ready, START + g * 8 + u + 1)
                p = slice(R8 * j, R8 * j + R8)
                n = 4 * u + j
                pe.wait_ge(e_ready, START + (g * 32 + n - 1 if n >= 2 else g * 32))
                for k in range(2):
                    at = b * SEQ + k * 128
                    mm = pe.matmul(st_ps[:, j % 2, k * SEQ:(k + 1) * SEQ], qk[p, 4 + a, at:at + 128],
                                   q2[p, u % 2, :], start=True, stop=True)
                mm.then_inc(st_done, 1)

            def turn_out(g, b):
                pe.wait_ge(q2_ready, START + g * 8 + (turn_out_at + 1 if b == 0 else 8))
                if b == 1:
                    pe.wait_ge(x_added if not project else ot_ready, START + g * 2 + 1)
                if project:
                    pe.wait_ge(on_ready, START + g * 8 + 4 * b + 4)
                    for t in range(2):
                        mm = pe.transpose(m_ps[:, 256 + t * 128:384 + t * 128], on[:, b, t, :], ident[:, :])
                    mm.then_inc(ot_done, 1)
                else:
                    for t in range(2):
                        if b == 1 and t == 1:
                            pe.wait_ge(mix_ready1, START + g + 1)
                        else:
                            pe.wait_ge(mix_ready, START + g * 3 + 2 * b + t + 1)
                        for h in range(HEADS):
                            at = 256 + h * 16 + t * 8
                            mm = pe.matmul(m_ps[:, at:at + 8], mix[:, t, h, :], mix_sel[:, :], start=True, stop=True)
                    mm.then_inc(ot_done, 1)

            with pe.Fori(0, NG) as g:
                pe.wait_ge(xs_ready, START + g + 1)
                pe.wait_ge(max_ready, START + g * 16)
                for i in range(8):
                    a = i % 4
                    w = (wq if i < 4 else wk)
                    bank = i % 4 if not rope else 2 * (i % 2)
                    back = 4 if not rope else 2
                    if i >= back and rope:
                        pe.wait_ge(t_ready, START + g * 16 + 2 * (i - back) + 2)
                    elif i >= back:
                        pe.wait_ge(high_ready, START + g * 8 + i - back + 1)
                    pe.matmul(s_ps[:, bank, :], w[:, a, :], xs[:, :], start=True, stop=True).then_inc(proj_done, 1)
                    if rope:
                        wr = (wqr if i < 4 else wkr)
                        pe.matmul(s_ps[:, bank + 1, :], wr[:, a, :], xs[:, :], start=True, stop=True).then_inc(rot_done, 1)
                pe.wait_ge(x_added if not project else ot_ready, START + g * 2)
                for t in range(4):
                    mm = pe.matmul(m_ps[:, t * D:(t + 1) * D], xs[:, t * 128:(t + 1) * 128], wv[:, :], start=True, stop=True)
                mm.then_inc(v_done, 1)
                scores(g, 0)
                turn_max(g, 0)
                for u in range(9):
                    if u < 7:
                        scores(g, u + 1)
                    if u > 1:
                        turn_values(g, u - 2)
                    if u == turn_out_at:
                        turn_out(g, 0)
                    for j in range(4):
                        if u < 8:
                            turned_scores(g, u, j)
                        if u > 0:
                            values(g, u - 1, j)
                    if u < 7:
                        turn_max(g, u + 1)
                turn_values(g, 7)
                turn_out(g, 1)
                if project:
                    pe.wait_ge(ot_ready, START + g * 2 + 2)
                    pe.matmul(st_ps[:, 0, :], wo[:, :], ot[:, :], start=True, stop=True).then_inc(y_done, 1)

        @block.scalar
        def _(act):
            act.preload_act_table_set(LN_EXP)
            act.wait_ge(loaded, START + 16 * n_load)

            def exps(g, u):
                for j in range(4):
                    act.wait_ge(st_done, START + g * 32 + 4 * u + j + 1)
                    act.wait_ge(pv_done, START + (g * 32 + 4 * (u - 2) + j + 1 if u >= 2 else g * 32))
                    act.activation(e[:, u % 2, j, :], st_ps[:, j % 2, :], ACT.Exp, scale=scale).then_inc(e_ready, 1)

            with act.Fori(0, NG) as g:
                act.wait_ge(v_done, START + g)
                if affine:
                    act.activation(xs[:, :], xn[:, at_group(g)], ACT.Identity, bias=beta[:, :], scale=gamma[:, :]).then_inc(xs_ready, 1)
                else:
                    act.activation(xs[:, :], xn[:, at_group(g)], ACT.Copy).then_inc(xs_ready, 1)
                for i in range(8):
                    if i >= 2:
                        act.wait_ge(qk_ready, START + g * 8 + i - 1)
                    if rope:
                        act.wait_ge(sum_ready, START + g * 8 + i + 1)
                        act.activation(high[:, i % 2, :], t1[:, i % 2, :], ACT.Copy).then_inc(high_ready, 1)
                    else:
                        act.wait_ge(proj_done, START + g * 8 + i + 1)
                        act.activation(full[:, i % 2, :], s_ps[:, i % 4, :], ACT.Identity, bias=qkb[:, i:i + 1]).then_inc(full_ready, 1)
                        act.activation(high[:, i % 2, :], s_ps[:, i % 4, :], ACT.Identity, bias=qkb[:, i:i + 1]).then_inc(high_ready, 1)
                for u in range(9):
                    if u < 8:
                        exps(g, u)
                    if u > 0:
                        act.wait_ge(pv_done, START + g * 32 + 4 * u)
                        act.activation(otr[:, :], o_rows, ACT.Copy).then_inc(otr_ready, 1)

        @block.gpsimd
        def _(pool):
            pool.memset(mpad[:, :, :, :, :], 0.0).then_inc(zeroed, 1)
            pool.memset(v[:, :, :, :], 0.0).then_inc(zeroed, 1)
            pool.wait_ge(zeroed, START + 2)
            for t in range(4):
                ones = pool.memset(head_cols[:, t, :, :, 8:16], 1.0)
            ones.then_inc(zeroed, 1)
            if not rope and project:
                return
            with pool.Fori(0, NG) as g:
                if rope:
                    for i in range(8):
                        pool.wait_ge(t_ready, START + g * 16 + 2 * i + 2)
                        pool.tensor_tensor(t1[:, i % 2, :], t1[:, i % 2, :], t2[:, i % 2, :], ALU.add).then_inc(sum_ready, 1)
                if not project:
                    for b in range(2):
                        pool.wait_ge(on_ready, START + g * 8 + 4 * b + 4)
                        pool.wait_ge(ot_done, START + g * 2 + b)
                        for t in range(2 - b):
                            pool.tensor_tensor(*mixed(b, t), ALU.mult).then_inc(mix_ready, 1)

        @block.vector
        def _(ve):
            ve.wait_ge(loaded, START + 16 * n_load)
            ve.wait_ge(zeroed, START + 3)
            if W.get("lora"):
                for n, w in enumerate((wq, wk, wv, wo)):
                    view = w[:, :, :].rearrange("p a c -> p (a c)") if n < 2 else w[:, :]
                    ve.wait_ge(aux, START + n + 1)
                    ve.scalar_tensor_tensor(view, s_ps[:, n, 0:512 if n < 2 else 128], 2.0, view, ALU.mult, ALU.add).then_inc(tmp_ready, 1)
            two = lambda ap: ap.rearrange("p (b t) -> p b t", b=2)

            def maxima(g, u):
                b, a = divmod(u, 4)
                for pair in range(2):
                    ve.wait_ge(s_done, START + g * 16 + 2 * u + pair + 1)
                    src = s_ps[:, 2 * pair:2 * pair + 2, :].rearrange("p j (t k) -> p j t k", t=2)
                    dst = negmax[:, u % 2, :, 2 * pair:2 * pair + 2].rearrange("p t j -> p j t")
                    ve.tensor_reduce(dst, src, X_AXIS, ALU.max, negate=True).then_inc(max_ready, 1)
                ve.wait_ge(max_ready, START + g * 16 + 2 * u + 2)
                if u >= 2:
                    ve.wait_ge(mt_done, START + g * 8 + u - 1)
                ve.tensor_copy(mpad[:, u % 2, :, :, 24], negmax[:, u % 2, :, :]).then_inc(mhi_ready, 1)
                ve.wait_ge(mhi_ready, START + g * 8 + u + 1)
                ve.tensor_tensor(mpad[:, u % 2, :, :, 25], negmax[:, u % 2, :, :], mpad[:, u % 2, :, :, 24], ALU.subtract).then_inc(mpad_ready, 1)

            def split(g, i):
                ve.wait_ge(high_ready, START + g * 8 + i + 1)
                ve.scalar_tensor_tensor(qk[:, i, :], high[:, i % 2, :], low[:, i // 4:i // 4 + 1], (t1 if rope else full)[:, i % 2, :],
                                        ALU.mult, ALU.add).then_inc(qk_ready, 1)

            def normalise(g, u):
                b, a = divmod(u, 4)
                ve.wait_ge(toks_done, START + g * 8 + u + 1)
                toks = o_toks.rearrange("p (t j c) -> p t j c", t=2, j=4)
                ve.reciprocal(rden[:, :, :], toks[:, :, :, 8]).then_inc(rden_ready, 1)
                ve.wait_ge(rden_ready, START + g * 8 + u + 1)
                for t in range(2):
                    nn = ve.tensor_tensor(on[:, b, t, a * 32:(a + 1) * 32].rearrange("p (j d) -> p j d", j=4), toks[:, t, :, 0:8],
                                          rden[:, t, :].unsqueeze(2).to_broadcast([128, 4, 8]), ALU.mult)
                nn.then_inc(on_ready, 1)

            def keep_out(g, b):
                ve.wait_ge(ot_done, START + g * 2 + b + 1)
                if project:
                    ve.tensor_copy(ot[:, b * SEQ:(b + 1) * SEQ], m_ps[:, 256:512]).then_inc(ot_ready, 1)
                else:
                    xa = x[:, bass.ds(g * GT + b * SEQ, SEQ)]
                    ve.tensor_tensor(xa, xa, m_ps[:, 256:512], ALU.add).then_inc(x_added, 1)

            with ve.Fori(0, NG) as g:
                for i in range(8):
                    if rope:
                        if i >= 2:
                            ve.wait_ge(qk_ready, START + g * 8 + i - 1)
                        tab = lambda t: t[:, :].unsqueeze(1).to_broadcast([128, 2, SEQ])
                        bank = 2 * (i % 2)
                        ve.wait_ge(proj_done, START + g * 8 + i + 1)
                        ve.scalar_tensor_tensor(two(t1[:, i % 2, :]), two(s_ps[:, bank, :]), qkb[:, i:i + 1], tab(cos), ALU.add, ALU.mult).then_inc(t_ready, 1)
                        ve.wait_ge(rot_done, START + g * 8 + i + 1)
                        ve.scalar_tensor_tensor(two(t2[:, i % 2, :]), two(s_ps[:, bank + 1, :]), qkbr[:, i:i + 1], tab(sin), ALU.add, ALU.mult).then_inc(t_ready, 1)
                        if i >= 1:
                            split(g, i - 1)
                    else:
                        split(g, i)
                if rope:
                    split(g, 7)
                ve.wait_ge(v_done, START + g + 1)
                vbb = vb[:, :].rearrange("p (a j d) -> p a j d", a=4, j=4)
                for t in range(4):
                    vv = ve.tensor_tensor(head_cols[:, t, :, :, 0:8], m_ps[:, t * D:(t + 1) * D].rearrange("p (a j d) -> p a j d", a=4, j=4), vbb, ALU.add)
                vv.then_inc(v_ready, 1)
                maxima(g, 0)
                for u in range(9):
                    if u < 8:
                        ve.wait_ge(mt_done, START + g * 8 + u + 1)
                        if u >= 2:
                            ve.wait_ge(st_done, START + g * 32 + 4 * u - 4)
                        a = u % 4
                        ve.tensor_tensor(q2[:, u % 2, :], qk[:, a, (u // 4) * SEQ:(u // 4 + 1) * SEQ], mt_ps[:, 0:SEQ], ALU.add).then_inc(q2_ready, 1)
                    if u > 1:
                        normalise(g, u - 2)
                    if u < 7:
                        maxima(g, u + 1)
                    if u == turn_out_at:
                        keep_out(g, 0)
                normalise(g, 7)
                if not project:
                    ve.wait_ge(on_ready, START + g * 8 + 8)
                    ve.tensor_tensor(*mixed(1, 1), ALU.mult).then_inc(mix_ready1, 1)
                keep_out(g, 1)
                if project:
                    ve.wait_ge(y_done, START + g + 1)
                    ve.tensor_scalar(yt[:, :], st_ps[:, 0, :], wob[:, 0:1], None, ALU.add).then_inc(aux, 1)
                    ve.wait_ge(aux, START + g + 1 + 4 * nw)
                    ve.tensor_tensor(x[:, at_group(g)], x[:, at_group(g)], yt[:, :], ALU.add).then_inc(x_added, 1)
                    if residual:
                        ve.wait_ge(x_added, START + g * 2 + 1)
                        ve.tensor_tensor(x[:, at_group(g)], x[:, at_group(g)], xn[:, at_group(g)], ALU.add).then_inc(x_added, 1)


DH = 64
NB = HEADS * DH // 128


class Geometry:

    def __init__(self, R, band):
        m = R["masks"]
        if band:
            self.first_key, self.q1_from = 96, 0
            self.mask_q0, self.mask_q1 = m["band"], m["band_q1"]
        else:
            self.first_key, self.q1_from = 0, 128
            self.mask_q0 = self.mask_q1 = m["causal"]
        self.n_q1 = 256 - self.first_key


def attn64_core(nc, R, T, geo, sem):
    qt, kt, v, on, negmax, e, et, rden = (T[n] for n in ("qt", "kt", "v", "on", "negmax", "e", "et", "rden"))
    s_ps, et_ps, o_ps = T["s_ps"], T["st_ps"], T["o_ps"]
    ident_bf, ident = R["ident_bf"], R["ident"]
    NU = 16

    class Core:
        @staticmethod
        def scores(pe, n, u):
            i, b = divmod(u, 2)
            slot = u % 2
            if u >= 2:
                pe.wait_ge(sem["e_ready"], START + n * NU + u - 1)
            for p in range(2):
                bank = 2 * slot + p
                pe.matmul(s_ps[:, bank, 0:128], qt[:, i, b * SEQ:b * SEQ + 128],
                          kt[:, i, p, b * SEQ:b * SEQ + 128], start=True, stop=False)
                pe.matmul(s_ps[:, bank, 0:128], ident_bf, geo.mask_q0, start=False, stop=True)
                lo, hi = 128, 128 + geo.n_q1
                pe.matmul(s_ps[:, bank, lo:hi], qt[:, i, b * SEQ + 128:b * SEQ + SEQ],
                          kt[:, i, p, b * SEQ + geo.first_key:(b + 1) * SEQ], start=True, stop=False)
                mm = pe.matmul(s_ps[:, bank, lo + geo.q1_from:hi], ident_bf, geo.mask_q1, start=False, stop=True)
            mm.then_inc(sem["s_done"], 1)

        @staticmethod
        def turn_probs(pe, n, u):
            pe.wait_ge(sem["e_ready"], START + n * NU + u + 1)
            for p in range(2):
                if u >= 1:
                    pe.wait_ge(sem["et_ready0" if p == 0 else "et_ready1"], START + n * NU + u)
                for k in range(3):
                    mm = pe.transpose(et_ps[:, p, k * 128:(k + 1) * 128], e[:, u % 2, p, k * 128:(k + 1) * 128], ident[:, :])
            mm.then_inc(sem["et_done"], 1)

        @staticmethod
        def values(pe, n, u):
            i, b = divmod(u, 2)
            if u >= 2:
                pe.wait_ge(sem["o_read"], START + n * NU + u - 1)
            for p in range(2):
                pe.wait_ge(sem["et_ready0" if p == 0 else "et_ready1"], START + n * NU + u + 1)
                h = 2 * i + p
                out = lambda t: o_ps[:, u % 2, (2 * t + p) * 65:(2 * t + p + 1) * 65]
                w = lambda k: et[:, u % 2, p, k * 128:(k + 1) * 128]
                pe.matmul(out(0), w(0), v[:, 2 * b, h, :], start=True, stop=True)
                pe.matmul(out(1), w(1), v[:, 2 * b, h, :], start=True, stop=False)
                mm = pe.matmul(out(1), w(2), v[:, 2 * b + 1, h, :], start=False, stop=True)
            mm.then_inc(sem["pv_done"], 1)

        @staticmethod
        def exps(act, n, u):
            slot = u % 2
            act.wait_ge(sem["max_ready"], START + n * NU + u + 1)
            if u >= 2:
                act.wait_ge(sem["et_done"], START + n * NU + u - 1)
            for p in range(2):
                bank = 2 * slot + p
                act.activation(e[:, slot, p, 0:128], s_ps[:, bank, 0:128], ACT.Exp, bias=negmax[:, slot, 0, p:p + 1])
                last = act.activation(e[:, slot, p, 128 + geo.first_key:384], s_ps[:, bank, 128:128 + geo.n_q1], ACT.Exp,
                                      bias=negmax[:, slot, 1, p:p + 1])
            last.then_inc(sem["e_ready"], 1)

        @staticmethod
        def keep_probs0(act, n, u):
            act.wait_ge(sem["et_done"], START + n * NU + u + 1)
            if u >= 2:
                act.wait_ge(sem["pv_done"], START + n * NU + u - 1)
            act.activation(et[:, u % 2, 0, :], et_ps[:, 0, 0:384], ACT.Copy).then_inc(sem["et_ready0"], 1)

        @staticmethod
        def keep_probs1(ve, n, u):
            ve.wait_ge(sem["et_done"], START + n * NU + u + 1)
            if u >= 2:
                ve.wait_ge(sem["pv_done"], START + n * NU + u - 1)
            ve.tensor_copy(et[:, u % 2, 1, :], et_ps[:, 1, 0:384]).then_inc(sem["et_ready1"], 1)

        @staticmethod
        def maxima(ve, n, u):
            slot = u % 2
            ve.wait_ge(sem["s_done"], START + n * NU + u + 1)
            banks = s_ps[:, 2 * slot:2 * slot + 2, :]
            ve.tensor_reduce(negmax[:, slot, 0, :], banks[:, :, 0:128], X_AXIS, ALU.max, negate=True)
            ve.tensor_reduce(negmax[:, slot, 1, :], banks[:, :, 128:128 + geo.n_q1], X_AXIS, ALU.max, negate=True).then_inc(sem["max_ready"], 1)

        @staticmethod
        def normalise(ve, n, u):
            i, b = divmod(u, 2)
            ve.wait_ge(sem["pv_done"], START + n * NU + u + 1)
            o = o_ps[:, u % 2, 0:260].rearrange("q (t d) -> q t d", t=4)
            ve.reciprocal(rden[:, u % 2, :], o[:, :, 64]).then_inc(sem["rden_ready"], 1)
            ve.wait_ge(sem["rden_ready"], START + n * NU + u + 1)
            for t in range(2):
                dst = on[:, 2 * b + t, i * 128:(i + 1) * 128].rearrange("q (h d) -> q h d", h=2)
                nn = ve.tensor_tensor(dst, o[:, 2 * t:2 * t + 2, 0:64],
                                      rden[:, u % 2, 2 * t:2 * t + 2].unsqueeze(2).to_broadcast([128, 2, 64]), ALU.mult)
            nn.then_inc(sem["o_read"], 1)

        @staticmethod
        def turn_out(pe, n, i):
            if i == 0:
                pe.wait_ge(sem["e_ready"], START + n * NU + NU)
                pe.wait_ge(sem["o_read"], START + n * NU + NU)
            if i >= 4:
                pe.wait_ge(sem["ot_ready"], START + n * NB + i - 3)
            for t in range(4):
                mm = pe.transpose(s_ps[:, i % 4, t * 128:(t + 1) * 128], on[:, t, i * 128:(i + 1) * 128], ident[:, :])
            mm.then_inc(sem["ot_done"], 1)

    return Core


CORE_SEMS = "max_ready s_done e_ready et_done et_ready0 et_ready1 pv_done o_read rden_ready ot_done ot_ready".split()


def named(s, names):
    return dict(zip(names, s.sems(" ".join(names))))


def attn64_tiles(s):
    return {
        "qt": s.sb("qt", [128, NB, GT]), "kt": s.sb("kt", [128, NB, 2, GT]),
        "v": s.sb("v", [128, 4, HEADS, DH + 1]), "on": s.sb("on", [128, 4, HEADS * DH]),
        "negmax": s.sb("negmax", [128, 2, 2, 2]), "e": s.sb("e", [128, 2, 2, 384]), "et": s.sb("et", [128, 2, 2, 384]),
        "rden": s.sb("rden", [128, 2, 4]), "ot": s.sb("ot", [128, 2, GT]),
        "s_ps": s.ps("s", [128, 4, 512]), "st_ps": s.ps("st", [128, 2, 512]), "o_ps": s.ps("o", [128, 2, 512]),
    }


def attn64_stage(nc, R, name, W, scale):
    with Stage(nc, name) as s:
        T = attn64_tiles(s)
        xs = s.sb("xs", [128, GT])
        wq, wk, wv, wo = (s.sb(n, [128, HEADS * DH]) for n in ("wq", "wk", "wv", "wo"))
        geo = Geometry(R, band=False)
        sem = named(s, CORE_SEMS + ["loaded", "zeroed", "xs_ready", "proj_done", "proj_ready", "v_done", "v_ready", "y_done", "x_added"])
        core = attn64_core(nc, R, T, geo, sem)
        block = s.block()
        x, xn = R["x"], R["xn"]
        qt, kt, v, ot = T["qt"], T["kt"], T["v"], T["ot"]
        s_ps, st_ps = T["s_ps"], T["st_ps"]

        @block.sync
        def _(sp):
            for dst, src in ((wq, "wq"), (wk, "wk"), (wv, "wv"), (wo, "wo")):
                sp.dma_start(dst[:, :], W[src]).then_inc(sem["loaded"], 16)
            sp.wait_ge(sem["loaded"], START + 64)

        @block.tensor
        def _(pe):
            pe.wait_ge(sem["loaded"], START + 64)
            pe.wait_ge(sem["zeroed"], START + 3)
            with pe.Fori(0, NG) as g:
                pe.wait_ge(sem["xs_ready"], START + g + 1)
                pe.wait_ge(sem["ot_ready"], START + g * NB)
                for i in range(16):
                    w, c = (wq, i) if i < NB else (wk, i - NB)
                    if i >= 4:
                        pe.wait_ge(sem["proj_ready"], START + g * 16 + i - 3)
                    pe.matmul(s_ps[:, i % 4, :], w[:, c * 128:(c + 1) * 128], xs[:, :], start=True, stop=True).then_inc(sem["proj_done"], 1)
                for i in range(8):
                    t, half = divmod(i, 2)
                    pe.wait_ge(sem["v_ready"], START + (g * 8 + i - 1 if i >= 2 else g * 8))
                    if i == 0:
                        pe.wait_ge(sem["x_added"], START + g)
                    pe.matmul(st_ps[:, half, :], xs[:, t * 128:(t + 1) * 128], wv[:, half * 512:(half + 1) * 512], start=True, stop=True).then_inc(sem["v_done"], 1)
                pe.wait_ge(sem["proj_ready"], START + g * 16 + 16)
                pe.wait_ge(sem["v_ready"], START + g * 8 + 8)
                core.scores(pe, g, 0)
                core.scores(pe, g, 1)
                for u in range(17):
                    if u < 16:
                        core.turn_probs(pe, g, u)
                    if u < 14:
                        core.scores(pe, g, u + 2)
                    if u > 0:
                        core.values(pe, g, u - 1)
                for i in range(NB):
                    core.turn_out(pe, g, i)
                    if i >= 1:
                        pe.wait_ge(sem["ot_ready"], START + g * NB + i)
                        pe.matmul(st_ps[:, 0, :], wo[:, (i - 1) * 128:i * 128], ot[:, (i - 1) % 2, :], start=(i == 1), stop=False)
                pe.wait_ge(sem["ot_ready"], START + g * NB + NB)
                pe.matmul(st_ps[:, 0, :], wo[:, (NB - 1) * 128:], ot[:, (NB - 1) % 2, :], start=False, stop=True).then_inc(sem["y_done"], 1)

        @block.scalar
        def _(act):
            act.preload_act_table_set(LN_EXP)
            with act.Fori(0, NG) as g:
                act.wait_ge(sem["v_done"], START + g * 8)
                act.activation(xs[:, :], xn[:, at_group(g)], ACT.Copy).then_inc(sem["xs_ready"], 1)
                for i in range(16):
                    act.wait_ge(sem["proj_done"], START + g * 16 + i + 1)
                    if i < NB:
                        act.activation(qt[:, i, :], s_ps[:, i % 4, :], ACT.Copy, scale=scale).then_inc(sem["proj_ready"], 1)
                    else:
                        act.activation(kt[0:64, i - NB, 0, :], s_ps[0:64, i % 4, :], ACT.Copy)
                        act.activation(kt[64:128, i - NB, 1, :], s_ps[64:128, i % 4, :], ACT.Copy).then_inc(sem["proj_ready"], 1)
                core.exps(act, g, 0)
                core.exps(act, g, 1)
                for u in range(16):
                    core.keep_probs0(act, g, u)
                    if u < 14:
                        core.exps(act, g, u + 2)

        @block.gpsimd
        def _(pool):
            pool.memset(T["e"][:, :, :, :], 0.0).then_inc(sem["zeroed"], 1)
            pool.memset(v[:, :, :, :], 1.0).then_inc(sem["zeroed"], 1)
            pool.memset(kt[:, :, :, :], 0.0).then_inc(sem["zeroed"], 1)

        @block.vector
        def _(ve):
            ve.wait_ge(sem["zeroed"], START + 3)
            with ve.Fori(0, NG) as g:
                for i in range(8):
                    t, half = divmod(i, 2)
                    ve.wait_ge(sem["v_done"], START + g * 8 + i + 1)
                    ve.tensor_copy(v[:, t, 8 * half:8 * half + 8, 0:DH], st_ps[:, half, :].rearrange("p (h d) -> p h d", h=8)).then_inc(sem["v_ready"], 1)
                core.maxima(ve, g, 0)
                core.maxima(ve, g, 1)
                for u in range(17):
                    if u < 16:
                        core.keep_probs1(ve, g, u)
                    if u < 14:
                        core.maxima(ve, g, u + 2)
                    if u > 0:
                        core.normalise(ve, g, u - 1)
                for i in range(NB):
                    ve.wait_ge(sem["ot_done"], START + g * NB + i + 1)
                    ve.tensor_copy(ot[:, i % 2, :], s_ps[:, i % 4, :]).then_inc(sem["ot_ready"], 1)
                ve.wait_ge(sem["y_done"], START + g + 1)
                ve.tensor_tensor(x[:, at_group(g)], x[:, at_group(g)], st_ps[:, 0, :], ALU.add).then_inc(sem["x_added"], 1)


def gate_stage(nc, R, name, W, capacity):
    NE = 8
    with Stage(nc, name) as s:
        wg, bias = s.sb("wg", [128, NE]), s.sb("bias", [128, NE])
        p_, sc, t_ = (s.sb(n, [128, NT, NE]) for n in ("p", "sc", "t"))
        oh = [s.sb(f"oh{k}", [128, NT, NE]) for k in range(2)]
        red, w_, sm, rk = (s.sb(n, [128, 2, NT]) for n in ("red", "w", "sm", "rk"))
        first = s.sb("first", [128, NE])
        lg = s.ps("lg", [128, NT * NE])
        loaded, gates_done, dv, exp_ready, cum_done = s.sems("loaded gates_done dv exp_ready cum_done")
        if capacity:
            ohb = s.sb("ohb", [128, NT, 2, NE], BF16)
            cum = [s.sb(f"cum{i}", [128, NT, 2, NE]) for i in range(2)]
            rank = s.sb("rank", [128, NT, 2, NE])
            cum_ps, tot_ps = s.ps("cumps", [128, NT * 2 * NE]), s.ps("totps", [128, NT * 2 * NE])
        block = s.block()
        comb = R["comb"]
        bc = lambda t: t.unsqueeze(2).to_broadcast([128, NT, NE])
        bt = lambda t: t.unsqueeze(1).to_broadcast([128, NT, NE])

        @block.sync
        def _(sp):
            sp.dma_start(wg[:, :], W["wg"]).then_inc(loaded, 16)
            if not capacity:
                sp.dma_start(bias[:, :], W["bg"].broadcast_to([128, NE])).then_inc(loaded, 16)
            sp.wait_ge(loaded, START + (16 if capacity else 32))

        @block.tensor
        def _(pe):
            pe.wait_ge(loaded, START + (16 if capacity else 32))
            for t in range(NT):
                mm = pe.matmul(lg[:, t * NE:(t + 1) * NE], R["xn"][:, t * 128:(t + 1) * 128], wg[:, :], start=True, stop=True)
            mm.then_inc(gates_done, 1)
            if capacity:
                pe.wait_ge(cum_done, START + 1)
                flat = ohb[:, :, :, :].rearrange("p t k e -> p (t k e)")
                pe.matmul(cum_ps[:, :], R["upper_bf"], flat, start=True, stop=True)
                pe.matmul(tot_ps[:, :], R["ones_bf"], flat, start=True, stop=True).then_inc(cum_done, 1)

        @block.scalar
        def _(act):
            act.preload_act_table_set(LN_EXP)
            act.wait_ge(dv, START + 4)
            act.activation(p_[:, :, :], sc[:, :, :], ACT.Exp).then_inc(exp_ready, 1)

        @block.gpsimd
        def _(pool):
            pass

        @block.vector
        def _(ve):
            step = [0]

            def done(ins):
                step[0] += 1
                ins.then_inc(dv, 1)
                ve.wait_ge(dv, START + step[0])

            logits = lg[:, :].rearrange("p (t e) -> p t e", e=NE)
            done(ve.tensor_copy(first[:, :], R["first"]))
            ve.wait_ge(gates_done, START + 1)
            if not capacity:
                ve.wait_ge(loaded, START + 32)
                done(ve.tensor_tensor(t_[:, :, :], logits, bt(bias[:, :]), ALU.add))
            else:
                done(ve.tensor_copy(t_[:, :, :], logits))
            done(ve.tensor_reduce(red[:, 0, :], t_[:, :, :], X_AXIS, ALU.max))
            done(ve.tensor_tensor(sc[:, :, :], t_[:, :, :], bc(red[:, 0, :]), ALU.subtract))
            ve.wait_ge(exp_ready, START + 1)
            done(ve.tensor_reduce(red[:, 0, :], p_[:, :, :], X_AXIS, ALU.add))
            done(ve.reciprocal(red[:, 1, :], red[:, 0, :]))
            done(ve.tensor_tensor(p_[:, :, :], p_[:, :, :], bc(red[:, 1, :]), ALU.mult))
            done(ve.tensor_copy(sc[:, :, :], p_[:, :, :]))
            for k in range(2):
                done(ve.tensor_reduce(w_[:, k, :], sc[:, :, :], X_AXIS, ALU.max))
                done(ve.tensor_tensor(t_[:, :, :], sc[:, :, :], bc(w_[:, k, :]), ALU.is_equal))
                done(ve.tensor_tensor(t_[:, :, :], t_[:, :, :], bt(first[:, :]), ALU.mult))
                done(ve.tensor_reduce(red[:, 0, :], t_[:, :, :], X_AXIS, ALU.max))
                done(ve.tensor_tensor(oh[k][:, :, :], bt(first[:, :]), bc(red[:, 0, :]), ALU.is_equal))
                if k == 0:
                    done(ve.scalar_tensor_tensor(sc[:, :, :], oh[0][:, :, :], -2.0, sc[:, :, :], ALU.mult, ALU.add))
            if capacity:
                done(ve.tensor_tensor(sm[:, 0, :], w_[:, 0, :], w_[:, 1, :], ALU.add))
                done(ve.tensor_scalar(sm[:, 0, :], sm[:, 0, :], 1e-9, None, ALU.add))
                done(ve.reciprocal(sm[:, 1, :], sm[:, 0, :]))
                for k in range(2):
                    done(ve.tensor_tensor(w_[:, k, :], w_[:, k, :], sm[:, 1, :], ALU.mult))
                    done(ve.tensor_copy(ohb[:, :, k, :], oh[k][:, :, :]))
                ve.tensor_copy(sm[:, 0, :], w_[:, 0, :]).then_inc(cum_done, 1)
                ve.wait_ge(cum_done, START + 2)
                v4 = lambda ps: ps[:, :].rearrange("p (t k e) -> p t k e", k=2, e=NE)
                done(ve.memset(cum[0][:, 0:1, :, :], 0.0))
                done(ve.tensor_copy(cum[0][:, 1:NT, :, :], v4(tot_ps)[:, 0:NT - 1]))
                at, d = 0, 1
                while d < NT:
                    a, b = cum[at], cum[1 - at]
                    done(ve.tensor_copy(b[:, 0:d, :, :], a[:, 0:d, :, :]))
                    done(ve.tensor_tensor(b[:, d:NT, :, :], a[:, d:NT, :, :], a[:, 0:NT - d, :, :], ALU.add))
                    at, d = 1 - at, 2 * d
                done(ve.tensor_tensor(rank[:, :, :, :], cum[at][:, :, :, :], v4(cum_ps), ALU.add))
                done(ve.tensor_tensor(rank[:, :, :, :], rank[:, :, :, :], ohb[:, :, :, :], ALU.mult))
                for k in range(2):
                    done(ve.tensor_reduce(rk[:, k, :], rank[:, :, k, :], X_AXIS, ALU.add))
                    done(ve.tensor_scalar(rk[:, k, :], rk[:, k, :], float(capacity) + 0.5, None, ALU.is_lt))
                    done(ve.tensor_tensor(w_[:, k, :], w_[:, k, :], rk[:, k, :], ALU.mult))
            done(ve.tensor_tensor(t_[:, :, :], oh[0][:, :, :], bc(w_[:, 0, :]), ALU.mult))
            done(ve.tensor_tensor(sc[:, :, :], oh[1][:, :, :], bc(w_[:, 1, :]), ALU.mult))
            done(ve.tensor_tensor(comb[:, :, :], t_[:, :, :], sc[:, :, :], ALU.add))


def experts_stage(nc, R, name, W, gated):
    NE = 8
    with Stage(nc, name) as s:
        HB = 2 if gated else 4
        xs = s.sb("xs", [128, GT])
        w1 = s.sb("w1", [128, NE, 512])
        w2 = s.sb("w2", [128, NE, HB, D])
        h = s.sb("h", [128, 2, HB, GT])
        cs = s.sb("cs", [128, 4, NE])
        acc = s.sb("acc", [128, 4, D])
        h_ps, y_ps = s.ps("h", [128, 4, 512]), s.ps("y", [128, 2, 512])
        i_ps, f_ps = s.ps("i", [128, 512]), s.ps("f", [128, 512])
        (loaded, xs_ready, cs_ready, h_done, h_ready, y_done, acc_step, f_done, x_added, init_done, ct_ready, ct_done, sg_ready) = s.sems(
            "loaded xs_ready cs_ready h_done h_ready y_done acc_step f_done x_added init_done ct_ready ct_done sg_ready")
        n_load = 2
        if gated:
            sg = s.sb("sg", [128, 2, 2, GT])
        else:
            b1, b2, ct = s.sb("b1", [128, NE, 4]), s.sb("b2", [NE, D]), s.sb("ct", [NE, GT])
            n_load = 4
        block = s.block()
        x, xn, comb, ident = R["x"], R["xn"], R["comb"], R["ident"]

        @block.sync
        def _(sp):
            sp.dma_start(w1[:, :, :], W["w1"]).then_inc(loaded, 16)
            sp.dma_start(w2[:, :, :, :], W["w2"]).then_inc(loaded, 16)
            if not gated:
                sp.dma_start(b1[:, :, :], W["b1"]).then_inc(loaded, 16)
                sp.dma_start(b2[:, :], W["b2"]).then_inc(loaded, 16)
            sp.wait_ge(loaded, START + 16 * n_load)

        @block.tensor
        def _(pe):
            pe.wait_ge(loaded, START + 16 * n_load)

            def hidden(g, ex):
                for i in range(4):
                    n = 4 * ex + i
                    if n >= 4:
                        pe.wait_ge(h_ready, START + g * 32 + n - 3)
                    else:
                        pe.wait_ge(h_ready, START + g * 32)
                    pe.matmul(h_ps[:, i, :], w1[:, ex, i * 128:(i + 1) * 128], xs[:, :], start=True, stop=True).then_inc(h_done, 1)

            def down(g, ex):
                pe.wait_ge(h_ready, START + g * 32 + 4 * ex + 4)
                if ex >= 2:
                    pe.wait_ge(acc_step, START + g * 9 + ex)
                else:
                    pe.wait_ge(acc_step, START + g * 9)
                for t in range(4):
                    for c in range(HB):
                        mm = pe.matmul(y_ps[:, ex % 2, t * D:(t + 1) * D], h[:, ex % 2, c, t * 128:(t + 1) * 128],
                                       w2[:, ex, c, :], start=(c == 0), stop=(c == HB - 1))
                mm.then_inc(y_done, 1)

            with pe.Fori(0, NG) as g:
                pe.wait_ge(xs_ready, START + g + 1)
                pe.wait_ge(cs_ready, START + g + 1)
                if not gated:
                    for t in range(4):
                        mm = pe.transpose(i_ps[0:NE, t * 128:(t + 1) * 128], cs[:, t, :], ident[:, :])
                    mm.then_inc(ct_done, 1)
                    pe.wait_ge(ct_ready, START + g + 1)
                    for t in range(4):
                        mm = pe.matmul(i_ps[:, t * D:(t + 1) * D], ct[:, t * 128:(t + 1) * 128], b2[:, :], start=True, stop=True)
                    mm.then_inc(init_done, 1)
                hidden(g, 0)
                for ex in range(NE):
                    if ex < NE - 1:
                        hidden(g, ex + 1)
                    down(g, ex)
                pe.wait_ge(acc_step, START + g * 9 + 9)
                for t in range(4):
                    mm = pe.transpose(f_ps[:, t * 128:(t + 1) * 128], acc[:, t, :], ident[:, :])
                mm.then_inc(f_done, 1)

        @block.scalar
        def _(act):
            act.wait_ge(loaded, START + 16 * n_load)
            with act.Fori(0, NG) as g:
                act.wait_ge(h_done, START + g * 32)
                act.activation(xs[:, :], xn[:, at_group(g)], ACT.Copy).then_inc(xs_ready, 1)
                for ex in range(NE):
                    if gated:
                        act.wait_ge(h_ready, START + (g * 32 + 4 * (ex - 1) if ex >= 2 else g * 32))
                    else:
                        act.wait_ge(y_done, START + (g * 8 + ex - 1 if ex >= 2 else g * 8))
                    if gated:
                        for i in range(2):
                            act.wait_ge(h_done, START + g * 32 + 4 * ex + 2 * i + 1)
                            act.activation(sg[:, ex % 2, i, :], h_ps[:, 2 * i, :], ACT.Silu).then_inc(sg_ready, 1)
                    else:
                        for i in range(4):
                            act.wait_ge(h_done, START + g * 32 + 4 * ex + i + 1)
                            act.activation(h[:, ex % 2, i, :], h_ps[:, i, :], ACT.Relu, bias=b1[:, ex, i:i + 1]).then_inc(h_ready, 1)

        @block.gpsimd
        def _(pool):
            pass

        @block.vector
        def _(ve):
            with ve.Fori(0, NG) as g:
                if not gated:
                    ve.wait_ge(ct_done, START + g)
                ve.wait_ge(acc_step, START + g * 9)
                ve.tensor_copy(cs[:, :, :], comb[:, bass.ds(g * 4, 4), :]).then_inc(cs_ready, 1)
                ve.wait_ge(cs_ready, START + g + 1)
                if gated:
                    ve.wait_ge(f_done, START + g)
                    ve.memset(acc[:, :, :], 0.0).then_inc(acc_step, 1)
                else:
                    ve.wait_ge(ct_done, START + g + 1)
                    ve.tensor_copy(ct[:, :], i_ps[0:NE, :]).then_inc(ct_ready, 1)
                    ve.wait_ge(init_done, START + g + 1)
                    ve.wait_ge(f_done, START + g)
                    ve.tensor_copy(acc[:, :, :], i_ps[:, :].rearrange("p (t d) -> p t d", t=4)).then_inc(acc_step, 1)

                def product(ex):
                    for i in range(2):
                        ve.wait_ge(h_done, START + g * 32 + 4 * ex + 2 * i + 2)
                        ve.wait_ge(sg_ready, START + g * 16 + 2 * ex + i + 1)
                        ve.tensor_tensor(h[:, ex % 2, i, :], sg[:, ex % 2, i, :], h_ps[:, 2 * i + 1, :], ALU.mult).then_inc(h_ready, 2)

                if gated:
                    product(0)
                for ex in range(NE):
                    if gated and ex < NE - 1:
                        if ex >= 1:
                            ve.wait_ge(y_done, START + g * 8 + ex)
                        product(ex + 1)
                    ve.wait_ge(y_done, START + g * 8 + ex + 1)
                    ve.wait_ge(acc_step, START + g * 9 + ex + 1)
                    for t in range(4):
                        a = ve.scalar_tensor_tensor(acc[:, t, :], y_ps[:, ex % 2, t * D:(t + 1) * D], cs[:, t, ex:ex + 1],
                                                    acc[:, t, :], ALU.mult, ALU.add)
                    a.then_inc(acc_step, 1)
                ve.wait_ge(f_done, START + g + 1)
                ve.tensor_tensor(x[:, at_group(g)], x[:, at_group(g)], f_ps[:, :], ALU.add).then_inc(x_added, 1)


def binary_stage(nc, R, name, W):
    with Stage(nc, name) as s:
        w1, w1t = s.sb("w1", [128, 4, D]), s.sb("w1t", [128, 512])
        w2, w2t = s.sb("w2", [128, 512]), s.sb("w2t", [128, 4, D])
        b1, b2 = s.sb("b1", [128, 4]), s.sb("b2", [128, 1])
        a1, a2 = s.sb("a1", [128, 4]), s.sb("a2", [128, 1])
        h = s.sb("h", [128, 2, 4, GT])
        yt = s.sb("yt", [128, GT])
        h_ps, y_ps = s.ps("h", [128, 4, 512]), s.ps("y", [128, 2, 512])
        loaded, summed, scaled, signed, h_done, h_ready, y_done, yt_ready, x_added = s.sems(
            "loaded summed scaled signed h_done h_ready y_done yt_ready x_added")
        block = s.block()
        x, xn = R["x"], R["xn"]

        @block.sync
        def _(sp):
            for dst, src in ((w1[:, :, :], "w1"), (w1t[:, :], "w1t"), (w2[:, :], "w2"), (w2t[:, :, :], "w2t"), (b1[:, :], "b1"), (b2[:, :], "b2")):
                sp.dma_start(dst, W[src]).then_inc(loaded, 16)
            sp.wait_ge(loaded, START + 96)

        @block.tensor
        def _(pe):
            pe.wait_ge(signed, START + 2)

            def up(g, n):
                for i in range(4):
                    pe.matmul(h_ps[:, i, :], w1t[:, i * 128:(i + 1) * 128], xn[:, at_group(g)], start=True, stop=True).then_inc(h_done, 1)

            with pe.Fori(0, NG) as g:
                up(g, 0)
                pe.wait_ge(h_ready, START + g * 4 + 4)
                pe.wait_ge(yt_ready, START + g)
                for i in range(4):
                    mm = pe.matmul(y_ps[:, 0, :], w2t[:, i, :], h[:, 0, i, :], start=(i == 0), stop=(i == 3))
                mm.then_inc(y_done, 1)

        @block.scalar
        def _(act):
            act.wait_ge(loaded, START + 96)
            act.activation(w1t[:, :], w1t[:, :], ACT.Sign).then_inc(signed, 1)
            act.activation(w2t[:, :, :], w2t[:, :, :], ACT.Sign).then_inc(signed, 1)
            act.wait_ge(scaled, START + 2)
            with act.Fori(0, NG) as g:
                for i in range(4):
                    act.wait_ge(h_done, START + g * 4 + i + 1)
                    if i == 0:
                        act.wait_ge(y_done, START + g)
                    act.activation(h[:, 0, i, :], h_ps[:, i, :], ACT.Gelu, bias=b1[:, i:i + 1], scale=a1[:, i:i + 1]).then_inc(h_ready, 1)

        @block.gpsimd
        def _(pool):
            pass

        @block.vector
        def _(ve):
            ve.wait_ge(loaded, START + 96)
            ve.tensor_reduce(a1[:, :], w1[:, :, :], X_AXIS, ALU.add, apply_absolute_value=True).then_inc(summed, 1)
            ve.tensor_reduce(a2[:, :], w2[:, :], X_AXIS, ALU.add, apply_absolute_value=True).then_inc(summed, 1)
            ve.wait_ge(summed, START + 2)
            ve.tensor_scalar(a1[:, :], a1[:, :], 1.0 / D, None, ALU.mult).then_inc(scaled, 1)
            ve.tensor_scalar(a2[:, :], a2[:, :], 1.0 / 512, None, ALU.mult).then_inc(scaled, 1)
            ve.wait_ge(scaled, START + 2)
            with ve.Fori(0, NG) as g:
                ve.wait_ge(y_done, START + g + 1)
                ve.wait_ge(x_added, START + g)
                ve.tensor_scalar(yt[:, :], y_ps[:, 0, :], a2[:, 0:1], b2[:, 0:1], ALU.mult, ALU.add).then_inc(yt_ready, 1)
                ve.wait_ge(yt_ready, START + g + 1)
                ve.tensor_tensor(x[:, at_group(g)], x[:, at_group(g)], yt[:, :], ALU.add).then_inc(x_added, 1)


DEPTH = 6
FF = 341
WA, WM = 6148, 1161
FB = [(0, 128), (128, 256), (256, 341)]


def local_stage(nc, R, name, W):
    with Stage(nc, name) as s:
        T = attn64_tiles(s)
        xs2 = s.sb("xs", [128, 2, GT])
        xs = xs2[:, 0, :]
        wa, wm = s.sb("wa", [128, WA]), s.sb("wm", [128, WM])
        w_qk = wa[:, 0:2048].rearrange("p (a c) -> p a c", a=2)
        w_rot = wa[:, 2048:4096].rearrange("p (a c) -> p a c", a=2)
        wv, wo, scales = wa[:, 4096:5120], wa[:, 5120:6144], wa[:, 6144:6148]
        w1 = wm[:, 0:768].rearrange("p (a c) -> p a c", a=6)
        w2 = wm[:, 768:1152].rearrange("p (a c) -> p a c", a=3)
        cols = wm[:, 1152:1161]
        tables = s.sb("tables", [128, 4, SEQ])
        tab = s.sb("tab", [128, 4, SEQ])
        sq, m1, m2 = (s.sb(n, [128, 2, GT]) for n in ("sq", "m1", "m2"))
        rn = s.sb("rn", [128, 2, GT])
        xc, sqx, rstd = m1, sq, m2
        xg = T["qt"][:, :, :].rearrange("p i t -> p (i t)")
        gl, h = s.sb("gl", [128, 3, GT]), s.sb("h", [128, 3, GT])
        ten, thirteen, tiny = s.sb("ten", [128, 1]), s.sb("thirteen", [128, 1]), s.sb("tiny", [128, 1])
        geo = Geometry(R, band=True)
        sem = named(s, CORE_SEMS + [
            "loaded", "zeroed", "attn_w", "mlp_w", "tab_ready", "xs_ready", "proj_done", "rot_done", "squared", "m_ready",
            "summed", "norm_done", "norm_ln", "rn_ready", "qk_ready", "k_ready", "v_done",
            "v_ready", "y_done", "y_added", "mean_done", "centred", "sqx_ready", "var_done", "ln_done", "rstd_ready", "xg_step",
            "xg_ready", "shifted", "up_done", "gl_ready", "h_ready", "out_done", "out_added", "x_added"])
        core = attn64_core(nc, R, T, geo, sem)
        block = s.block()
        x, y = R["x"], R["xn"]
        qt, kt, v, ot = T["qt"], T["kt"], T["v"], T["ot"]
        s_ps, st_ps, o_ps = T["s_ps"], T["st_ps"], T["o_ps"]
        k_raw = T["on"][:, :, :].rearrange("p t c -> p (t c)").rearrange("p (i t) -> p i t", i=NB)
        raw = [qt, k_raw]
        two = lambda ap: ap.rearrange("p (b t) -> p b t", b=2)

        @block.sync
        def _(sp):
            sp.dma_start(tables[:, :, :], W["tables"]).then_inc(sem["loaded"], 16)
            with sp.Fori(0, DEPTH) as d:
                off_a, off_m = sp.snap(d * (128 * WA)), sp.snap(d * (128 * WM))
                sp.wait_ge(sem["y_added"], START + d * NG)
                sp.dma_start(wa[:, :], W["wa"][bass.ds(off_a, 128 * WA)].rearrange("(p c) -> p c", p=128)).then_inc(sem["attn_w"], 16)
                sp.wait_ge(sem["out_added"], START + d * NG)
                sp.dma_start(wm[:, :], W["wm"][bass.ds(off_m, 128 * WM)].rearrange("(p c) -> p c", p=128)).then_inc(sem["mlp_w"], 16)
            sp.wait_ge(sem["attn_w"], START + DEPTH * 16)
            sp.wait_ge(sem["mlp_w"], START + DEPTH * 16)
            sp.wait_ge(sem["loaded"], START + 16)

        @block.tensor
        def _(pe):
            pe.wait_ge(sem["zeroed"], START + 7)

            def attn(n):
                pe.wait_ge(sem["xs_ready"], START + n + 1)
                pe.wait_ge(sem["ot_ready"], START + n * NB)
                for i in range(16):
                    a, c = divmod(i, NB)
                    bank = 2 * (i % 2)
                    pe.wait_ge(sem["m_ready"], START + (n * 32 + 2 * (i - 1) if i >= 2 else n * 32))
                    pe.wait_ge(sem["squared"], START + (n * 16 + i - 1 if i >= 2 else n * 16))
                    pe.matmul(s_ps[:, bank, :], w_qk[:, a, c * 128:(c + 1) * 128], xs, start=True, stop=True).then_inc(sem["proj_done"], 1)
                    pe.matmul(s_ps[:, bank + 1, :], w_rot[:, a, c * 128:(c + 1) * 128], xs, start=True, stop=True).then_inc(sem["rot_done"], 1)
                    if i >= 1:
                        norms(n, i - 1)
                norms(n, 15)
                pe.wait_ge(sem["m_ready"], START + n * 32 + 32)
                pe.wait_ge(sem["k_ready"], START + n * 8 + 1)
                core.scores(pe, n, 0)
                core.scores(pe, n, 1)
                for i in range(8):
                    t, half = divmod(i, 2)
                    if i >= 2:
                        pe.wait_ge(sem["v_ready"], START + n * 8 + i - 1)
                    pe.matmul(o_ps[:, half, :], xs[:, t * 128:(t + 1) * 128], wv[:, half * 512:(half + 1) * 512], start=True, stop=True).then_inc(sem["v_done"], 1)
                pe.wait_ge(sem["norm_ln"], START + n * 16 + 16)
                for u in range(17):
                    if u < 16:
                        core.turn_probs(pe, n, u)
                    if u < 14:
                        pe.wait_ge(sem["k_ready"], START + n * 8 + u // 2 + 2)
                        core.scores(pe, n, u + 2)
                    if u == 1:
                        pe.wait_ge(sem["v_ready"], START + n * 8 + 8)
                    if u > 0:
                        core.values(pe, n, u - 1)
                for i in range(NB):
                    core.turn_out(pe, n, i)
                    if i >= 1:
                        pe.wait_ge(sem["ot_ready"], START + n * NB + i)
                        pe.matmul(st_ps[:, 0, :], wo[:, (i - 1) * 128:i * 128], ot[:, (i - 1) % 2, :], start=(i == 1), stop=False)
                pe.wait_ge(sem["ot_ready"], START + n * NB + NB)
                pe.matmul(st_ps[:, 0, :], wo[:, (NB - 1) * 128:], ot[:, (NB - 1) % 2, :], start=False, stop=True).then_inc(sem["y_done"], 1)

            def norms(n, i):
                pe.wait_ge(sem["squared"], START + n * 16 + i + 1)
                if i >= 2:
                    pe.wait_ge(sem["norm_ln"], START + n * 16 + i - 1)
                else:
                    pe.wait_ge(sem["y_added"], START + n)
                pe.matmul(st_ps[:, i % 2, :], R["head_ones"][:, :], sq[:, i % 2, :], start=True, stop=True).then_inc(sem["norm_done"], 1)

            def layer_norm(m):
                for k in range(2):
                    pe.wait_ge(sem["shifted"], START + m * 2 + k + 1)
                    pe.matmul(s_ps[:, k, :], R["mean_w"][:, :], xs2[:, k, :], start=True, stop=True).then_inc(sem["mean_done"], 1)
                for k in range(2):
                    pe.wait_ge(sem["sqx_ready"], START + m * 2 + k + 1)
                    pe.matmul(s_ps[:, 2 + k, :], R["mean_w"][:, :], sqx[:, k, :], start=True, stop=True).then_inc(sem["var_done"], 1)

            banks = [st_ps[:, 0, :], st_ps[:, 1, :], o_ps[:, 0, :], s_ps[:, 2, :], s_ps[:, 3, :], o_ps[:, 1, :]]

            def up(n, g, i):
                a, b = FB[i]
                for k in (i, 3 + i):
                    mm = pe.matmul(banks[k][0:b - a, :], w1[:, k, 0:b - a], xg[:, at_group(g)], start=True, stop=True)
                mm.then_inc(sem["up_done"], 1)

            def down(n, i):
                a, b = FB[i]
                pe.wait_ge(sem["h_ready"], START + n * 3 + i + 1)
                if i == 0:
                    pe.wait_ge(sem["out_added"], START + n)
                mm = pe.matmul(s_ps[:, 0, :], w2[0:b - a, i, :], h[0:b - a, i, :], start=(i == 0), stop=(i == 2))
                if i == 2:
                    mm.then_inc(sem["out_done"], 1)

            with pe.Fori(0, DEPTH) as d:
                with pe.Fori(0, NG) as g:
                    pe.wait_ge(sem["attn_w"], START + d * 16 + 16)
                    attn(d * NG + g)
                with pe.Fori(0, NG // 2) as g2:
                    layer_norm(d * (NG // 2) + g2)
                pe.wait_ge(sem["mlp_w"], START + d * 16 + 16)
                pe.wait_ge(sem["xg_ready"], START + d * NG + NG)
                for i in range(3):
                    up(d * NG, 0, i)
                with pe.Fori(1, NG) as g:
                    for i in range(3):
                        down(d * NG + g - 1, i)
                        up(d * NG + g, g, i)
                for i in range(3):
                    down(d * NG + NG - 1, i)

        @block.scalar
        def _(act):
            act.wait_ge(sem["zeroed"], START + 7)

            def shift(xs, g, ready):
                act.activation(xs[0:64, :], y[0:64, at_group(g)], ACT.Copy)
                for b in range(2):
                    last = act.activation(xs[64:128, b * SEQ + 1:(b + 1) * SEQ], y[64:128, bass.ds(g * GT + b * SEQ, SEQ - 1)], ACT.Copy)
                last.then_inc(ready, 1)

            def inverse_norms(n, i):
                act.wait_ge(sem["norm_done"], START + n * 16 + i + 1)
                act.wait_ge(sem["qk_ready"], START + n * 16 + max(0, i - 1))
                act.activation(rn[:, i % 2, :], st_ps[:, i % 2, :], ACT.Ln, scale=float(2 ** 20), bias=tiny[:, :]).then_inc(sem["norm_ln"], 1)
                act.wait_ge(sem["norm_ln"], START + n * 16 + i + 1)
                act.activation(rn[:, i % 2, :], rn[:, i % 2, :], ACT.Exp, scale=-0.5, bias=(thirteen if i < NB else ten)[:, :]).then_inc(sem["rn_ready"], 1)

            def spread_k(n, i):
                act.wait_ge(sem["qk_ready"], START + n * 16 + 8 + i + 1)
                act.activation(kt[0:64, i, 0, :], k_raw[0:64, i, :], ACT.Copy)
                act.activation(kt[64:128, i, 1, :], k_raw[64:128, i, :], ACT.Copy).then_inc(sem["k_ready"], 1)

            def attn(n, g, d):
                act.wait_ge(sem["v_done"], START + n * 8)
                act.wait_ge(sem["out_added"], START + d * NG)
                shift(xs, g, sem["xs_ready"])
                for i in range(16):
                    act.wait_ge(sem["proj_done"], START + n * 16 + i + 1)
                    act.wait_ge(sem["m_ready"], START + n * 32 + 2 * i + 1)
                    act.wait_ge(sem["norm_done"], START + (n * 16 + i - 1 if i >= 2 else n * 16))
                    act.activation(sq[:, i % 2, :], s_ps[:, 2 * (i % 2), :], ACT.Square).then_inc(sem["squared"], 1)
                    if i >= 1:
                        inverse_norms(n, i - 1)
                    if i >= 12:
                        spread_k(n, i - 12)
                inverse_norms(n, 15)
                for i in range(8):
                    if i < 4:
                        spread_k(n, 4 + i)
                    t, half = divmod(i, 2)
                    act.wait_ge(sem["v_done"], START + n * 8 + i + 1)
                    act.activation(v[:, t, 8 * half:8 * half + 8, 0:DH], o_ps[:, half, :].rearrange("p (h d) -> p h d", h=8), ACT.Copy).then_inc(sem["v_ready"], 1)
                core.exps(act, n, 0)
                core.exps(act, n, 1)
                for u in range(16):
                    core.keep_probs0(act, n, u)
                    if u < 14:
                        core.exps(act, n, u + 2)

            def layer_norm(m, g2, d):
                act.wait_ge(sem["centred"], START + m * 2)
                for k in range(2):
                    shift(xs2[:, k, :], g2 * 2 + k, sem["shifted"])
                for k in range(2):
                    act.wait_ge(sem["centred"], START + m * 2 + k + 1)
                    act.activation(sqx[:, k, :], xc[:, k, :], ACT.Square).then_inc(sem["sqx_ready"], 1)
                for k in range(2):
                    act.wait_ge(sem["var_done"], START + m * 2 + k + 1)
                    act.activation(sqx[:, k, :], s_ps[:, 2 + k, :], ACT.Ln, bias=R["eps"][:, :]).then_inc(sem["ln_done"], 1)
                for k in range(2):
                    act.wait_ge(sem["ln_done"], START + m * 2 + k + 1)
                    act.activation(rstd[:, k, :], sqx[:, k, :], ACT.Exp, scale=-0.5).then_inc(sem["rstd_ready"], 1)
                for k in range(2):
                    act.wait_ge(sem["xg_step"], START + m * 2 + k + 1)
                    act.activation(xg[:, bass.ds((g2 * 2 + k) * GT, GT)], xc[:, k, :], ACT.Identity, scale=cols[:, 0:1], bias=cols[:, 1:2]).then_inc(sem["xg_ready"], 1)

            banks = [s_ps[:, 2, :], s_ps[:, 3, :], o_ps[:, 1, :]]
            with act.Fori(0, DEPTH) as d:
                act.preload_act_table_set(LN_EXP)
                with act.Fori(0, NG) as g:
                    attn(d * NG + g, g, d)
                act.wait_ge(sem["v_done"], START + d * 64 + 64)
                act.wait_ge(sem["y_added"], START + d * NG + NG)
                act.wait_ge(sem["mlp_w"], START + d * 16 + 16)
                with act.Fori(0, NG // 2) as g2:
                    layer_norm(d * (NG // 2) + g2, g2, d)
                act.preload_act_table_set(GELU)
                with act.Fori(0, NG) as g:
                    n = d * NG + g
                    for i, (a, b) in enumerate(FB):
                        act.wait_ge(sem["up_done"], START + n * 3 + i + 1)
                        act.activation(gl[0:b - a, i, :], banks[i][0:b - a, :], ACT.Gelu, bias=cols[0:b - a, 5 + i:6 + i]).then_inc(sem["gl_ready"], 1)

        @block.gpsimd
        def _(pool):
            pool.memset(T["e"][:, :, :, :], 0.0).then_inc(sem["zeroed"], 1)
            pool.memset(v[:, :, :, :], 1.0).then_inc(sem["zeroed"], 1)
            pool.memset(kt[:, :, :, :], 0.0).then_inc(sem["zeroed"], 1)
            pool.memset(tiny[:, :], 1e-24).then_inc(sem["zeroed"], 1)
            pool.memset(xs2[:, :, :], 0.0).then_inc(sem["zeroed"], 1)
            pool.memset(ten[:, :], float(10 * np.log(2.0))).then_inc(sem["zeroed"], 1)
            pool.memset(thirteen[:, :], float(13 * np.log(2.0))).then_inc(sem["zeroed"], 1)
            pool.wait_ge(sem["zeroed"], START + 7)

            with pool.Fori(0, DEPTH) as d:
                with pool.Fori(0, NG) as g:
                    n = d * NG + g
                    for i in range(16):
                        pool.wait_ge(sem["m_ready"], START + n * 32 + 2 * i + 2)
                        pool.tensor_tensor(raw[i // NB][:, i % NB, :], m1[:, i % 2, :], m2[:, i % 2, :], ALU.add).then_inc(sem["summed"], 1)

        @block.vector
        def _(ve):
            ve.wait_ge(sem["zeroed"], START + 7)
            ve.wait_ge(sem["loaded"], START + 16)

            def scale_block(n, i):
                a, c = divmod(i, NB)
                ve.wait_ge(sem["rn_ready"], START + n * 16 + i + 1)
                ve.wait_ge(sem["summed"], START + n * 16 + i + 1)
                ve.scalar_tensor_tensor(raw[a][:, c, :], rn[:, i % 2, :], 8e12 if a == 0 else 1e12, raw[a][:, c, :], ALU.min, ALU.mult).then_inc(sem["qk_ready"], 1)

            def attn(n, g):
                for i in range(16):
                    a, c = divmod(i, NB)
                    if i >= 2:
                        ve.wait_ge(sem["summed"], START + n * 16 + i - 1)
                    else:
                        ve.wait_ge(sem["summed"], START + n * 16)
                    tb = lambda k: tab[:, k, :].unsqueeze(1).to_broadcast([128, 2, SEQ])
                    ve.wait_ge(sem["proj_done"], START + n * 16 + i + 1)
                    ve.tensor_tensor(two(m1[:, i % 2, :]), two(s_ps[:, 2 * (i % 2), :]), tb(2 * a), ALU.mult).then_inc(sem["m_ready"], 1)
                    ve.wait_ge(sem["rot_done"], START + n * 16 + i + 1)
                    ve.tensor_tensor(two(m2[:, i % 2, :]), two(s_ps[:, 2 * (i % 2) + 1, :]), tb(2 * a + 1), ALU.mult).then_inc(sem["m_ready"], 1)
                    if i >= 2:
                        scale_block(n, i - 2)
                core.maxima(ve, n, 0)
                scale_block(n, 14)
                core.maxima(ve, n, 1)
                scale_block(n, 15)
                for u in range(17):
                    if u < 16:
                        core.keep_probs1(ve, n, u)
                    if u < 14:
                        core.maxima(ve, n, u + 2)
                    if u == 1:
                        ve.wait_ge(sem["k_ready"], START + n * 8 + 8)
                    if u > 0:
                        core.normalise(ve, n, u - 1)
                for i in range(NB):
                    ve.wait_ge(sem["ot_done"], START + n * NB + i + 1)
                    ve.tensor_copy(ot[:, i % 2, :], s_ps[:, i % 4, :]).then_inc(sem["ot_ready"], 1)
                ve.wait_ge(sem["y_done"], START + n + 1)
                ve.tensor_tensor(y[:, at_group(g)], y[:, at_group(g)], st_ps[:, 0, :], ALU.add).then_inc(sem["y_added"], 1)

            def layer_norm(m):
                for k in range(2):
                    ve.wait_ge(sem["mean_done"], START + m * 2 + k + 1)
                    ve.wait_ge(sem["xg_ready"], START + m * 2)
                    ve.tensor_tensor(xc[:, k, :], xs2[:, k, :], s_ps[:, k, :], ALU.subtract).then_inc(sem["centred"], 1)
                for k in range(2):
                    ve.wait_ge(sem["rstd_ready"], START + m * 2 + k + 1)
                    ve.tensor_tensor(xc[:, k, :], xc[:, k, :], rstd[:, k, :], ALU.mult).then_inc(sem["xg_step"], 1)

            lin = [st_ps[:, 0, :], st_ps[:, 1, :], o_ps[:, 0, :]]

            def hidden(n, i):
                a, b = FB[i]
                ve.wait_ge(sem["gl_ready"], START + n * 3 + i + 1)
                ve.scalar_tensor_tensor(h[0:b - a, i, :], lin[i][0:b - a, :], cols[0:b - a, 2 + i:3 + i], gl[0:b - a, i, :],
                                        ALU.add, ALU.mult).then_inc(sem["h_ready"], 1)

            def add_out(n, g):
                ve.wait_ge(sem["out_done"], START + n + 1)
                ve.scalar_tensor_tensor(y[:, at_group(g)], s_ps[:, 0, :], cols[:, 8:9], y[:, at_group(g)], ALU.add, ALU.add).then_inc(sem["out_added"], 1)

            with ve.Fori(0, DEPTH) as d:
                ve.wait_ge(sem["attn_w"], START + d * 16 + 16)
                for k in range(4):
                    tt = ve.tensor_scalar(tab[:, k, :], tables[:, k, :], scales[:, k:k + 1], None, ALU.mult)
                    tt.then_inc(sem["tab_ready"], 1)
                with ve.Fori(0, NG) as g:
                    ve.wait_ge(sem["tab_ready"], START + d * 4 + 4)
                    attn(d * NG + g, g)
                with ve.Fori(0, NG // 2) as g2:
                    layer_norm(d * (NG // 2) + g2)
                for i in range(3):
                    hidden(d * NG, i)
                with ve.Fori(1, NG) as g:
                    hidden(d * NG + g, 0)
                    add_out(d * NG + g - 1, g - 1)
                    hidden(d * NG + g, 1)
                    hidden(d * NG + g, 2)
                add_out(d * NG + NG - 1, NG - 1)
            with ve.Fori(0, NG) as g:
                ve.wait_ge(sem["out_added"], START + DEPTH * NG)
                ve.tensor_tensor(x[:, at_group(g)], x[:, at_group(g)], y[:, at_group(g)], ALU.add).then_inc(sem["x_added"], 1)


def store_stage(nc, R, out):
    with Stage(nc, "store") as s:
        (stored,) = s.sems("stored")
        block = s.block()

        @block.sync
        def _(sp):
            sp.dma_start(out, R["x"][:, :]).then_inc(stored, 16)
            sp.wait_ge(stored, START + 16)


CONST_BF = [("ident", 128), ("causal", 128), ("band", 128), ("band_q1", 160), 
            ("upper", 128), ("ones", 128), ("first", 8), ("head_ones", 128)]


def build(nc, IN, out, stages):
    with ExitStack() as ctx:
        sb = lambda n, shape, dt=F32: ctx.enter_context(nc.sbuf_tensor(n, shape, dt))
        R = {"x": sb("x_res", [128, TOK]), "xn": sb("xn_res", [128, TOK]), "ident": sb("ident", [128, 128]),
             "mean_w": sb("mean_w", [128, 128]), "eps": sb("eps", [128, 1]), "comb": sb("comb", [128, NT, 8]),
             "head_ones": sb("head_ones", [128, 128]), "c_bf": sb("consts_bf", [128, sum(w for _, w in CONST_BF)], BF16)}
        at, C = 0, {}
        for n, w in CONST_BF:
            C[n] = R["c_bf"][:, at:at + w]
            at += w
        R["masks"] = C
        R["ident_bf"], R["upper_bf"], R["ones_bf"], R["first"] = C["ident"], C["upper"], C["ones"], C["first"]
        load_stage(nc, R, IN)
        if "norm0" in stages:
            norm_stage(nc, R, "norm0")
        if "attn0" in stages:
            attn64_stage(nc, R, "attn0", {k: IN[f"a0_{k}"] for k in ("wq", "wk", "wv", "wo")}, 0.125)
        if "ffn0" in stages:
            gate_stage(nc, R, "gate0", {"wg": IN["f0_wg"], "bg": IN["f0_bg"]}, None)
            experts_stage(nc, R, "ffn0", {k: IN[f"f0_{k}"] for k in ("w1", "w2", "b1", "b2")}, False)
        if "norm1" in stages:
            norm_stage(nc, R, "norm1")
        if "attn1" in stages:
            attn8_stage(nc, R, "attn1", {"low": IN["c_low"], "mix_sel": IN["c_mix_sel"], "mix_mask": IN["c_mix_mask"], **{k: IN[f"a1_{k}"] for k in ("wq", "wk", "wv", "vb", "qkb")}}, 1.0)
        if "ffn1" in stages:
            local_stage(nc, R, "ffn1", {"tables": IN["c_tables"], **{k: IN[f"f1_{k}"] for k in ("wa", "wm")}})
        if "norm2" in stages:
            norm_stage(nc, R, "norm2")
        if "attn2" in stages:
            attn8_stage(nc, R, "attn2", {"low": IN["c_low"], "lora": True, **{k: IN[f"a2_{k}"] for k in ("wq", "wk", "wv", "vb", "qkb", "wo", "wob", "lora_a", "lora_b")}},
                        8 ** -0.5, project=True)
        if "ffn2" in stages:
            binary_stage(nc, R, "ffn2", {k: IN[f"f2_{k}"] for k in ("w1", "w1t", "w2", "w2t", "b1", "b2")})
        if "norm3" in stages:
            norm_stage(nc, R, "norm3")
        if "ffn3" in stages:
            gate_stage(nc, R, "gate3", {"wg": IN["f3_wg"]}, int(1.25 * TOK / 8))
            experts_stage(nc, R, "ffn3", {k: IN[f"f3_{k}"] for k in ("w1", "w2")}, True)
        if "attn3" in stages:
            with Stage(nc, "copy3") as s:
                (added,) = s.sems("added")
                block = s.block()

                @block.vector
                def _(ve):
                    with ve.Fori(0, NG) as g:
                        ve.tensor_tensor(R["x"][:, at_group(g)], R["x"][:, at_group(g)], R["xn"][:, at_group(g)], ALU.add).then_inc(added, 1)
            norm_stage(nc, R, "norm3b", again=True)
            attn8_stage(nc, R, "attn3", {"low": IN["c_low"], **{k: IN[f"a3_{k}"] for k in ("wq", "wk", "wv", "vb", "qkb", "wo", "wob", "gamma", "beta", "wqr", "wkr", "qkbr")},
                                         "cos": IN["c_cos"], "sin": IN["c_sin"]},
                        8 ** -0.5, affine=True, rope=True, project=True)
        store_stage(nc, R, out)


def layouts(a):
    f = np.float32
    T = lambda w: np.ascontiguousarray(np.asarray(w).T)
    L = {"x_t": T(np.asarray(a["L0_attn_x"]).reshape(TOK, D))}
    for n in "qkv":
        L[f"a0_w{n}"] = T(np.asarray(a[f"L0_attn_w_{n}"]).reshape(HEADS * DH, D))
    blocks = lambda w, n: np.ascontiguousarray(w.reshape(n, 128, -1).transpose(1, 0, 2))
    L["a0_wo"] = blocks(T(a["L0_attn_w_o"]), NB).reshape(128, 1024)
    L["f0_wg"], L["f0_bg"] = np.asarray(a["L0_ffn_gate_w"]), np.asarray(a["L0_ffn_gate_b"]).reshape(1, 8)
    L["f0_w1"] = np.ascontiguousarray(np.asarray(a["L0_ffn_w1"]).transpose(1, 0, 2))
    L["f0_w2"] = np.ascontiguousarray(np.asarray(a["L0_ffn_w2"]).reshape(8, 4, 128, D).transpose(2, 0, 1, 3))
    L["f0_b1"] = np.ascontiguousarray(np.asarray(a["L0_ffn_b1"]).reshape(8, 4, 128).transpose(2, 0, 1))
    L["f0_b2"] = np.asarray(a["L0_ffn_b2"])

    def spread(w, key):
        o = np.zeros((w.shape[0], 4, 4, 32), w.dtype)
        o[..., 0:24] = np.tile(w.reshape(-1, 4, 4, 8), (1, 1, 1, 3))
        return o.reshape(-1, 4, 128)

    def spread_bias(bq, bk, one=1.0):
        q, k = (np.zeros((4, 4, 32), f) for _ in range(2))
        q[..., 0:24] = np.tile(bq.reshape(4, 4, 8), (1, 1, 3))
        k[..., 0:24] = np.tile(bk.reshape(4, 4, 8), (1, 1, 3))
        k[..., 24:26] = one
        return np.ascontiguousarray(np.concatenate([q, k]).reshape(8, 128).T)

    def heads8(pre, wq, wk, wv, bq, bk, bv):
        L[f"{pre}_wq"], L[f"{pre}_wk"] = spread(wq, "q"), spread(wk, "k")
        L[f"{pre}_wv"], L[f"{pre}_vb"] = np.ascontiguousarray(wv), bv.reshape(1, D)
        L[f"{pre}_qkb"] = spread_bias(bq, bk)

    w, b = np.asarray(a["L1_attn_W_qkv"]), np.asarray(a["L1_attn_b_qkv"])
    heads8("a1", w[:, 0:128], w[:, 128:256], w[:, 256:384], b[0:128], b[128:256], b[256:384])
    heads8("a2", *(T(a[f"L2_attn_W{n}"]) for n in "qkv"), *(np.asarray(a[f"L2_attn_b{n}"]) for n in "qkv"))
    L["a2_wo"], L["a2_wob"] = T(a["L2_attn_Wo"]), np.asarray(a["L2_attn_bo"]).reshape(D, 1)
    L["a2_lora_a"] = np.stack([np.asarray(a[f"L2_attn_A{n}"]) for n in "qkvo"], 1)
    lb = np.zeros((8, 4, 512), f)
    for n, c in enumerate("qkvo"):
        bt = T(a[f"L2_attn_B{c}"])
        if n < 2:
            lb[:, n] = spread(bt, "").reshape(8, 512)
        else:
            lb[:, n, 0:128] = bt
    L["a2_lora_b"] = lb
    w, b = np.asarray(a["L3_attn_W_in"]), np.asarray(a["L3_attn_b_in"])
    heads8("a3", w[:, 0:128], w[:, 128:256], w[:, 256:384], b[0:128], b[128:256], b[256:384])
    swap = np.array([1, 0, 3, 2, 4, 5, 6, 7])
    turn = lambda m: m.reshape(-1, 16, 8)[:, :, swap].reshape(m.shape[0] if m.ndim > 1 else -1, *([128] if m.ndim > 1 else []))
    L["a3_wqr"], L["a3_wkr"] = spread(turn(w[:, 0:128]), "q"), spread(turn(w[:, 128:256]), "k")
    L["a3_qkbr"] = spread_bias(turn(b[0:128]).reshape(-1), turn(b[128:256]).reshape(-1), 0.0)
    L["a3_wo"], L["a3_wob"] = np.asarray(a["L3_attn_W_out"]), np.asarray(a["L3_attn_b_out"]).reshape(D, 1)
    L["a3_gamma"], L["a3_beta"] = (np.asarray(a[f"L3_attn_{n}"]).reshape(D, 1) for n in ("gamma", "beta"))

    wq = np.asarray(a["L1_ffn_Wqkv"])
    wa = [wq[:, :, 0:2048], wq[:, :, 0:2048].reshape(DEPTH, D, 32, 2, 32)[:, :, :, ::-1].reshape(DEPTH, D, 2048), wq[:, :, 2048:],
          np.asarray(a["L1_ffn_Wo"]).reshape(DEPTH, NB, 128, D).transpose(0, 2, 1, 3).reshape(DEPTH, 128, 1024)]
    w1 = np.zeros((DEPTH, D, 6, 128), f)
    b1 = np.zeros((DEPTH, 128, 6), f)
    w2 = np.zeros((DEPTH, 128, 3, D), f)
    for i, (lo, hi) in enumerate(FB):
        for part in range(2):
            cols = slice(part * FF + lo, part * FF + hi)
            w1[:, :, 3 * part + i, 0:hi - lo] = np.asarray(a["L1_ffn_W1"])[:, :, cols]
            b1[:, 0:hi - lo, 3 * part + i] = np.asarray(a["L1_ffn_b1"])[:, cols]
        w2[:, 0:hi - lo, i] = np.asarray(a["L1_ffn_W2"])[:, lo:hi]
    qs, ks = np.asarray(a["L1_ffn_q_scale"]), np.asarray(a["L1_ffn_k_scale"])
    rot = lambda v: np.concatenate([v[:, 32:], v[:, :32]], 1)
    wa += [np.tile(v, (1, 2))[:, :, None] for v in (qs, rot(qs), ks, rot(ks))]
    wm = [w1.reshape(DEPTH, D, 768), w2.reshape(DEPTH, 128, 384)]
    wm += [np.asarray(a[f"L1_ffn_{n}"])[:, :, None] for n in ("ln_g", "ln_b")] + [b1, np.asarray(a["L1_ffn_b2"])[:, :, None]]
    L["f1_wa"], L["f1_wm"] = (np.ascontiguousarray(np.concatenate(w, 2)).reshape(-1) for w in (wa, wm))

    w1, w2 = np.asarray(a["L2_ffn_w1"]), np.asarray(a["L2_ffn_w2"])
    L["f2_w1"], L["f2_w1t"] = blocks(w1, 4), T(w1)
    L["f2_w2"], L["f2_w2t"] = w2, blocks(T(w2), 4)
    L["f2_b1"] = T(np.asarray(a["L2_ffn_b1"]).reshape(4, 128))
    L["f2_b2"] = np.asarray(a["L2_ffn_b2"]).reshape(D, 1)
    L["f3_wg"] = T(a["L3_ffn_gate_w"])
    gp, up = (np.asarray(a[f"L3_ffn_{n}_proj_w"]).reshape(8, 2, 128, D) for n in ("gate", "up"))
    L["f3_w1"] = np.ascontiguousarray(np.stack([gp, up], 2).transpose(4, 0, 1, 2, 3)).reshape(D, 8, 512)
    L["f3_w2"] = np.ascontiguousarray(np.asarray(a["L3_ffn_down_proj_w"]).reshape(8, D, 2, 128).transpose(3, 0, 2, 1))
    return L


def constants():
    f = np.float32
    i, j = np.arange(128)[:, None], np.arange(128)[None, :]
    m = lambda bad: np.where(bad, NEG, 0.0).astype(f)
    C = {"ident": np.eye(128, dtype=f), "causal": m(j > i)}
    band = lambda q, k: m((k > q) | (k < q - 32))
    j160 = np.arange(160)[None, :]
    C["band"] = band(i, j)
    C["band_q1"] = band(128 + i, 96 + j160)
    C["upper"] = (i <= j).astype(f)
    C["ones"] = np.ones((128, 128), f)
    C["first"] = np.broadcast_to(np.arange(8, 0, -1).astype(f), (128, 8))
    C["head_ones"] = (i // 64 == j // 64).astype(f)
    out = {"c_bf": np.concatenate([C[n] for n, _ in CONST_BF], 1), "c_ident": C["ident"]}
    out["c_mix_sel"] = (i // 16 == np.arange(8)[None, :]).astype(f)
    out["c_mix_mask"] = (i % 16 == j // 8).astype(f)
    low = np.zeros((4, 32, 2), f)
    low[:, 8:16, 0] = low[:, 16:24, 1] = -1.0
    out["c_low"] = low.reshape(128, 2)
    t = np.arange(SEQ, dtype=f)
    fr = np.repeat(t[:, None] * (1.0 / 10000.0 ** (np.arange(0, 4, 2, dtype=f) / f(4))).astype(f)[None], 2, -1)
    cos, sin = np.ones((4, 32, SEQ), f), np.zeros((4, 32, SEQ), f)
    for r in range(3):
        cos[:, 8 * r:8 * r + 4] = np.cos(fr).T
        sin[:, 8 * r:8 * r + 4] = np.sin(fr).T * np.array([-1, 1, -1, 1], f)[:, None]
    out["c_cos"], out["c_sin"] = cos.reshape(128, SEQ), sin.reshape(128, SEQ)
    half = np.arange(0, DH, 2, dtype=f)
    fr = t[:, None] * (1.0 / 10000.0 ** (half / f(DH))).astype(f)[None]
    sc = (((half + f(0.4 * DH)) / f(1.4 * DH))[None] ** ((t - SEQ // 2) / f(16))[:, None]).astype(f)
    both = lambda a, sign: np.tile(np.concatenate([a * sign, a], 1), (1, 2)).T
    cos, sin = np.cos(fr).astype(f), np.sin(fr).astype(f)
    inv = (f(1.0) / sc).astype(f)
    out["c_tables"] = np.ascontiguousarray(np.stack([both(cos * sc, 1), both(sin * sc, -1), both(cos * inv, 1), both(sin * inv, -1)], 1)).astype(f)
    return out


STAGES = "norm0 attn0 ffn0 norm1 attn1 ffn1 norm2 attn2 ffn2 norm3 ffn3 attn3".split()


def kernel(**inputs):
    import concourse.bacc as _bacc
    from concourse.bass_utils import run_bass_kernel_spmd as _run

    nc = _bacc.Bacc("TRN2", target_bir_lowering=False, num_devices=1)
    arrays = {n: np.ascontiguousarray(a) for n, a in {**layouts(inputs), **constants()}.items()}
    IN = {n: nc.dram_tensor(n, a.shape, mybir.dt.from_np(a.dtype), kind="ExternalInput").ap() for n, a in arrays.items()}
    out = nc.dram_tensor("out_t", (128, TOK), F32, kind="ExternalOutput").ap()
    build(nc, IN, out, STAGES)
    r = _run(nc, [arrays], core_ids=[0])
    return np.ascontiguousarray(np.asarray(r.results[0]["out_t"]).T).reshape(16, SEQ, D)
```

```python
from contextlib import ExitStack

import numpy as np

import concourse.bass as bass
from concourse import mybir

F32 = mybir.dt.float32
BF16 = mybir.dt.bfloat16
ACT = mybir.ActivationFunctionType
ALU = mybir.AluOpType
X_AXIS = mybir.AxisListType.X
XY_AXIS = mybir.AxisListType.XY

D = 128
SEQ = 256
TOK = 16 * SEQ
GT = 512
NG = TOK // GT
NT = TOK // 128
HEADS = 16
EPS = 1e-5
LN_EXP = "natural_log_exp_and_others"
GELU = "gelu_and_others"
NEG = -1.0e30


START = 1


def at_group(g, width=GT):
    return bass.ds(g * width, width)


class Stage:

    def __init__(self, nc, name):
        self.nc, self.name, self.ctx, self.semaphores = nc, name, ExitStack(), []

    def __enter__(self):
        self.ctx.__enter__()
        return self

    def __exit__(self, *a):
        left = self.ctx.__exit__(*a)
        if a[0] is None:
            self.nc.clear_and_free_semaphores(self.semaphores)
            self.nc.all_engine_barrier()
        return left

    def sb(self, name, shape, dt=F32):
        return self.ctx.enter_context(self.nc.sbuf_tensor(f"{self.name}_{name}", shape, dt))

    def ps(self, name, shape, dt=F32):
        return self.ctx.enter_context(self.nc.psum_tensor(f"{self.name}_{name}_ps", shape, dt))

    def sems(self, names):
        new = [self.nc.alloc_semaphore(f"{self.name}_{n}") for n in names.split()]
        self.semaphores += new
        return new

    def block(self):
        for semaphore in self.semaphores:
            self.nc.gpsimd.sem_inc(semaphore, 1)
        self.nc.all_engine_barrier()
        return self.ctx.enter_context(self.nc.Block())


def load_stage(nc, R, IN):
    with Stage(nc, "load") as s:
        raw = s.sb("raw", [128, IN["c_bf"].shape[1]])
        (loaded, cast) = s.sems("loaded cast")
        block = s.block()

        @block.sync
        def _(sp):
            sp.dma_start(R["x"][:, :], IN["x_t"]).then_inc(loaded, 16)
            sp.dma_start(R["ident"][:, :], IN["c_ident"]).then_inc(loaded, 16)
            sp.dma_start(raw[:, :], IN["c_bf"]).then_inc(loaded, 16)
            sp.wait_ge(loaded, START + 48)

        @block.vector
        def _(ve):
            ve.memset(R["mean_w"][:, :], 1.0 / D).then_inc(cast, 1)
            ve.memset(R["eps"][:, :], EPS).then_inc(cast, 1)
            ve.wait_ge(loaded, START + 48)
            ve.tensor_copy(R["c_bf"][:, :], raw[:, :]).then_inc(cast, 1)
            ve.tensor_copy(R["head_ones"][:, :], raw[:, raw.shape[1] - 128:]).then_inc(cast, 1)
            ve.wait_ge(cast, START + 4)


def norm_stage(nc, R, name, again=False):
    with Stage(nc, name) as s:
        xc, sq, lnv, rstd = (s.sb(n, [128, GT]) for n in ("xc", "sq", "lnv", "rstd"))
        mean_ps, var_ps = s.ps("mean", [128, GT]), s.ps("var", [128, GT])
        mean_done, centred, squared, var_done, ln_done, rstd_done, normed = s.sems(
            "mean_done centred squared var_done ln_done rstd_done normed")
        block = s.block()
        x, xn = (R["xn"], R["xn"]) if again else (R["x"], R["xn"])

        @block.tensor
        def _(pe):
            with pe.Fori(0, NG) as g:
                pe.wait_ge(centred, START + g)
                pe.matmul(mean_ps[:, :], R["mean_w"][:, :], x[:, at_group(g)], start=True, stop=True).then_inc(mean_done, 1)
                pe.wait_ge(squared, START + g + 1)
                pe.matmul(var_ps[:, :], R["mean_w"][:, :], sq[:, :], start=True, stop=True).then_inc(var_done, 1)

        @block.scalar
        def _(act):
            act.preload_act_table_set(LN_EXP)
            with act.Fori(0, NG) as g:
                act.wait_ge(centred, START + g + 1)
                act.activation(sq[:, :], xc[:, :], ACT.Square).then_inc(squared, 1)
                act.wait_ge(var_done, START + g + 1)
                act.activation(lnv[:, :], var_ps[:, :], ACT.Ln, bias=R["eps"][:, :]).then_inc(ln_done, 1)
                act.wait_ge(ln_done, START + g + 1)
                act.wait_ge(normed, START + g)
                act.activation(rstd[:, :], lnv[:, :], ACT.Exp, scale=-0.5).then_inc(rstd_done, 1)

        @block.vector
        def _(ve):
            with ve.Fori(0, NG) as g:
                ve.wait_ge(mean_done, START + g + 1)
                ve.wait_ge(normed, START + g)
                ve.tensor_tensor(xc[:, :], x[:, at_group(g)], mean_ps[:, :], ALU.subtract).then_inc(centred, 1)
                ve.wait_ge(rstd_done, START + g + 1)
                ve.tensor_tensor(xn[:, at_group(g)], xc[:, :], rstd[:, :], ALU.mult).then_inc(normed, 1)


def attn8_stage(nc, R, name, W, scale, affine=False, rope=False, project=False, residual=False):
    R8 = 32
    with Stage(nc, name) as s:
        xs = s.sb("xs", [128, GT])
        wq, wk = s.sb("wq", [128, 4, 128]), s.sb("wk", [128, 4, 128])
        wv, vb = s.sb("wv", [128, D]), s.sb("vb", [128, D])
        qkb, low = s.sb("qkb", [128, 8]), s.sb("low", [128, 2])
        low_bias = s.sb("low_bias", [128, 8])
        high = s.sb("high", [128, 2, GT], BF16)
        qk = s.sb("qk", [128, 8, GT], BF16)
        kp = s.sb("kp", [128, 4, 4, GT], BF16)
        q2 = s.sb("q2", [128, 2, SEQ], BF16)
        v = s.sb("v", [128, 4, HEADS, 32])
        otr = s.sb("otr", [128, SEQ])
        negmax = s.sb("negmax", [128, 2, 2, 4])
        mpad = s.sb("mpad", [128, 2, 2, 4, 32], BF16)
        e = s.sb("e", [128, 2, 4, 2 * SEQ])
        rden = s.sb("rden", [128, 2, 4])
        on = s.sb("on", [128, 2, 2, D])
        ot = s.sb("ot", [128, GT])
        s_ps = s.ps("s", [128, 4, 512])
        st_ps = s.ps("st", [128, 2, 512])
        o_ps = s.ps("o", [128, 512])
        o_rows, o_toks = o_ps[:, 0:SEQ], o_ps[:, SEQ:512]
        m_ps = s.ps("m", [128, 512])
        (loaded, zeroed, xs_ready, proj_done, bias_ready, high_ready, qk_ready, v_done, v_ready, s_done, max_ready,
         mhi_ready, mpad_ready, mt_done, q2_ready, st_done, e_ready, pv_done, rden_ready, on_ready, ot_done,
         ot_ready, y_done, x_added, aux, tmp_ready, otr_ready, toks_done, kp_ready) = s.sems(
            "loaded zeroed xs_ready proj_done bias_ready high_ready qk_ready v_done v_ready s_done max_ready "
            "mhi_ready mpad_ready mt_done q2_ready st_done e_ready pv_done rden_ready on_ready ot_done "
            "ot_ready y_done x_added aux tmp_ready otr_ready toks_done kp_ready")
        n_load = 6
        if project:
            wo, wob = s.sb("wo", [128, D]), s.sb("wob", [128, 1])
            yt = s.sb("yt", [128, GT])
            n_load += 2
        if W.get("lora"):
            lora_a, lora_b = s.sb("lora_a", [8, 4, 128]), s.sb("lora_b", [8, 4, 512])
            n_load += 2
        if affine:
            gamma, beta = s.sb("gamma", [128, 1]), s.sb("beta", [128, 1])
            n_load += 2
        if rope:
            cos, sin = s.sb("cos", [128, SEQ]), s.sb("sin", [128, SEQ])
            wqr, wkr = s.sb("wqr", [128, 4, 128]), s.sb("wkr", [128, 4, 128])
            qkbr = s.sb("qkbr", [128, 8])
            t1 = s.sb("t1", [128, 2, GT])
            t2 = s.sb("t2", [128, 2, GT])
            n_load += 5
            (rot_done, t_ready, sum_ready) = s.sems("rot_done t_ready sum_ready")
        if not project:
            mix, mix_sel, mix_mask = s.sb("mix", [128, 2, HEADS, 128]), s.sb("mix_sel", [128, 8]), s.sb("mix_mask", [128, 128])
            (mix_ready, mix_ready1) = s.sems("mix_ready mix_ready1")
            n_load += 2
        block = s.block()
        ident = R["ident"]
        identb = R["ident_bf"]
        x, xn = R["x"], R["xn"]
        mt_ps = m_ps[:, :].bitcast(BF16)
        nw = 1 if W.get("lora") else 0
        turn_out_at = 6 if project else 7

        def mixed(b, t):
            return (mix[:, t, :, :].rearrange("p h (s d) -> p h s d", d=8),
                    on[:, b, t, :].rearrange("p (h d) -> p h d", h=HEADS).unsqueeze(2).to_broadcast([128, HEADS, 16, 8]),
                    mix_mask[:, :].rearrange("p (s d) -> p s d", d=8).unsqueeze(1).to_broadcast([128, HEADS, 16, 8]))

        @block.sync
        def _(sp):
            for dst, src in ((wq, W["wq"]), (wk, W["wk"])):
                sp.dma_start(dst[:, :, :], src).then_inc(loaded, 16)
            sp.dma_start(wv[:, :], W["wv"]).then_inc(loaded, 16)
            sp.dma_start(vb[:, :], W["vb"].broadcast_to([128, D])).then_inc(loaded, 16)
            sp.dma_start(qkb[:, :], W["qkb"]).then_inc(loaded, 16)
            sp.dma_start(low[:, :], W["low"]).then_inc(loaded, 16)
            if project:
                sp.dma_start(wo[:, :], W["wo"]).then_inc(loaded, 16)
                sp.dma_start(wob[:, :], W["wob"]).then_inc(loaded, 16)
            if not project:
                sp.dma_start(mix_sel[:, :], W["mix_sel"]).then_inc(loaded, 16)
                sp.dma_start(mix_mask[:, :], W["mix_mask"]).then_inc(loaded, 16)
            if W.get("lora"):
                sp.dma_start(lora_a[:, :, :], W["lora_a"]).then_inc(loaded, 16)
                sp.dma_start(lora_b[:, :, :], W["lora_b"]).then_inc(loaded, 16)
            if affine:
                sp.dma_start(gamma[:, :], W["gamma"]).then_inc(loaded, 16)
                sp.dma_start(beta[:, :], W["beta"]).then_inc(loaded, 16)
            if rope:
                sp.dma_start(cos[:, :], W["cos"]).then_inc(loaded, 16)
                sp.dma_start(sin[:, :], W["sin"]).then_inc(loaded, 16)
                sp.dma_start(wqr[:, :, :], W["wqr"]).then_inc(loaded, 16)
                sp.dma_start(wkr[:, :, :], W["wkr"]).then_inc(loaded, 16)
                sp.dma_start(qkbr[:, :], W["qkbr"]).then_inc(loaded, 16)
            sp.wait_ge(loaded, START + 16 * n_load)

        @block.tensor
        def _(pe):
            pe.wait_ge(loaded, START + 16 * n_load)
            pe.wait_ge(zeroed, START + 4)
            if W.get("lora"):
                for n in range(4):
                    width = 512 if n < 2 else 128
                    mm = pe.matmul(s_ps[:, n, 0:width], lora_a[:, n, :], lora_b[:, n, 0:width], start=True, stop=True)
                    mm.then_inc(aux, 1)
                pe.wait_ge(tmp_ready, START + 4)

            def scores(g, u):
                b, a = divmod(u, 4)
                for pair in range(2):
                    if u == 0:
                        pe.wait_ge(qk_ready, START + g * 8 + 8)
                    else:
                        pe.wait_ge(max_ready, START + g * 16 + 2 * (u - 1) + pair + 1)
                    pe.wait_ge(kp_ready, START + g * 4 + a + 1)
                    for t in range(2):
                        for j in (2 * pair, 2 * pair + 1):
                            at = b * SEQ + t * 128
                            mm = pe.matmul(s_ps[:, j, t * SEQ:(t + 1) * SEQ], qk[:, a, at:at + 128],
                                           kp[:, a, j, b * SEQ:(b + 1) * SEQ], start=True, stop=True)
                    mm.then_inc(s_done, 1)

            def values(g, u):
                b, a = divmod(u, 4)
                pe.wait_ge(on_ready, START + g * 8 + u)
                pe.wait_ge(e_ready, START + g * 32 + 4 * u + 4)
                for k in range(2):
                    for j in range(4):
                        mm = pe.matmul(o_ps[R8 * j:R8 * j + R8, 0:SEQ], v[:, 2 * b + k, 4 * a + j, :], e[:, u % 2, j, k * SEQ:(k + 1) * SEQ],
                                       start=(k == 0), stop=(k == 1))
                mm.then_inc(pv_done, 4)

            def turn_values(g, u):
                pe.wait_ge(otr_ready, START + g * 8 + u + 1)
                for t in range(2):
                    mm = pe.transpose(o_toks[:, t * 128:(t + 1) * 128], otr[:, t * 128:(t + 1) * 128], ident[:, :])
                mm.then_inc(toks_done, 1)

            def turn_max(g, u):
                pe.wait_ge(mpad_ready, START + g * 8 + u + 1)
                if u == 0:
                    pe.wait_ge(v_ready, START + g + 1)
                else:
                    pe.wait_ge(q2_ready, START + g * 8 + u)
                if u == turn_out_at + 1:
                    pe.wait_ge(x_added if not project else ot_ready, START + g * 2 + 1)
                for t in range(2):
                    mm = pe.transpose(mt_ps[:, t * 128:(t + 1) * 128],
                                      mpad[:, u % 2, t, :, :].rearrange("p j r -> p (j r)"), identb)
                mm.then_inc(mt_done, 1)

            def turned_scores(g, u, pair):
                b, a = divmod(u, 4)
                pe.wait_ge(q2_ready, START + g * 8 + u + 1)
                pe.wait_ge(e_ready, START + g * 32 + 4 * u + 2 * pair)
                for k in range(2):
                    for j in (2 * pair, 2 * pair + 1):
                        at = b * SEQ + k * 128
                        mm = pe.matmul(st_ps[:, j % 2, k * SEQ:(k + 1) * SEQ], kp[:, a, j, at:at + 128],
                                       q2[:, u % 2, :], start=True, stop=True)
                mm.then_inc(st_done, 2)

            def turn_out(g, b):
                pe.wait_ge(q2_ready, START + g * 8 + (turn_out_at + 1 if b == 0 else 8))
                if b == 1:
                    pe.wait_ge(x_added if not project else ot_ready, START + g * 2 + 1)
                if project:
                    pe.wait_ge(on_ready, START + g * 8 + 4 * b + 4)
                    for t in range(2):
                        mm = pe.transpose(m_ps[:, 256 + t * 128:384 + t * 128], on[:, b, t, :], ident[:, :])
                    mm.then_inc(ot_done, 1)
                else:
                    for t in range(2):
                        if b == 1 and t == 1:
                            pe.wait_ge(mix_ready1, START + g + 1)
                        else:
                            pe.wait_ge(mix_ready, START + g * 3 + 2 * b + t + 1)
                        for h in range(HEADS):
                            at = 256 + h * 16 + t * 8
                            mm = pe.matmul(m_ps[:, at:at + 8], mix[:, t, h, :], mix_sel[:, :], start=True, stop=True)
                    mm.then_inc(ot_done, 1)

            with pe.Fori(0, NG) as g:
                pe.wait_ge(xs_ready, START + g + 1)
                pe.wait_ge(max_ready, START + g * 16)
                for i in range(8):
                    a = i % 4
                    w = (wq if i < 4 else wk)
                    bank = i % 4 if not rope else 2 * (i % 2)
                    back = 4 if not rope else 2
                    if i >= back and rope:
                        pe.wait_ge(t_ready, START + g * 16 + 2 * (i - back) + 2)
                    elif i >= back:
                        pe.wait_ge(qk_ready, START + g * 8 + i - back + 1)
                    pe.matmul(s_ps[:, bank, :], w[:, a, :], xs[:, :], start=True, stop=True).then_inc(proj_done, 1)
                    if rope:
                        wr = (wqr if i < 4 else wkr)
                        pe.matmul(s_ps[:, bank + 1, :], wr[:, a, :], xs[:, :], start=True, stop=True).then_inc(rot_done, 1)
                pe.wait_ge(x_added if not project else ot_ready, START + g * 2)
                for t in range(4):
                    mm = pe.matmul(m_ps[:, t * D:(t + 1) * D], xs[:, t * 128:(t + 1) * 128], wv[:, :], start=True, stop=True)
                mm.then_inc(v_done, 1)
                scores(g, 0)
                turn_max(g, 0)
                for u in range(9):
                    if u < 7:
                        scores(g, u + 1)
                    if u == turn_out_at:
                        turn_out(g, 0)
                    if u < 8:
                        turned_scores(g, u, 0)
                    if u > 0:
                        values(g, u - 1)
                    if u < 8:
                        turned_scores(g, u, 1)
                    if u > 0:
                        turn_values(g, u - 1)
                    if u < 7:
                        turn_max(g, u + 1)
                turn_out(g, 1)
                if project:
                    pe.wait_ge(ot_ready, START + g * 2 + 2)
                    pe.matmul(st_ps[:, 0, :], wo[:, :], ot[:, :], start=True, stop=True).then_inc(y_done, 1)

        @block.scalar
        def _(act):
            act.preload_act_table_set(LN_EXP)
            act.wait_ge(loaded, START + 16 * n_load)
            act.wait_ge(zeroed, START + 4)
            act.wait_ge(bias_ready, START + 2)

            def exps(g, u, heads):
                for j in heads:
                    act.wait_ge(st_done, START + g * 32 + 4 * u + j // 2 * 2 + 2)
                    act.wait_ge(pv_done, START + (g * 32 + 4 * (u - 2) + j + 1 if u >= 2 else g * 32))
                    act.activation(e[:, u % 2, j, :], st_ps[:, j % 2, :], ACT.Exp, scale=scale).then_inc(e_ready, 1)

            def spread_k(g, a):
                act.wait_ge(qk_ready, START + g * 8 + 4 + a + 1)
                for j in range(4):
                    p = slice(R8 * j, R8 * j + R8)
                    last = act.activation(kp[p, a, j, :], qk[p, 4 + a, :], ACT.Copy)
                last.then_inc(kp_ready, 1)

            with act.Fori(0, NG) as g:
                act.wait_ge(v_done, START + g)
                if affine:
                    act.activation(xs[:, :], xn[:, at_group(g)], ACT.Identity, bias=beta[:, :], scale=gamma[:, :]).then_inc(xs_ready, 1)
                else:
                    act.activation(xs[:, :], xn[:, at_group(g)], ACT.Copy).then_inc(xs_ready, 1)
                for i in range(8):
                    if i >= 2:
                        act.wait_ge(qk_ready, START + g * 8 + i - 1)
                    if rope:
                        act.wait_ge(sum_ready, START + g * 8 + i + 1)
                        act.activation(high[:, i % 2, :], t1[:, i % 2, :], ACT.Copy).then_inc(high_ready, 1)
                    else:
                        act.wait_ge(proj_done, START + g * 8 + i + 1)
                        act.activation(high[:, i % 2, :], s_ps[:, i % 4, :], ACT.Identity, bias=low_bias[:, i:i + 1],
                                       scale=low[:, i // 4:i // 4 + 1]).then_inc(high_ready, 1)
                    if i >= 6:
                        spread_k(g, i - 6)
                spread_k(g, 2)
                spread_k(g, 3)
                for u in range(9):
                    if u < 8:
                        exps(g, u, (0, 1))
                    if u > 0:
                        act.wait_ge(pv_done, START + g * 32 + 4 * u)
                        act.activation(otr[:, :], o_rows, ACT.Copy).then_inc(otr_ready, 1)
                    if u < 8:
                        exps(g, u, (2, 3))

        @block.gpsimd
        def _(pool):
            pool.memset(mpad[:, :, :, :, :], 0.0).then_inc(zeroed, 1)
            pool.memset(v[:, :, :, :], 0.0).then_inc(zeroed, 1)
            pool.memset(kp[:, :, :, :], 0.0).then_inc(zeroed, 1)
            pool.wait_ge(zeroed, START + 3)
            pool.memset(v[:, :, :, 8:16], 1.0).then_inc(zeroed, 1)
            if not rope and project:
                return
            with pool.Fori(0, NG) as g:
                if rope:
                    for i in range(8):
                        pool.wait_ge(t_ready, START + g * 16 + 2 * i + 2)
                        pool.tensor_tensor(t1[:, i % 2, :], t1[:, i % 2, :], t2[:, i % 2, :], ALU.add).then_inc(sum_ready, 1)
                if not project:
                    for b in range(2):
                        pool.wait_ge(on_ready, START + g * 8 + 4 * b + 4)
                        pool.wait_ge(ot_done, START + g * 2 + b)
                        for t in range(2 - b):
                            pool.tensor_tensor(*mixed(b, t), ALU.mult).then_inc(mix_ready, 1)

        @block.vector
        def _(ve):
            ve.wait_ge(loaded, START + 16 * n_load)
            ve.wait_ge(zeroed, START + 4)
            for k in range(2):
                ve.tensor_tensor(low_bias[:, 4 * k:4 * k + 4], qkb[:, 4 * k:4 * k + 4], low[:, k:k + 1].to_broadcast([128, 4]), ALU.mult).then_inc(bias_ready, 1)
            if W.get("lora"):
                for n, w in enumerate((wq, wk, wv, wo)):
                    view = w[:, :, :].rearrange("p a c -> p (a c)") if n < 2 else w[:, :]
                    ve.wait_ge(aux, START + n + 1)
                    ve.scalar_tensor_tensor(view, s_ps[:, n, 0:512 if n < 2 else 128], 2.0, view, ALU.mult, ALU.add).then_inc(tmp_ready, 1)
            two = lambda ap: ap.rearrange("p (b t) -> p b t", b=2)

            def pair_maxima(g, u, pair):
                ve.wait_ge(s_done, START + g * 16 + 2 * u + pair + 1)
                src = s_ps[:, 2 * pair:2 * pair + 2, :].rearrange("p j (t k) -> p j t k", t=2)
                dst = negmax[:, u % 2, :, 2 * pair:2 * pair + 2].rearrange("p t j -> p j t")
                ve.tensor_reduce(dst, src, X_AXIS, ALU.max, negate=True).then_inc(max_ready, 1)

            def split_maxima(g, u):
                ve.wait_ge(max_ready, START + g * 16 + 2 * u + 2)
                if u >= 2:
                    ve.wait_ge(mt_done, START + g * 8 + u - 1)
                ve.tensor_copy(mpad[:, u % 2, :, :, 24], negmax[:, u % 2, :, :]).then_inc(mhi_ready, 1)
                ve.wait_ge(mhi_ready, START + g * 8 + u + 1)
                ve.tensor_tensor(mpad[:, u % 2, :, :, 25], negmax[:, u % 2, :, :], mpad[:, u % 2, :, :, 24], ALU.subtract).then_inc(mpad_ready, 1)

            def split(g, i):
                ve.wait_ge(high_ready, START + g * 8 + i + 1)
                if rope:
                    ve.scalar_tensor_tensor(qk[:, i, :], high[:, i % 2, :], low[:, i // 4:i // 4 + 1], t1[:, i % 2, :],
                                            ALU.mult, ALU.add).then_inc(qk_ready, 1)
                else:
                    ve.scalar_tensor_tensor(qk[:, i, :], s_ps[:, i % 4, :], qkb[:, i:i + 1], high[:, i % 2, :],
                                            ALU.add, ALU.add).then_inc(qk_ready, 1)

            def normalise(g, u):
                b, a = divmod(u, 4)
                ve.wait_ge(toks_done, START + g * 8 + u + 1)
                toks = o_toks.rearrange("p (t j c) -> p t j c", t=2, j=4)
                ve.reciprocal(rden[:, :, :], toks[:, :, :, 8]).then_inc(rden_ready, 1)
                ve.wait_ge(rden_ready, START + g * 8 + u + 1)
                for t in range(2):
                    nn = ve.tensor_tensor(on[:, b, t, a * 32:(a + 1) * 32].rearrange("p (j d) -> p j d", j=4), toks[:, t, :, 0:8],
                                          rden[:, t, :].unsqueeze(2).to_broadcast([128, 4, 8]), ALU.mult)
                nn.then_inc(on_ready, 1)

            def keep_out(g, b):
                ve.wait_ge(ot_done, START + g * 2 + b + 1)
                if project:
                    ve.tensor_copy(ot[:, b * SEQ:(b + 1) * SEQ], m_ps[:, 256:512]).then_inc(ot_ready, 1)
                else:
                    xa = x[:, bass.ds(g * GT + b * SEQ, SEQ)]
                    ve.tensor_tensor(xa, xa, m_ps[:, 256:512], ALU.add).then_inc(x_added, 1)

            with ve.Fori(0, NG) as g:
                for i in range(8):
                    if rope:
                        if i >= 2:
                            ve.wait_ge(qk_ready, START + g * 8 + i - 1)
                        tab = lambda t: t[:, :].unsqueeze(1).to_broadcast([128, 2, SEQ])
                        bank = 2 * (i % 2)
                        ve.wait_ge(proj_done, START + g * 8 + i + 1)
                        ve.scalar_tensor_tensor(two(t1[:, i % 2, :]), two(s_ps[:, bank, :]), qkb[:, i:i + 1], tab(cos), ALU.add, ALU.mult).then_inc(t_ready, 1)
                        ve.wait_ge(rot_done, START + g * 8 + i + 1)
                        ve.scalar_tensor_tensor(two(t2[:, i % 2, :]), two(s_ps[:, bank + 1, :]), qkbr[:, i:i + 1], tab(sin), ALU.add, ALU.mult).then_inc(t_ready, 1)
                        if i >= 1:
                            split(g, i - 1)
                    else:
                        split(g, i)
                if rope:
                    split(g, 7)
                ve.wait_ge(v_done, START + g + 1)
                vbb = vb[:, :].rearrange("p (h d) -> p h d", h=HEADS)
                for t in range(4):
                    vv = ve.tensor_tensor(v[:, t, :, 0:8], m_ps[:, t * D:(t + 1) * D].rearrange("p (h d) -> p h d", h=HEADS), vbb, ALU.add)
                vv.then_inc(v_ready, 1)
                pair_maxima(g, 0, 0)
                pair_maxima(g, 0, 1)
                split_maxima(g, 0)
                for u in range(9):
                    if u < 8:
                        ve.wait_ge(mt_done, START + g * 8 + u + 1)
                        if u >= 2:
                            ve.wait_ge(st_done, START + g * 32 + 4 * u - 4)
                        a = u % 4
                        ve.tensor_tensor(q2[:, u % 2, :], qk[:, a, (u // 4) * SEQ:(u // 4 + 1) * SEQ], mt_ps[:, 0:SEQ], ALU.add).then_inc(q2_ready, 1)
                    if u < 7:
                        pair_maxima(g, u + 1, 0)
                        pair_maxima(g, u + 1, 1)
                        split_maxima(g, u + 1)
                    if 0 < u < 8:
                        normalise(g, u - 1)
                    if u == turn_out_at:
                        keep_out(g, 0)
                normalise(g, 7)
                if not project:
                    ve.wait_ge(on_ready, START + g * 8 + 8)
                    ve.tensor_tensor(*mixed(1, 1), ALU.mult).then_inc(mix_ready1, 1)
                keep_out(g, 1)
                if project:
                    ve.wait_ge(y_done, START + g + 1)
                    ve.tensor_scalar(yt[:, :], st_ps[:, 0, :], wob[:, 0:1], None, ALU.add).then_inc(aux, 1)
                    ve.wait_ge(aux, START + g + 1 + 4 * nw)
                    ve.tensor_tensor(x[:, at_group(g)], x[:, at_group(g)], yt[:, :], ALU.add).then_inc(x_added, 1)
                    if residual:
                        ve.wait_ge(x_added, START + g * 2 + 1)
                        ve.tensor_tensor(x[:, at_group(g)], x[:, at_group(g)], xn[:, at_group(g)], ALU.add).then_inc(x_added, 1)


DH = 64
NB = HEADS * DH // 128


class Geometry:

    def __init__(self, R, band):
        m = R["masks"]
        if band:
            self.first_key, self.q1_from = 96, 0
            self.mask_q0, self.mask_q1 = m["band"], m["band_q1"]
        else:
            self.first_key, self.q1_from = 0, 128
            self.mask_q0 = self.mask_q1 = m["causal"]
        self.n_q1 = 256 - self.first_key


def attn64_core(nc, R, T, geo, sem):
    qt, kt, v, negmax, e, et, den, rden, ot = (T[n] for n in ("qt", "kt", "v", "negmax", "e", "et", "den", "rden", "ot"))
    s_ps, et_ps, o_ps = T["s_ps"], T["st_ps"], T["o_ps"]
    ident_bf, ident = R["ident_bf"], R["ident"]
    NU = 16

    class Core:
        @staticmethod
        def scores(pe, n, u):
            i, b = divmod(u, 2)
            slot = u % 2
            if u >= 2:
                pe.wait_ge(sem["e_ready"], START + n * NU + u - 1)
            for p in range(2):
                bank = 2 * slot + p
                pe.matmul(s_ps[:, bank, 0:128], qt[:, i, b * SEQ:b * SEQ + 128],
                          kt[:, i, p, b * SEQ:b * SEQ + 128], start=True, stop=False)
                pe.matmul(s_ps[:, bank, 0:128], ident_bf, geo.mask_q0, start=False, stop=True)
                lo, hi = 128, 128 + geo.n_q1
                pe.matmul(s_ps[:, bank, lo:hi], qt[:, i, b * SEQ + 128:b * SEQ + SEQ],
                          kt[:, i, p, b * SEQ + geo.first_key:(b + 1) * SEQ], start=True, stop=False)
                mm = pe.matmul(s_ps[:, bank, lo + geo.q1_from:hi], ident_bf, geo.mask_q1, start=False, stop=True)
            mm.then_inc(sem["s_done"], 1)

        @staticmethod
        def turn_probs(pe, n, u):
            pe.wait_ge(sem["probs_ready"], START + n * NU + u + 1)
            for p in range(2):
                if u >= 1:
                    pe.wait_ge(sem["et_ready0" if p == 0 else "et_ready1"], START + n * NU + u)
                for k in range(3):
                    mm = pe.transpose(et_ps[:, p, k * 128:(k + 1) * 128], e[:, u % 2, p, k * 128:(k + 1) * 128], ident[:, :])
            mm.then_inc(sem["et_done"], 1)

        @staticmethod
        def values(pe, n, u):
            i, b = divmod(u, 2)
            if b == 0:
                pe.wait_ge(sem["ot_ready"], START + n * NB + i)
            for p in range(2):
                pe.wait_ge(sem["et_ready0" if p == 0 else "et_ready1"], START + n * NU + u + 1)
                h = 2 * i + p
                out = lambda t: o_ps[64 * p:64 * p + 64, 0, b * SEQ + t * 128:b * SEQ + (t + 1) * 128]
                w = lambda k: et[:, u % 2, p, k * 128:(k + 1) * 128]
                pe.matmul(out(0), v[:, 2 * b, h, :], w(0), start=True, stop=True)
                pe.matmul(out(1), v[:, 2 * b, h, :], w(1), start=True, stop=False)
                mm = pe.matmul(out(1), v[:, 2 * b + 1, h, :], w(2), start=False, stop=True)
            mm.then_inc(sem["pv_done"], 1)

        @staticmethod
        def project(pe, n, i, wo):
            pe.wait_ge(sem["ot_ready"], START + n * NB + i + 1)
            mm = pe.matmul(o_ps[:, 1, :], wo[:, i * 128:(i + 1) * 128], ot[:, i % 2, :], start=(i == 0), stop=(i == NB - 1))
            mm.then_inc(sem["ot_used"], 1)

        @staticmethod
        def exps(act, n, u):
            slot = u % 2
            act.wait_ge(sem["max_ready"], START + n * NU + u + 1)
            if u >= 2:
                act.wait_ge(sem["et_done"], START + n * NU + u - 1)
            for p in range(2):
                bank = 2 * slot + p
                act.activation(e[:, slot, p, 0:128], s_ps[:, bank, 0:128], ACT.Exp, bias=negmax[:, slot, 0, p:p + 1],
                               accum_out=den[:, slot, p, 0:1])
                last = act.activation(e[:, slot, p, 128 + geo.first_key:384], s_ps[:, bank, 128:128 + geo.n_q1], ACT.Exp,
                                      bias=negmax[:, slot, 1, p:p + 1], accum_out=den[:, slot, p, 1:2])
            last.then_inc(sem["e_ready"], 1)

        @staticmethod
        def keep_probs0(act, n, u):
            act.wait_ge(sem["et_done"], START + n * NU + u + 1)
            if u >= 2:
                act.wait_ge(sem["pv_done"], START + n * NU + u - 1)
            act.activation(et[:, u % 2, 0, :], et_ps[:, 0, 0:384], ACT.Copy).then_inc(sem["et_ready0"], 1)

        @staticmethod
        def keep_probs1(ve, n, u):
            ve.wait_ge(sem["et_done"], START + n * NU + u + 1)
            if u >= 2:
                ve.wait_ge(sem["pv_done"], START + n * NU + u - 1)
            ve.tensor_copy(et[:, u % 2, 1, :], et_ps[:, 1, 0:384]).then_inc(sem["et_ready1"], 1)

        @staticmethod
        def maxima(ve, n, u):
            slot = u % 2
            ve.wait_ge(sem["s_done"], START + n * NU + u + 1)
            banks = s_ps[:, 2 * slot:2 * slot + 2, :]
            ve.tensor_reduce(negmax[:, slot, 0, :], banks[:, :, 0:128], X_AXIS, ALU.max, negate=True)
            ve.tensor_reduce(negmax[:, slot, 1, :], banks[:, :, 128:128 + geo.n_q1], X_AXIS, ALU.max, negate=True).then_inc(sem["max_ready"], 1)

        @staticmethod
        def invert(ve, n, u):
            slot = u % 2
            ve.wait_ge(sem["e_ready"], START + n * NU + u + 1)
            ve.reciprocal(rden[:, slot, :, 0:2], den[:, slot, :, :])
            ve.reciprocal(rden[:, slot, :, 2], den[:, slot, :, 1]).then_inc(sem["rden_ready"], 1)

        @staticmethod
        def normalise(pool, n, u):
            slot = u % 2
            pool.wait_ge(sem["rden_ready"], START + n * NU + u + 1)
            tiles = e[:, slot, :, :].rearrange("q p (k c) -> q p k c", k=3)
            pool.tensor_tensor(tiles, tiles, rden[:, slot, :, :].unsqueeze(3).to_broadcast([128, 2, 3, 128]), ALU.mult).then_inc(sem["probs_ready"], 1)

        @staticmethod
        def keep_out(ve, n, i):
            ve.wait_ge(sem["pv_done"], START + n * NU + 2 * i + 2)
            if i >= 2:
                ve.wait_ge(sem["ot_used"], START + n * NB + i - 1)
            ve.tensor_copy(ot[:, i % 2, :], o_ps[:, 0, :]).then_inc(sem["ot_ready"], 1)

        @staticmethod
        def attend(pe, n, u, wo, scores):
            if u < NU:
                Core.turn_probs(pe, n, u)
            if u < NU - 2:
                scores(pe, n, u + 2)
            if u % 2 == 1 and u >= 3:
                Core.project(pe, n, (u - 3) // 2, wo)
            if u > 0:
                Core.values(pe, n, u - 1)

    return Core


CORE_SEMS = "max_ready s_done e_ready rden_ready probs_ready et_done et_ready0 et_ready1 pv_done ot_ready ot_used".split()


def named(s, names):
    return dict(zip(names, s.sems(" ".join(names))))


def attn64_tiles(s):
    return {
        "qt": s.sb("qt", [128, NB, GT]), "kt": s.sb("kt", [128, NB, 2, GT]),
        "v": s.sb("v", [128, 4, HEADS, DH]),
        "negmax": s.sb("negmax", [128, 2, 2, 2]), "e": s.sb("e", [128, 2, 2, 384]), "et": s.sb("et", [128, 2, 2, 384]),
        "den": s.sb("den", [128, 2, 2, 2]), "rden": s.sb("rden", [128, 2, 2, 3]), "ot": s.sb("ot", [128, 2, GT]),
        "s_ps": s.ps("s", [128, 4, 512]), "st_ps": s.ps("st", [128, 2, 512]), "o_ps": s.ps("o", [128, 2, 512]),
    }


def attn64_stage(nc, R, name, W, scale):
    with Stage(nc, name) as s:
        T = attn64_tiles(s)
        xs = s.sb("xs", [128, GT])
        wq, wk, wv, wo = (s.sb(n, [128, HEADS * DH]) for n in ("wq", "wk", "wv", "wo"))
        geo = Geometry(R, band=False)
        sem = named(s, CORE_SEMS + ["loaded", "zeroed", "xs_ready", "proj_done", "proj_ready", "v_done", "v_ready", "x_added"])
        core = attn64_core(nc, R, T, geo, sem)
        block = s.block()
        x, xn = R["x"], R["xn"]
        qt, kt, v = T["qt"], T["kt"], T["v"]
        s_ps, o_ps = T["s_ps"], T["o_ps"]

        @block.sync
        def _(sp):
            for dst, src in ((wq, "wq"), (wk, "wk"), (wv, "wv"), (wo, "wo")):
                sp.dma_start(dst[:, :], W[src]).then_inc(sem["loaded"], 16)
            sp.wait_ge(sem["loaded"], START + 64)

        @block.tensor
        def _(pe):
            pe.wait_ge(sem["loaded"], START + 64)
            pe.wait_ge(sem["zeroed"], START + 2)
            with pe.Fori(0, NG) as g:
                pe.wait_ge(sem["xs_ready"], START + g + 1)
                pe.wait_ge(sem["ot_ready"], START + g * NB)
                for i in range(16):
                    w, c = (wq, i) if i < NB else (wk, i - NB)
                    if i >= 4:
                        pe.wait_ge(sem["proj_ready"], START + g * 16 + i - 3)
                    pe.matmul(s_ps[:, i % 4, :], w[:, c * 128:(c + 1) * 128], xs[:, :], start=True, stop=True).then_inc(sem["proj_done"], 1)
                pe.wait_ge(sem["proj_ready"], START + g * 16 + 16)
                core.scores(pe, g, 0)
                core.scores(pe, g, 1)
                for i in range(8):
                    t, half = divmod(i, 2)
                    pe.wait_ge(sem["v_ready"], START + (g * 8 + i - 1 if i >= 2 else g * 8))
                    if i == 0:
                        pe.wait_ge(sem["x_added"], START + g)
                    pe.matmul(o_ps[:, half, :], xs[:, t * 128:(t + 1) * 128], wv[:, half * 512:(half + 1) * 512], start=True, stop=True).then_inc(sem["v_done"], 1)
                for u in range(17):
                    if u == 1:
                        pe.wait_ge(sem["v_ready"], START + g * 8 + 8)
                    core.attend(pe, g, u, wo, core.scores)
                core.project(pe, g, NB - 1, wo)

        @block.scalar
        def _(act):
            act.preload_act_table_set(LN_EXP)
            with act.Fori(0, NG) as g:
                act.wait_ge(sem["v_done"], START + g * 8)
                act.activation(xs[:, :], xn[:, at_group(g)], ACT.Copy).then_inc(sem["xs_ready"], 1)
                for i in range(16):
                    act.wait_ge(sem["proj_done"], START + g * 16 + i + 1)
                    if i < NB:
                        act.activation(qt[:, i, :], s_ps[:, i % 4, :], ACT.Copy, scale=scale).then_inc(sem["proj_ready"], 1)
                    else:
                        act.activation(kt[0:64, i - NB, 0, :], s_ps[0:64, i % 4, :], ACT.Copy)
                        act.activation(kt[64:128, i - NB, 1, :], s_ps[64:128, i % 4, :], ACT.Copy).then_inc(sem["proj_ready"], 1)
                core.exps(act, g, 0)
                core.exps(act, g, 1)
                for u in range(16):
                    core.keep_probs0(act, g, u)
                    if u < 14:
                        core.exps(act, g, u + 2)

        @block.gpsimd
        def _(pool):
            pool.memset(T["e"][:, :, :, :], 0.0).then_inc(sem["zeroed"], 1)
            pool.memset(kt[:, :, :, :], 0.0).then_inc(sem["zeroed"], 1)
            pool.wait_ge(sem["zeroed"], START + 2)
            with pool.Fori(0, NG) as g:
                for u in range(16):
                    core.normalise(pool, g, u)

        @block.vector
        def _(ve):
            ve.wait_ge(sem["zeroed"], START + 2)
            with ve.Fori(0, NG) as g:
                core.maxima(ve, g, 0)
                for i in range(8):
                    t, half = divmod(i, 2)
                    if i == 2:
                        core.maxima(ve, g, 1)
                    if i == 5:
                        core.invert(ve, g, 0)
                    ve.wait_ge(sem["v_done"], START + g * 8 + i + 1)
                    ve.tensor_copy(v[:, t, 8 * half:8 * half + 8, :], o_ps[:, half, :].rearrange("p (h d) -> p h d", h=8)).then_inc(sem["v_ready"], 1)
                for u in range(16):
                    if u % 2 == 1 and u >= 3:
                        core.keep_out(ve, g, (u - 3) // 2)
                    if u < 15:
                        core.invert(ve, g, u + 1)
                    core.keep_probs1(ve, g, u)
                    if u < 14:
                        core.maxima(ve, g, u + 2)
                core.keep_out(ve, g, NB - 1)
                ve.wait_ge(sem["ot_used"], START + g * NB + NB)
                ve.tensor_tensor(x[:, at_group(g)], x[:, at_group(g)], o_ps[:, 1, :], ALU.add).then_inc(sem["x_added"], 1)


def gate_stage(nc, R, name, W, capacity):
    NE = 8
    with Stage(nc, name) as s:
        wg, bias = s.sb("wg", [128, NE]), s.sb("bias", [128, NE])
        p_, sc, t_ = (s.sb(n, [128, NT, NE]) for n in ("p", "sc", "t"))
        oh = [s.sb(f"oh{k}", [128, NT, NE]) for k in range(2)]
        red, w_, sm, rk = (s.sb(n, [128, 2, NT]) for n in ("red", "w", "sm", "rk"))
        first = s.sb("first", [128, NE])
        lg = s.ps("lg", [128, NT * NE])
        loaded, gates_done, dv, exp_ready, cum_done = s.sems("loaded gates_done dv exp_ready cum_done")
        if capacity:
            ohb = s.sb("ohb", [128, NT, 2, NE], BF16)
            cum = [s.sb(f"cum{i}", [128, NT, 2, NE]) for i in range(2)]
            rank = s.sb("rank", [128, NT, 2, NE])
            cum_ps, tot_ps = s.ps("cumps", [128, NT * 2 * NE]), s.ps("totps", [128, NT * 2 * NE])
        block = s.block()
        comb = R["comb"]
        bc = lambda t: t.unsqueeze(2).to_broadcast([128, NT, NE])
        bt = lambda t: t.unsqueeze(1).to_broadcast([128, NT, NE])

        @block.sync
        def _(sp):
            sp.dma_start(wg[:, :], W["wg"]).then_inc(loaded, 16)
            if not capacity:
                sp.dma_start(bias[:, :], W["bg"].broadcast_to([128, NE])).then_inc(loaded, 16)
            sp.wait_ge(loaded, START + (16 if capacity else 32))

        @block.tensor
        def _(pe):
            pe.wait_ge(loaded, START + (16 if capacity else 32))
            for t in range(NT):
                mm = pe.matmul(lg[:, t * NE:(t + 1) * NE], R["xn"][:, t * 128:(t + 1) * 128], wg[:, :], start=True, stop=True)
            mm.then_inc(gates_done, 1)
            if capacity:
                pe.wait_ge(cum_done, START + 1)
                flat = ohb[:, :, :, :].rearrange("p t k e -> p (t k e)")
                pe.matmul(cum_ps[:, :], R["upper_bf"], flat, start=True, stop=True)
                pe.matmul(tot_ps[:, :], R["ones_bf"], flat, start=True, stop=True).then_inc(cum_done, 1)

        @block.scalar
        def _(act):
            act.preload_act_table_set(LN_EXP)
            act.wait_ge(dv, START + 4)
            act.activation(p_[:, :, :], sc[:, :, :], ACT.Exp).then_inc(exp_ready, 1)

        @block.gpsimd
        def _(pool):
            pass

        @block.vector
        def _(ve):
            step = [0]

            def done(ins):
                step[0] += 1
                ins.then_inc(dv, 1)
                ve.wait_ge(dv, START + step[0])

            logits = lg[:, :].rearrange("p (t e) -> p t e", e=NE)
            done(ve.tensor_copy(first[:, :], R["first"]))
            ve.wait_ge(gates_done, START + 1)
            if not capacity:
                ve.wait_ge(loaded, START + 32)
                done(ve.tensor_tensor(t_[:, :, :], logits, bt(bias[:, :]), ALU.add))
            else:
                done(ve.tensor_copy(t_[:, :, :], logits))
            done(ve.tensor_reduce(red[:, 0, :], t_[:, :, :], X_AXIS, ALU.max))
            done(ve.tensor_tensor(sc[:, :, :], t_[:, :, :], bc(red[:, 0, :]), ALU.subtract))
            ve.wait_ge(exp_ready, START + 1)
            done(ve.tensor_reduce(red[:, 0, :], p_[:, :, :], X_AXIS, ALU.add))
            done(ve.reciprocal(red[:, 1, :], red[:, 0, :]))
            done(ve.tensor_tensor(p_[:, :, :], p_[:, :, :], bc(red[:, 1, :]), ALU.mult))
            done(ve.tensor_copy(sc[:, :, :], p_[:, :, :]))
            for k in range(2):
                done(ve.tensor_reduce(w_[:, k, :], sc[:, :, :], X_AXIS, ALU.max))
                done(ve.tensor_tensor(t_[:, :, :], sc[:, :, :], bc(w_[:, k, :]), ALU.is_equal))
                done(ve.tensor_tensor(t_[:, :, :], t_[:, :, :], bt(first[:, :]), ALU.mult))
                done(ve.tensor_reduce(red[:, 0, :], t_[:, :, :], X_AXIS, ALU.max))
                done(ve.tensor_tensor(oh[k][:, :, :], bt(first[:, :]), bc(red[:, 0, :]), ALU.is_equal))
                if k == 0:
                    done(ve.scalar_tensor_tensor(sc[:, :, :], oh[0][:, :, :], -2.0, sc[:, :, :], ALU.mult, ALU.add))
            if capacity:
                done(ve.tensor_tensor(sm[:, 0, :], w_[:, 0, :], w_[:, 1, :], ALU.add))
                done(ve.tensor_scalar(sm[:, 0, :], sm[:, 0, :], 1e-9, None, ALU.add))
                done(ve.reciprocal(sm[:, 1, :], sm[:, 0, :]))
                for k in range(2):
                    done(ve.tensor_tensor(w_[:, k, :], w_[:, k, :], sm[:, 1, :], ALU.mult))
                    done(ve.tensor_copy(ohb[:, :, k, :], oh[k][:, :, :]))
                ve.tensor_copy(sm[:, 0, :], w_[:, 0, :]).then_inc(cum_done, 1)
                ve.wait_ge(cum_done, START + 2)
                v4 = lambda ps: ps[:, :].rearrange("p (t k e) -> p t k e", k=2, e=NE)
                done(ve.memset(cum[0][:, 0:1, :, :], 0.0))
                done(ve.tensor_copy(cum[0][:, 1:NT, :, :], v4(tot_ps)[:, 0:NT - 1]))
                at, d = 0, 1
                while d < NT:
                    a, b = cum[at], cum[1 - at]
                    done(ve.tensor_copy(b[:, 0:d, :, :], a[:, 0:d, :, :]))
                    done(ve.tensor_tensor(b[:, d:NT, :, :], a[:, d:NT, :, :], a[:, 0:NT - d, :, :], ALU.add))
                    at, d = 1 - at, 2 * d
                done(ve.tensor_tensor(rank[:, :, :, :], cum[at][:, :, :, :], v4(cum_ps), ALU.add))
                done(ve.tensor_tensor(rank[:, :, :, :], rank[:, :, :, :], ohb[:, :, :, :], ALU.mult))
                for k in range(2):
                    done(ve.tensor_reduce(rk[:, k, :], rank[:, :, k, :], X_AXIS, ALU.add))
                    done(ve.tensor_scalar(rk[:, k, :], rk[:, k, :], float(capacity) + 0.5, None, ALU.is_lt))
                    done(ve.tensor_tensor(w_[:, k, :], w_[:, k, :], rk[:, k, :], ALU.mult))
            done(ve.tensor_tensor(t_[:, :, :], oh[0][:, :, :], bc(w_[:, 0, :]), ALU.mult))
            done(ve.tensor_tensor(sc[:, :, :], oh[1][:, :, :], bc(w_[:, 1, :]), ALU.mult))
            done(ve.tensor_tensor(comb[:, :, :], t_[:, :, :], sc[:, :, :], ALU.add))


def experts_stage(nc, R, name, W, gated):
    NE = 8
    with Stage(nc, name) as s:
        HB = 2 if gated else 4
        xs = s.sb("xs", [128, GT])
        w1 = s.sb("w1", [128, NE, 512])
        w2 = s.sb("w2", [128, NE, HB, D])
        h = s.sb("h", [128, 2, HB, GT])
        cs = s.sb("cs", [128, 4, NE])
        acc = s.sb("acc", [128, 4, D])
        h_ps, y_ps = s.ps("h", [128, 4, 512]), s.ps("y", [128, 2, 512])
        i_ps, f_ps = s.ps("i", [128, 512]), s.ps("f", [128, 512])
        (loaded, xs_ready, cs_ready, h_done, h_ready, y_done, acc_step, f_done, x_added, init_done, ct_ready, ct_done, sg_ready) = s.sems(
            "loaded xs_ready cs_ready h_done h_ready y_done acc_step f_done x_added init_done ct_ready ct_done sg_ready")
        n_load = 2
        if gated:
            sg = s.sb("sg", [128, 2, 2, GT])
        else:
            b1, b2, ct = s.sb("b1", [128, NE, 4]), s.sb("b2", [NE, D]), s.sb("ct", [NE, GT])
            n_load = 4
        block = s.block()
        x, xn, comb, ident = R["x"], R["xn"], R["comb"], R["ident"]

        @block.sync
        def _(sp):
            sp.dma_start(w1[:, :, :], W["w1"]).then_inc(loaded, 16)
            sp.dma_start(w2[:, :, :, :], W["w2"]).then_inc(loaded, 16)
            if not gated:
                sp.dma_start(b1[:, :, :], W["b1"]).then_inc(loaded, 16)
                sp.dma_start(b2[:, :], W["b2"]).then_inc(loaded, 16)
            sp.wait_ge(loaded, START + 16 * n_load)

        @block.tensor
        def _(pe):
            pe.wait_ge(loaded, START + 16 * n_load)

            def hidden(g, ex):
                for i in range(4):
                    n = 4 * ex + i
                    if n >= 4:
                        pe.wait_ge(h_ready, START + g * 32 + n - 3)
                    else:
                        pe.wait_ge(h_ready, START + g * 32)
                    pe.matmul(h_ps[:, i, :], w1[:, ex, i * 128:(i + 1) * 128], xs[:, :], start=True, stop=True).then_inc(h_done, 1)

            def down(g, ex):
                pe.wait_ge(h_ready, START + g * 32 + 4 * ex + 4)
                if ex >= 2:
                    pe.wait_ge(acc_step, START + g * 9 + ex)
                else:
                    pe.wait_ge(acc_step, START + g * 9)
                for t in range(4):
                    for c in range(HB):
                        mm = pe.matmul(y_ps[:, ex % 2, t * D:(t + 1) * D], h[:, ex % 2, c, t * 128:(t + 1) * 128],
                                       w2[:, ex, c, :], start=(c == 0), stop=(c == HB - 1))
                mm.then_inc(y_done, 1)

            with pe.Fori(0, NG) as g:
                pe.wait_ge(xs_ready, START + g + 1)
                pe.wait_ge(cs_ready, START + g + 1)
                if not gated:
                    for t in range(4):
                        mm = pe.transpose(i_ps[0:NE, t * 128:(t + 1) * 128], cs[:, t, :], ident[:, :])
                    mm.then_inc(ct_done, 1)
                    pe.wait_ge(ct_ready, START + g + 1)
                    for t in range(4):
                        mm = pe.matmul(i_ps[:, t * D:(t + 1) * D], ct[:, t * 128:(t + 1) * 128], b2[:, :], start=True, stop=True)
                    mm.then_inc(init_done, 1)
                hidden(g, 0)
                for ex in range(NE):
                    if ex < NE - 1:
                        hidden(g, ex + 1)
                    down(g, ex)
                pe.wait_ge(acc_step, START + g * 9 + 9)
                for t in range(4):
                    mm = pe.transpose(f_ps[:, t * 128:(t + 1) * 128], acc[:, t, :], ident[:, :])
                mm.then_inc(f_done, 1)

        @block.scalar
        def _(act):
            act.wait_ge(loaded, START + 16 * n_load)
            with act.Fori(0, NG) as g:
                act.wait_ge(h_done, START + g * 32)
                act.activation(xs[:, :], xn[:, at_group(g)], ACT.Copy).then_inc(xs_ready, 1)
                for ex in range(NE):
                    if gated:
                        act.wait_ge(h_ready, START + (g * 32 + 4 * (ex - 1) if ex >= 2 else g * 32))
                    else:
                        act.wait_ge(y_done, START + (g * 8 + ex - 1 if ex >= 2 else g * 8))
                    if gated:
                        for i in range(2):
                            act.wait_ge(h_done, START + g * 32 + 4 * ex + 2 * i + 1)
                            act.activation(sg[:, ex % 2, i, :], h_ps[:, 2 * i, :], ACT.Silu).then_inc(sg_ready, 1)
                    else:
                        for i in range(4):
                            act.wait_ge(h_done, START + g * 32 + 4 * ex + i + 1)
                            act.activation(h[:, ex % 2, i, :], h_ps[:, i, :], ACT.Relu, bias=b1[:, ex, i:i + 1]).then_inc(h_ready, 1)

        @block.gpsimd
        def _(pool):
            pass

        @block.vector
        def _(ve):
            with ve.Fori(0, NG) as g:
                if not gated:
                    ve.wait_ge(ct_done, START + g)
                ve.wait_ge(acc_step, START + g * 9)
                ve.tensor_copy(cs[:, :, :], comb[:, bass.ds(g * 4, 4), :]).then_inc(cs_ready, 1)
                ve.wait_ge(cs_ready, START + g + 1)
                if gated:
                    ve.wait_ge(f_done, START + g)
                    ve.memset(acc[:, :, :], 0.0).then_inc(acc_step, 1)
                else:
                    ve.wait_ge(ct_done, START + g + 1)
                    ve.tensor_copy(ct[:, :], i_ps[0:NE, :]).then_inc(ct_ready, 1)
                    ve.wait_ge(init_done, START + g + 1)
                    ve.wait_ge(f_done, START + g)
                    ve.tensor_copy(acc[:, :, :], i_ps[:, :].rearrange("p (t d) -> p t d", t=4)).then_inc(acc_step, 1)

                def product(ex):
                    for i in range(2):
                        ve.wait_ge(h_done, START + g * 32 + 4 * ex + 2 * i + 2)
                        ve.wait_ge(sg_ready, START + g * 16 + 2 * ex + i + 1)
                        ve.tensor_tensor(h[:, ex % 2, i, :], sg[:, ex % 2, i, :], h_ps[:, 2 * i + 1, :], ALU.mult).then_inc(h_ready, 2)

                if gated:
                    product(0)
                for ex in range(NE):
                    if gated and ex < NE - 1:
                        if ex >= 1:
                            ve.wait_ge(y_done, START + g * 8 + ex)
                        product(ex + 1)
                    ve.wait_ge(y_done, START + g * 8 + ex + 1)
                    ve.wait_ge(acc_step, START + g * 9 + ex + 1)
                    for t in range(4):
                        a = ve.scalar_tensor_tensor(acc[:, t, :], y_ps[:, ex % 2, t * D:(t + 1) * D], cs[:, t, ex:ex + 1],
                                                    acc[:, t, :], ALU.mult, ALU.add)
                    a.then_inc(acc_step, 1)
                ve.wait_ge(f_done, START + g + 1)
                ve.tensor_tensor(x[:, at_group(g)], x[:, at_group(g)], f_ps[:, :], ALU.add).then_inc(x_added, 1)


def binary_stage(nc, R, name, W):
    with Stage(nc, name) as s:
        w1, w1t = s.sb("w1", [128, 4, D]), s.sb("w1t", [128, 512])
        w2, w2t = s.sb("w2", [128, 512]), s.sb("w2t", [128, 4, D])
        b1, b2 = s.sb("b1", [128, 4]), s.sb("b2", [128, 1])
        a1, a2 = s.sb("a1", [128, 4]), s.sb("a2", [128, 1])
        h = s.sb("h", [128, 2, 4, GT])
        yt = s.sb("yt", [128, GT])
        h_ps, y_ps = s.ps("h", [128, 4, 512]), s.ps("y", [128, 2, 512])
        loaded, summed, scaled, signed, h_done, h_ready, y_done, yt_ready, x_added = s.sems(
            "loaded summed scaled signed h_done h_ready y_done yt_ready x_added")
        block = s.block()
        x, xn = R["x"], R["xn"]

        @block.sync
        def _(sp):
            for dst, src in ((w1[:, :, :], "w1"), (w1t[:, :], "w1t"), (w2[:, :], "w2"), (w2t[:, :, :], "w2t"), (b1[:, :], "b1"), (b2[:, :], "b2")):
                sp.dma_start(dst, W[src]).then_inc(loaded, 16)
            sp.wait_ge(loaded, START + 96)

        @block.tensor
        def _(pe):
            pe.wait_ge(signed, START + 2)

            def up(g, n):
                for i in range(4):
                    pe.matmul(h_ps[:, i, :], w1t[:, i * 128:(i + 1) * 128], xn[:, at_group(g)], start=True, stop=True).then_inc(h_done, 1)

            with pe.Fori(0, NG) as g:
                up(g, 0)
                pe.wait_ge(h_ready, START + g * 4 + 4)
                pe.wait_ge(yt_ready, START + g)
                for i in range(4):
                    mm = pe.matmul(y_ps[:, 0, :], w2t[:, i, :], h[:, 0, i, :], start=(i == 0), stop=(i == 3))
                mm.then_inc(y_done, 1)

        @block.scalar
        def _(act):
            act.wait_ge(loaded, START + 96)
            act.activation(w1t[:, :], w1t[:, :], ACT.Sign).then_inc(signed, 1)
            act.activation(w2t[:, :, :], w2t[:, :, :], ACT.Sign).then_inc(signed, 1)
            act.wait_ge(scaled, START + 2)
            with act.Fori(0, NG) as g:
                for i in range(4):
                    act.wait_ge(h_done, START + g * 4 + i + 1)
                    if i == 0:
                        act.wait_ge(y_done, START + g)
                    act.activation(h[:, 0, i, :], h_ps[:, i, :], ACT.Gelu, bias=b1[:, i:i + 1], scale=a1[:, i:i + 1]).then_inc(h_ready, 1)

        @block.gpsimd
        def _(pool):
            pass

        @block.vector
        def _(ve):
            ve.wait_ge(loaded, START + 96)
            ve.tensor_reduce(a1[:, :], w1[:, :, :], X_AXIS, ALU.add, apply_absolute_value=True).then_inc(summed, 1)
            ve.tensor_reduce(a2[:, :], w2[:, :], X_AXIS, ALU.add, apply_absolute_value=True).then_inc(summed, 1)
            ve.wait_ge(summed, START + 2)
            ve.tensor_scalar(a1[:, :], a1[:, :], 1.0 / D, None, ALU.mult).then_inc(scaled, 1)
            ve.tensor_scalar(a2[:, :], a2[:, :], 1.0 / 512, None, ALU.mult).then_inc(scaled, 1)
            ve.wait_ge(scaled, START + 2)
            with ve.Fori(0, NG) as g:
                ve.wait_ge(y_done, START + g + 1)
                ve.wait_ge(x_added, START + g)
                ve.tensor_scalar(yt[:, :], y_ps[:, 0, :], a2[:, 0:1], b2[:, 0:1], ALU.mult, ALU.add).then_inc(yt_ready, 1)
                ve.wait_ge(yt_ready, START + g + 1)
                ve.tensor_tensor(x[:, at_group(g)], x[:, at_group(g)], yt[:, :], ALU.add).then_inc(x_added, 1)


DEPTH = 6
FF = 341
WA, WM = 6148, 1161
LN_GROUPS = 4
FB = [(0, 128), (128, 256), (256, 341)]


def local_stage(nc, R, name, W):
    with Stage(nc, name) as s:
        T = attn64_tiles(s)
        s_ps, st_ps, o_ps = T["s_ps"], T["st_ps"], T["o_ps"]
        xs4 = s.sb("xs", [128, LN_GROUPS, GT])
        xs = xs4[:, 0, :]
        wa, wm = s.sb("wa", [128, WA]), s.sb("wm", [128, WM])
        w_qk = wa[:, 0:2048].rearrange("p (a c) -> p a c", a=2)
        w_rot = wa[:, 2048:4096].rearrange("p (a c) -> p a c", a=2)
        wv, wo, scales = wa[:, 4096:5120], wa[:, 5120:6144], wa[:, 6144:6148]
        w1 = wm[:, 0:768].rearrange("p (a c) -> p a c", a=6)
        w2 = wm[:, 768:1152].rearrange("p (a c) -> p a c", a=3)
        cols = wm[:, 1152:1161]
        tables = s.sb("tables", [128, 4, SEQ])
        tab = s.sb("tab", [128, 4, SEQ])
        sq, m1, m2 = (s.sb(n, [128, 2, GT]) for n in ("sq", "m1", "m2"))
        rn = s.sb("rn", [128, 2, GT])
        xg = T["qt"][:, :, :].rearrange("p i t -> p (i t)")
        gl, h = s.sb("gl", [128, 3, GT]), s.sb("h", [128, 3, GT])
        ten, thirteen, tiny = s.sb("ten", [128, 1]), s.sb("thirteen", [128, 1]), s.sb("tiny", [128, 1])
        geo = Geometry(R, band=True)
        sem = named(s, CORE_SEMS + [
            "loaded", "zeroed", "attn_w", "mlp_w", "tab_ready", "xs_ready", "proj_done", "rot_done", "squared", "m_ready",
            "summed", "norm_done", "norm_ln", "rn_ready", "qk_ready", "k_ready", "v_done",
            "v_ready", "y_added", "mean_done", "centred", "sqx_ready", "var_done", "ln_done", "rstd_ready", "xg_step",
            "xg_ready", "shifted", "up_done", "gl_ready", "h_ready", "out_done", "out_added", "x_added"])
        core = attn64_core(nc, R, T, geo, sem)
        k_raw = s.sb("k_raw", [128, NB, GT])
        xc, sqx = k_raw[:, 0:LN_GROUPS, :], k_raw[:, LN_GROUPS:2 * LN_GROUPS, :]
        rstd = [tile[:, k, :] for tile in (m1, m2) for k in range(2)]
        mean_ps = [s_ps[:, k, :] for k in range(4)]
        var_ps = [st_ps[:, 0, :], st_ps[:, 1, :], o_ps[:, 0, :], o_ps[:, 1, :]]
        block = s.block()
        x, y = R["x"], R["xn"]
        qt, kt, v = T["qt"], T["kt"], T["v"]
        raw = [qt, k_raw]
        two = lambda ap: ap.rearrange("p (b t) -> p b t", b=2)

        @block.sync
        def _(sp):
            sp.dma_start(tables[:, :, :], W["tables"]).then_inc(sem["loaded"], 16)
            with sp.Fori(0, DEPTH) as d:
                off_a, off_m = sp.snap(d * (128 * WA)), sp.snap(d * (128 * WM))
                sp.wait_ge(sem["y_added"], START + d * NG)
                sp.dma_start(wa[:, :], W["wa"][bass.ds(off_a, 128 * WA)].rearrange("(p c) -> p c", p=128)).then_inc(sem["attn_w"], 16)
                sp.wait_ge(sem["out_added"], START + d * NG)
                sp.dma_start(wm[:, :], W["wm"][bass.ds(off_m, 128 * WM)].rearrange("(p c) -> p c", p=128)).then_inc(sem["mlp_w"], 16)
            sp.wait_ge(sem["attn_w"], START + DEPTH * 16)
            sp.wait_ge(sem["mlp_w"], START + DEPTH * 16)
            sp.wait_ge(sem["loaded"], START + 16)

        @block.tensor
        def _(pe):
            pe.wait_ge(sem["zeroed"], START + 6)

            def attn(n):
                pe.wait_ge(sem["xs_ready"], START + n + 1)
                pe.wait_ge(sem["ot_ready"], START + n * NB)
                for i in range(16):
                    a, c = divmod(i, NB)
                    bank = 2 * (i % 2)
                    pe.wait_ge(sem["m_ready"], START + (n * 32 + 2 * (i - 1) if i >= 2 else n * 32))
                    pe.wait_ge(sem["squared"], START + (n * 16 + i - 1 if i >= 2 else n * 16))
                    pe.matmul(s_ps[:, bank, :], w_qk[:, a, c * 128:(c + 1) * 128], xs, start=True, stop=True).then_inc(sem["proj_done"], 1)
                    pe.matmul(s_ps[:, bank + 1, :], w_rot[:, a, c * 128:(c + 1) * 128], xs, start=True, stop=True).then_inc(sem["rot_done"], 1)
                    if i >= 1:
                        norms(n, i - 1)
                norms(n, 15)
                pe.wait_ge(sem["m_ready"], START + n * 32 + 32)
                pe.wait_ge(sem["k_ready"], START + n * 8 + 1)
                core.scores(pe, n, 0)
                core.scores(pe, n, 1)
                for i in range(8):
                    t, half = divmod(i, 2)
                    if i >= 2:
                        pe.wait_ge(sem["v_ready"], START + n * 8 + i - 1)
                    pe.matmul(o_ps[:, half, :], xs[:, t * 128:(t + 1) * 128], wv[:, half * 512:(half + 1) * 512], start=True, stop=True).then_inc(sem["v_done"], 1)
                pe.wait_ge(sem["norm_ln"], START + n * 16 + 16)
                def scores(pe, n, u):
                    pe.wait_ge(sem["k_ready"], START + n * 8 + u // 2 + 1)
                    core.scores(pe, n, u)

                for u in range(17):
                    if u == 1:
                        pe.wait_ge(sem["v_ready"], START + n * 8 + 8)
                    core.attend(pe, n, u, wo, scores)
                core.project(pe, n, NB - 1, wo)

            def norms(n, i):
                pe.wait_ge(sem["squared"], START + n * 16 + i + 1)
                if i >= 2:
                    pe.wait_ge(sem["norm_ln"], START + n * 16 + i - 1)
                else:
                    pe.wait_ge(sem["y_added"], START + n)
                pe.matmul(st_ps[:, i % 2, :], R["head_ones"][:, :], sq[:, i % 2, :], start=True, stop=True).then_inc(sem["norm_done"], 1)

            def layer_norm(m):
                for k in range(LN_GROUPS):
                    pe.wait_ge(sem["shifted"], START + m * LN_GROUPS + k + 1)
                    pe.matmul(mean_ps[k], R["mean_w"][:, :], xs4[:, k, :], start=True, stop=True).then_inc(sem["mean_done"], 1)
                for k in range(LN_GROUPS):
                    pe.wait_ge(sem["sqx_ready"], START + m * LN_GROUPS + k + 1)
                    pe.matmul(var_ps[k], R["mean_w"][:, :], sqx[:, k, :], start=True, stop=True).then_inc(sem["var_done"], 1)

            banks = [st_ps[:, 0, :], st_ps[:, 1, :], o_ps[:, 0, :], s_ps[:, 2, :], s_ps[:, 3, :], o_ps[:, 1, :]]

            def up(n, g, i):
                a, b = FB[i]
                for k in (i, 3 + i):
                    mm = pe.matmul(banks[k][0:b - a, :], w1[:, k, 0:b - a], xg[:, at_group(g)], start=True, stop=True)
                mm.then_inc(sem["up_done"], 1)

            def down(n, i):
                a, b = FB[i]
                pe.wait_ge(sem["h_ready"], START + n * 3 + i + 1)
                if i == 0:
                    pe.wait_ge(sem["out_added"], START + n)
                mm = pe.matmul(s_ps[:, 0, :], w2[0:b - a, i, :], h[0:b - a, i, :], start=(i == 0), stop=(i == 2))
                if i == 2:
                    mm.then_inc(sem["out_done"], 1)

            with pe.Fori(0, DEPTH) as d:
                with pe.Fori(0, NG) as g:
                    pe.wait_ge(sem["attn_w"], START + d * 16 + 16)
                    attn(d * NG + g)
                with pe.Fori(0, NG // LN_GROUPS) as g2:
                    layer_norm(d * (NG // LN_GROUPS) + g2)
                pe.wait_ge(sem["mlp_w"], START + d * 16 + 16)
                pe.wait_ge(sem["xg_ready"], START + d * NG + NG)
                for i in range(3):
                    up(d * NG, 0, i)
                with pe.Fori(1, NG) as g:
                    for i in range(3):
                        down(d * NG + g - 1, i)
                        up(d * NG + g, g, i)
                for i in range(3):
                    down(d * NG + NG - 1, i)

        @block.scalar
        def _(act):
            act.wait_ge(sem["zeroed"], START + 6)

            def shift(xs, g, ready):
                act.activation(xs[0:64, :], y[0:64, at_group(g)], ACT.Copy)
                for b in range(2):
                    last = act.activation(xs[64:128, b * SEQ + 1:(b + 1) * SEQ], y[64:128, bass.ds(g * GT + b * SEQ, SEQ - 1)], ACT.Copy)
                last.then_inc(ready, 1)

            def inverse_norms(n, i):
                act.wait_ge(sem["norm_done"], START + n * 16 + i + 1)
                act.wait_ge(sem["qk_ready"], START + n * 16 + max(0, i - 1))
                act.activation(rn[:, i % 2, :], st_ps[:, i % 2, :], ACT.Ln, scale=float(2 ** 20), bias=tiny[:, :]).then_inc(sem["norm_ln"], 1)
                act.wait_ge(sem["norm_ln"], START + n * 16 + i + 1)
                act.activation(rn[:, i % 2, :], rn[:, i % 2, :], ACT.Exp, scale=-0.5, bias=(thirteen if i < NB else ten)[:, :]).then_inc(sem["rn_ready"], 1)

            def spread_k(n, i):
                act.wait_ge(sem["qk_ready"], START + n * 16 + 8 + i + 1)
                act.activation(kt[0:64, i, 0, :], k_raw[0:64, i, :], ACT.Copy)
                act.activation(kt[64:128, i, 1, :], k_raw[64:128, i, :], ACT.Copy).then_inc(sem["k_ready"], 1)

            def attn(n, g, d):
                act.wait_ge(sem["v_done"], START + n * 8)
                act.wait_ge(sem["out_added"], START + d * NG)
                shift(xs, g, sem["xs_ready"])
                for i in range(16):
                    act.wait_ge(sem["proj_done"], START + n * 16 + i + 1)
                    act.wait_ge(sem["m_ready"], START + n * 32 + 2 * i + 1)
                    act.wait_ge(sem["norm_done"], START + (n * 16 + i - 1 if i >= 2 else n * 16))
                    act.activation(sq[:, i % 2, :], s_ps[:, 2 * (i % 2), :], ACT.Square).then_inc(sem["squared"], 1)
                    if i >= 1:
                        inverse_norms(n, i - 1)
                    if i >= 12:
                        spread_k(n, i - 12)
                inverse_norms(n, 15)
                for i in range(8):
                    if i in (2, 5):
                        core.exps(act, n, i // 3)
                    t, half = divmod(i, 2)
                    act.wait_ge(sem["v_done"], START + n * 8 + i + 1)
                    act.activation(v[:, t, 8 * half:8 * half + 8, :], o_ps[:, half, :].rearrange("p (h d) -> p h d", h=8), ACT.Copy).then_inc(sem["v_ready"], 1)
                for u in range(16):
                    core.keep_probs0(act, n, u)
                    if u < 4:
                        spread_k(n, 4 + u)
                    if u < 14:
                        core.exps(act, n, u + 2)

            def layer_norm(m, g2, d):
                act.wait_ge(sem["centred"], START + m * LN_GROUPS)
                for k in range(LN_GROUPS):
                    shift(xs4[:, k, :], g2 * LN_GROUPS + k, sem["shifted"])
                for k in range(LN_GROUPS):
                    act.wait_ge(sem["centred"], START + m * LN_GROUPS + k + 1)
                    act.activation(sqx[:, k, :], xc[:, k, :], ACT.Square).then_inc(sem["sqx_ready"], 1)
                for k in range(LN_GROUPS):
                    act.wait_ge(sem["var_done"], START + m * LN_GROUPS + k + 1)
                    act.activation(sqx[:, k, :], var_ps[k], ACT.Ln, bias=R["eps"][:, :]).then_inc(sem["ln_done"], 1)
                for k in range(LN_GROUPS):
                    act.wait_ge(sem["ln_done"], START + m * LN_GROUPS + k + 1)
                    act.activation(rstd[k], sqx[:, k, :], ACT.Exp, scale=-0.5).then_inc(sem["rstd_ready"], 1)
                for k in range(LN_GROUPS):
                    act.wait_ge(sem["xg_step"], START + m * LN_GROUPS + k + 1)
                    act.activation(xg[:, bass.ds((g2 * LN_GROUPS + k) * GT, GT)], xc[:, k, :], ACT.Identity, scale=cols[:, 0:1], bias=cols[:, 1:2]).then_inc(sem["xg_ready"], 1)

            banks = [s_ps[:, 2, :], s_ps[:, 3, :], o_ps[:, 1, :]]
            with act.Fori(0, DEPTH) as d:
                act.preload_act_table_set(LN_EXP)
                with act.Fori(0, NG) as g:
                    attn(d * NG + g, g, d)
                act.wait_ge(sem["v_done"], START + d * 64 + 64)
                act.wait_ge(sem["y_added"], START + d * NG + NG)
                act.wait_ge(sem["mlp_w"], START + d * 16 + 16)
                with act.Fori(0, NG // LN_GROUPS) as g2:
                    layer_norm(d * (NG // LN_GROUPS) + g2, g2, d)
                act.preload_act_table_set(GELU)
                with act.Fori(0, NG) as g:
                    n = d * NG + g
                    for i, (a, b) in enumerate(FB):
                        act.wait_ge(sem["up_done"], START + n * 3 + i + 1)
                        act.activation(gl[0:b - a, i, :], banks[i][0:b - a, :], ACT.Gelu, bias=cols[0:b - a, 5 + i:6 + i]).then_inc(sem["gl_ready"], 1)

        @block.gpsimd
        def _(pool):
            pool.memset(T["e"][:, :, :, :], 0.0).then_inc(sem["zeroed"], 1)
            pool.memset(kt[:, :, :, :], 0.0).then_inc(sem["zeroed"], 1)
            pool.memset(tiny[:, :], 1e-24).then_inc(sem["zeroed"], 1)
            pool.memset(xs4[:, :, :], 0.0).then_inc(sem["zeroed"], 1)
            pool.memset(ten[:, :], float(10 * np.log(2.0))).then_inc(sem["zeroed"], 1)
            pool.memset(thirteen[:, :], float(13 * np.log(2.0))).then_inc(sem["zeroed"], 1)
            pool.wait_ge(sem["zeroed"], START + 6)

            with pool.Fori(0, DEPTH) as d:
                with pool.Fori(0, NG) as g:
                    n = d * NG + g
                    for i in range(16):
                        pool.wait_ge(sem["m_ready"], START + n * 32 + 2 * i + 2)
                        pool.tensor_tensor(raw[i // NB][:, i % NB, :], m1[:, i % 2, :], m2[:, i % 2, :], ALU.add).then_inc(sem["summed"], 1)
                    for u in range(16):
                        core.normalise(pool, n, u)

        @block.vector
        def _(ve):
            ve.wait_ge(sem["zeroed"], START + 6)
            ve.wait_ge(sem["loaded"], START + 16)

            def scale_block(n, i):
                a, c = divmod(i, NB)
                ve.wait_ge(sem["rn_ready"], START + n * 16 + i + 1)
                ve.wait_ge(sem["summed"], START + n * 16 + i + 1)
                ve.scalar_tensor_tensor(raw[a][:, c, :], rn[:, i % 2, :], 8e12 if a == 0 else 1e12, raw[a][:, c, :], ALU.min, ALU.mult).then_inc(sem["qk_ready"], 1)

            def attn(n, g):
                for i in range(16):
                    a, c = divmod(i, NB)
                    if i >= 2:
                        ve.wait_ge(sem["summed"], START + n * 16 + i - 1)
                    else:
                        ve.wait_ge(sem["summed"], START + n * 16)
                    tb = lambda k: tab[:, k, :].unsqueeze(1).to_broadcast([128, 2, SEQ])
                    ve.wait_ge(sem["proj_done"], START + n * 16 + i + 1)
                    ve.tensor_tensor(two(m1[:, i % 2, :]), two(s_ps[:, 2 * (i % 2), :]), tb(2 * a), ALU.mult).then_inc(sem["m_ready"], 1)
                    ve.wait_ge(sem["rot_done"], START + n * 16 + i + 1)
                    ve.tensor_tensor(two(m2[:, i % 2, :]), two(s_ps[:, 2 * (i % 2) + 1, :]), tb(2 * a + 1), ALU.mult).then_inc(sem["m_ready"], 1)
                    if i >= 2:
                        scale_block(n, i - 2)
                core.maxima(ve, n, 0)
                scale_block(n, 14)
                core.maxima(ve, n, 1)
                core.invert(ve, n, 0)
                scale_block(n, 15)
                for u in range(16):
                    if u % 2 == 1 and u >= 3:
                        core.keep_out(ve, n, (u - 3) // 2)
                    if u < 15:
                        core.invert(ve, n, u + 1)
                    core.keep_probs1(ve, n, u)
                    if u < 14:
                        core.maxima(ve, n, u + 2)
                core.keep_out(ve, n, NB - 1)
                ve.wait_ge(sem["ot_used"], START + n * NB + NB)
                ve.tensor_tensor(y[:, at_group(g)], y[:, at_group(g)], o_ps[:, 1, :], ALU.add).then_inc(sem["y_added"], 1)

            def layer_norm(m):
                for k in range(LN_GROUPS):
                    ve.wait_ge(sem["mean_done"], START + m * LN_GROUPS + k + 1)
                    ve.wait_ge(sem["xg_ready"], START + m * LN_GROUPS)
                    ve.tensor_tensor(xc[:, k, :], xs4[:, k, :], mean_ps[k], ALU.subtract).then_inc(sem["centred"], 1)
                for k in range(LN_GROUPS):
                    ve.wait_ge(sem["rstd_ready"], START + m * LN_GROUPS + k + 1)
                    ve.tensor_tensor(xc[:, k, :], xc[:, k, :], rstd[k], ALU.mult).then_inc(sem["xg_step"], 1)

            lin = [st_ps[:, 0, :], st_ps[:, 1, :], o_ps[:, 0, :]]

            def hidden(n, i):
                a, b = FB[i]
                ve.wait_ge(sem["gl_ready"], START + n * 3 + i + 1)
                ve.scalar_tensor_tensor(h[0:b - a, i, :], lin[i][0:b - a, :], cols[0:b - a, 2 + i:3 + i], gl[0:b - a, i, :],
                                        ALU.add, ALU.mult).then_inc(sem["h_ready"], 1)

            def add_out(n, g):
                ve.wait_ge(sem["out_done"], START + n + 1)
                ve.scalar_tensor_tensor(y[:, at_group(g)], s_ps[:, 0, :], cols[:, 8:9], y[:, at_group(g)], ALU.add, ALU.add).then_inc(sem["out_added"], 1)

            with ve.Fori(0, DEPTH) as d:
                ve.wait_ge(sem["attn_w"], START + d * 16 + 16)
                for k in range(4):
                    tt = ve.tensor_scalar(tab[:, k, :], tables[:, k, :], scales[:, k:k + 1], None, ALU.mult)
                    tt.then_inc(sem["tab_ready"], 1)
                with ve.Fori(0, NG) as g:
                    ve.wait_ge(sem["tab_ready"], START + d * 4 + 4)
                    attn(d * NG + g, g)
                with ve.Fori(0, NG // LN_GROUPS) as g2:
                    layer_norm(d * (NG // LN_GROUPS) + g2)
                for i in range(3):
                    hidden(d * NG, i)
                with ve.Fori(1, NG) as g:
                    hidden(d * NG + g, 0)
                    add_out(d * NG + g - 1, g - 1)
                    hidden(d * NG + g, 1)
                    hidden(d * NG + g, 2)
                add_out(d * NG + NG - 1, NG - 1)
            with ve.Fori(0, NG) as g:
                ve.wait_ge(sem["out_added"], START + DEPTH * NG)
                ve.tensor_tensor(x[:, at_group(g)], x[:, at_group(g)], y[:, at_group(g)], ALU.add).then_inc(sem["x_added"], 1)


def store_stage(nc, R, out):
    with Stage(nc, "store") as s:
        (stored,) = s.sems("stored")
        block = s.block()

        @block.sync
        def _(sp):
            sp.dma_start(out, R["x"][:, :]).then_inc(stored, 16)
            sp.wait_ge(stored, START + 16)


CONST_BF = [("ident", 128), ("causal", 128), ("band", 128), ("band_q1", 160), 
            ("upper", 128), ("ones", 128), ("first", 8), ("head_ones", 128)]


def build(nc, IN, out, stages):
    with ExitStack() as ctx:
        sb = lambda n, shape, dt=F32: ctx.enter_context(nc.sbuf_tensor(n, shape, dt))
        R = {"x": sb("x_res", [128, TOK]), "xn": sb("xn_res", [128, TOK]), "ident": sb("ident", [128, 128]),
             "mean_w": sb("mean_w", [128, 128]), "eps": sb("eps", [128, 1]), "comb": sb("comb", [128, NT, 8]),
             "head_ones": sb("head_ones", [128, 128]), "c_bf": sb("consts_bf", [128, sum(w for _, w in CONST_BF)], BF16)}
        at, C = 0, {}
        for n, w in CONST_BF:
            C[n] = R["c_bf"][:, at:at + w]
            at += w
        R["masks"] = C
        R["ident_bf"], R["upper_bf"], R["ones_bf"], R["first"] = C["ident"], C["upper"], C["ones"], C["first"]
        load_stage(nc, R, IN)
        if "norm0" in stages:
            norm_stage(nc, R, "norm0")
        if "attn0" in stages:
            attn64_stage(nc, R, "attn0", {k: IN[f"a0_{k}"] for k in ("wq", "wk", "wv", "wo")}, 0.125)
        if "ffn0" in stages:
            gate_stage(nc, R, "gate0", {"wg": IN["f0_wg"], "bg": IN["f0_bg"]}, None)
            experts_stage(nc, R, "ffn0", {k: IN[f"f0_{k}"] for k in ("w1", "w2", "b1", "b2")}, False)
        if "norm1" in stages:
            norm_stage(nc, R, "norm1")
        if "attn1" in stages:
            attn8_stage(nc, R, "attn1", {"low": IN["c_low"], "mix_sel": IN["c_mix_sel"], "mix_mask": IN["c_mix_mask"], **{k: IN[f"a1_{k}"] for k in ("wq", "wk", "wv", "vb", "qkb")}}, 1.0)
        if "ffn1" in stages:
            local_stage(nc, R, "ffn1", {"tables": IN["c_tables"], **{k: IN[f"f1_{k}"] for k in ("wa", "wm")}})
        if "norm2" in stages:
            norm_stage(nc, R, "norm2")
        if "attn2" in stages:
            attn8_stage(nc, R, "attn2", {"low": IN["c_low"], "lora": True, **{k: IN[f"a2_{k}"] for k in ("wq", "wk", "wv", "vb", "qkb", "wo", "wob", "lora_a", "lora_b")}},
                        8 ** -0.5, project=True)
        if "ffn2" in stages:
            binary_stage(nc, R, "ffn2", {k: IN[f"f2_{k}"] for k in ("w1", "w1t", "w2", "w2t", "b1", "b2")})
        if "norm3" in stages:
            norm_stage(nc, R, "norm3")
        if "ffn3" in stages:
            gate_stage(nc, R, "gate3", {"wg": IN["f3_wg"]}, int(1.25 * TOK / 8))
            experts_stage(nc, R, "ffn3", {k: IN[f"f3_{k}"] for k in ("w1", "w2")}, True)
        if "attn3" in stages:
            with Stage(nc, "copy3") as s:
                (added,) = s.sems("added")
                block = s.block()

                @block.vector
                def _(ve):
                    with ve.Fori(0, NG) as g:
                        ve.tensor_tensor(R["x"][:, at_group(g)], R["x"][:, at_group(g)], R["xn"][:, at_group(g)], ALU.add).then_inc(added, 1)
            norm_stage(nc, R, "norm3b", again=True)
            attn8_stage(nc, R, "attn3", {"low": IN["c_low"], **{k: IN[f"a3_{k}"] for k in ("wq", "wk", "wv", "vb", "qkb", "wo", "wob", "gamma", "beta", "wqr", "wkr", "qkbr")},
                                         "cos": IN["c_cos"], "sin": IN["c_sin"]},
                        8 ** -0.5, affine=True, rope=True, project=True)
        store_stage(nc, R, out)


def layouts(a):
    f = np.float32
    T = lambda w: np.ascontiguousarray(np.asarray(w).T)
    L = {"x_t": T(np.asarray(a["L0_attn_x"]).reshape(TOK, D))}
    for n in "qkv":
        L[f"a0_w{n}"] = T(np.asarray(a[f"L0_attn_w_{n}"]).reshape(HEADS * DH, D))
    blocks = lambda w, n: np.ascontiguousarray(w.reshape(n, 128, -1).transpose(1, 0, 2))
    L["a0_wo"] = blocks(T(a["L0_attn_w_o"]), NB).reshape(128, 1024)
    L["f0_wg"], L["f0_bg"] = np.asarray(a["L0_ffn_gate_w"]), np.asarray(a["L0_ffn_gate_b"]).reshape(1, 8)
    L["f0_w1"] = np.ascontiguousarray(np.asarray(a["L0_ffn_w1"]).transpose(1, 0, 2))
    L["f0_w2"] = np.ascontiguousarray(np.asarray(a["L0_ffn_w2"]).reshape(8, 4, 128, D).transpose(2, 0, 1, 3))
    L["f0_b1"] = np.ascontiguousarray(np.asarray(a["L0_ffn_b1"]).reshape(8, 4, 128).transpose(2, 0, 1))
    L["f0_b2"] = np.asarray(a["L0_ffn_b2"])

    def spread(w, key):
        o = np.zeros((w.shape[0], 4, 4, 32), w.dtype)
        o[..., 0:24] = np.tile(w.reshape(-1, 4, 4, 8), (1, 1, 1, 3))
        return o.reshape(-1, 4, 128)

    def spread_bias(bq, bk, one=1.0):
        q, k = (np.zeros((4, 4, 32), f) for _ in range(2))
        q[..., 0:24] = np.tile(bq.reshape(4, 4, 8), (1, 1, 3))
        k[..., 0:24] = np.tile(bk.reshape(4, 4, 8), (1, 1, 3))
        k[..., 24:26] = one
        return np.ascontiguousarray(np.concatenate([q, k]).reshape(8, 128).T)

    def heads8(pre, wq, wk, wv, bq, bk, bv):
        L[f"{pre}_wq"], L[f"{pre}_wk"] = spread(wq, "q"), spread(wk, "k")
        L[f"{pre}_wv"], L[f"{pre}_vb"] = np.ascontiguousarray(wv), bv.reshape(1, D)
        L[f"{pre}_qkb"] = spread_bias(bq, bk)

    w, b = np.asarray(a["L1_attn_W_qkv"]), np.asarray(a["L1_attn_b_qkv"])
    heads8("a1", w[:, 0:128], w[:, 128:256], w[:, 256:384], b[0:128], b[128:256], b[256:384])
    heads8("a2", *(T(a[f"L2_attn_W{n}"]) for n in "qkv"), *(np.asarray(a[f"L2_attn_b{n}"]) for n in "qkv"))
    L["a2_wo"], L["a2_wob"] = T(a["L2_attn_Wo"]), np.asarray(a["L2_attn_bo"]).reshape(D, 1)
    L["a2_lora_a"] = np.stack([np.asarray(a[f"L2_attn_A{n}"]) for n in "qkvo"], 1)
    lb = np.zeros((8, 4, 512), f)
    for n, c in enumerate("qkvo"):
        bt = T(a[f"L2_attn_B{c}"])
        if n < 2:
            lb[:, n] = spread(bt, "").reshape(8, 512)
        else:
            lb[:, n, 0:128] = bt
    L["a2_lora_b"] = lb
    w, b = np.asarray(a["L3_attn_W_in"]), np.asarray(a["L3_attn_b_in"])
    heads8("a3", w[:, 0:128], w[:, 128:256], w[:, 256:384], b[0:128], b[128:256], b[256:384])
    swap = np.array([1, 0, 3, 2, 4, 5, 6, 7])
    turn = lambda m: m.reshape(-1, 16, 8)[:, :, swap].reshape(m.shape[0] if m.ndim > 1 else -1, *([128] if m.ndim > 1 else []))
    L["a3_wqr"], L["a3_wkr"] = spread(turn(w[:, 0:128]), "q"), spread(turn(w[:, 128:256]), "k")
    L["a3_qkbr"] = spread_bias(turn(b[0:128]).reshape(-1), turn(b[128:256]).reshape(-1), 0.0)
    L["a3_wo"], L["a3_wob"] = np.asarray(a["L3_attn_W_out"]), np.asarray(a["L3_attn_b_out"]).reshape(D, 1)
    L["a3_gamma"], L["a3_beta"] = (np.asarray(a[f"L3_attn_{n}"]).reshape(D, 1) for n in ("gamma", "beta"))

    wq = np.asarray(a["L1_ffn_Wqkv"])
    wa = [wq[:, :, 0:2048], wq[:, :, 0:2048].reshape(DEPTH, D, 32, 2, 32)[:, :, :, ::-1].reshape(DEPTH, D, 2048), wq[:, :, 2048:],
          np.asarray(a["L1_ffn_Wo"]).reshape(DEPTH, NB, 128, D).transpose(0, 2, 1, 3).reshape(DEPTH, 128, 1024)]
    w1 = np.zeros((DEPTH, D, 6, 128), f)
    b1 = np.zeros((DEPTH, 128, 6), f)
    w2 = np.zeros((DEPTH, 128, 3, D), f)
    for i, (lo, hi) in enumerate(FB):
        for part in range(2):
            cols = slice(part * FF + lo, part * FF + hi)
            w1[:, :, 3 * part + i, 0:hi - lo] = np.asarray(a["L1_ffn_W1"])[:, :, cols]
            b1[:, 0:hi - lo, 3 * part + i] = np.asarray(a["L1_ffn_b1"])[:, cols]
        w2[:, 0:hi - lo, i] = np.asarray(a["L1_ffn_W2"])[:, lo:hi]
    qs, ks = np.asarray(a["L1_ffn_q_scale"]), np.asarray(a["L1_ffn_k_scale"])
    rot = lambda v: np.concatenate([v[:, 32:], v[:, :32]], 1)
    wa += [np.tile(v, (1, 2))[:, :, None] for v in (qs, rot(qs), ks, rot(ks))]
    wm = [w1.reshape(DEPTH, D, 768), w2.reshape(DEPTH, 128, 384)]
    wm += [np.asarray(a[f"L1_ffn_{n}"])[:, :, None] for n in ("ln_g", "ln_b")] + [b1, np.asarray(a["L1_ffn_b2"])[:, :, None]]
    L["f1_wa"], L["f1_wm"] = (np.ascontiguousarray(np.concatenate(w, 2)).reshape(-1) for w in (wa, wm))

    w1, w2 = np.asarray(a["L2_ffn_w1"]), np.asarray(a["L2_ffn_w2"])
    L["f2_w1"], L["f2_w1t"] = blocks(w1, 4), T(w1)
    L["f2_w2"], L["f2_w2t"] = w2, blocks(T(w2), 4)
    L["f2_b1"] = T(np.asarray(a["L2_ffn_b1"]).reshape(4, 128))
    L["f2_b2"] = np.asarray(a["L2_ffn_b2"]).reshape(D, 1)
    L["f3_wg"] = T(a["L3_ffn_gate_w"])
    gp, up = (np.asarray(a[f"L3_ffn_{n}_proj_w"]).reshape(8, 2, 128, D) for n in ("gate", "up"))
    L["f3_w1"] = np.ascontiguousarray(np.stack([gp, up], 2).transpose(4, 0, 1, 2, 3)).reshape(D, 8, 512)
    L["f3_w2"] = np.ascontiguousarray(np.asarray(a["L3_ffn_down_proj_w"]).reshape(8, D, 2, 128).transpose(3, 0, 2, 1))
    return L


def constants():
    f = np.float32
    i, j = np.arange(128)[:, None], np.arange(128)[None, :]
    m = lambda bad: np.where(bad, NEG, 0.0).astype(f)
    C = {"ident": np.eye(128, dtype=f), "causal": m(j > i)}
    band = lambda q, k: m((k > q) | (k < q - 32))
    j160 = np.arange(160)[None, :]
    C["band"] = band(i, j)
    C["band_q1"] = band(128 + i, 96 + j160)
    C["upper"] = (i <= j).astype(f)
    C["ones"] = np.ones((128, 128), f)
    C["first"] = np.broadcast_to(np.arange(8, 0, -1).astype(f), (128, 8))
    C["head_ones"] = (i // 64 == j // 64).astype(f)
    out = {"c_bf": np.concatenate([C[n] for n, _ in CONST_BF], 1), "c_ident": C["ident"]}
    out["c_mix_sel"] = (i // 16 == np.arange(8)[None, :]).astype(f)
    out["c_mix_mask"] = (i % 16 == j // 8).astype(f)
    low = np.zeros((4, 32, 2), f)
    low[:, 8:16, 0] = low[:, 16:24, 1] = -1.0
    out["c_low"] = low.reshape(128, 2)
    t = np.arange(SEQ, dtype=f)
    fr = np.repeat(t[:, None] * (1.0 / 10000.0 ** (np.arange(0, 4, 2, dtype=f) / f(4))).astype(f)[None], 2, -1)
    cos, sin = np.ones((4, 32, SEQ), f), np.zeros((4, 32, SEQ), f)
    for r in range(3):
        cos[:, 8 * r:8 * r + 4] = np.cos(fr).T
        sin[:, 8 * r:8 * r + 4] = np.sin(fr).T * np.array([-1, 1, -1, 1], f)[:, None]
    out["c_cos"], out["c_sin"] = cos.reshape(128, SEQ), sin.reshape(128, SEQ)
    half = np.arange(0, DH, 2, dtype=f)
    fr = t[:, None] * (1.0 / 10000.0 ** (half / f(DH))).astype(f)[None]
    sc = (((half + f(0.4 * DH)) / f(1.4 * DH))[None] ** ((t - SEQ // 2) / f(16))[:, None]).astype(f)
    both = lambda a, sign: np.tile(np.concatenate([a * sign, a], 1), (1, 2)).T
    cos, sin = np.cos(fr).astype(f), np.sin(fr).astype(f)
    inv = (f(1.0) / sc).astype(f)
    out["c_tables"] = np.ascontiguousarray(np.stack([both(cos * sc, 1), both(sin * sc, -1), both(cos * inv, 1), both(sin * inv, -1)], 1)).astype(f)
    return out


STAGES = "norm0 attn0 ffn0 norm1 attn1 ffn1 norm2 attn2 ffn2 norm3 ffn3 attn3".split()


def kernel(**inputs):
    import concourse.bacc as _bacc
    from concourse.bass_utils import run_bass_kernel_spmd as _run

    nc = _bacc.Bacc("TRN2", target_bir_lowering=False, num_devices=1)
    arrays = {n: np.ascontiguousarray(a) for n, a in {**layouts(inputs), **constants()}.items()}
    IN = {n: nc.dram_tensor(n, a.shape, mybir.dt.from_np(a.dtype), kind="ExternalInput").ap() for n, a in arrays.items()}
    out = nc.dram_tensor("out_t", (128, TOK), F32, kind="ExternalOutput").ap()
    build(nc, IN, out, STAGES)
    r = _run(nc, [arrays], core_ids=[0])
    return np.ascontiguousarray(np.asarray(r.results[0]["out_t"]).T).reshape(16, SEQ, D)
```
